# Optimizing a Trainium2 kernel written in Bass

```python
import numpy as np
import jax
import jax.numpy as jnp

def _softmax(x, axis=-1):
    return jax.nn.softmax(x, axis=axis)

def _gelu(x):
    return jax.nn.gelu(x, approximate=True)

def _silu(x):
    return jax.nn.silu(x)

def _sigmoid(x):
    return jax.nn.sigmoid(x)

def _layernorm(x, axis=-1, eps=1e-05):
    m = jnp.mean(x, axis=axis, keepdims=True)
    v = jnp.var(x, axis=axis, keepdims=True)
    return (x - m) / jnp.sqrt(v + eps)

def _scatter_add(tgt, idx, src, axis=0):
    return tgt.at[idx].add(src)

def _segment_sum(src, seg, n):
    return jax.ops.segment_sum(src, seg, n)
kernel_name = 'mk_recurrent_d2_jaxref_r8_273ada'

def setup_inputs(seed: int=0):
    np.random.seed(seed)
    _w = jnp.asarray

    def _L0_attn_setup():
        import jax, jax.numpy as jnp
        import numpy as np
        from jax import lax
        DIM = 128
        H = 16
        HD = DIM // H
        D_INNER = 4
        CHUNK = 16
        BASE_LR = 0.001
        KSZ = 4

        def short_conv(x, w):
            xT = jnp.transpose(x, (0, 2, 1))
            y = lax.conv_general_dilated(xT, w[:, None, :], window_strides=(1,), padding=[(KSZ - 1, 0)], feature_group_count=x.shape[-1], dimension_numbers=('NCH', 'OIH', 'NCH'))
            return jnp.transpose(y + xT, (0, 2, 1))

        def l2norm(x):
            return x / jnp.linalg.norm(x, axis=-1, keepdims=True)

        def attn(q, k, v):
            s = jnp.einsum('bqhd,bkhd->bhqk', q, k) / jnp.sqrt(jnp.asarray(q.shape[-1], q.dtype))
            p = jax.nn.softmax(s, axis=-1)
            return jnp.einsum('bhqk,bkhd->bqhd', p, v)

        def _forward(hidden_states, Wq, Wk, Wv, Wlr, Wg, Wo, cq, ck, cv, W_in_init, W_out_init, ln_g, ln_b):
            b, l, _ = hidden_states.shape
            q = l2norm(jax.nn.silu(short_conv(hidden_states @ Wq.T, cq)).reshape(b, l, H, HD))
            k = l2norm(jax.nn.silu(short_conv(hidden_states @ Wk.T, ck)).reshape(b, l, H, HD))
            v = jax.nn.silu(short_conv(hidden_states @ Wv.T, cv)).reshape(b, l, H, HD)
            lr = jax.nn.softplus(hidden_states @ Wlr.T + BASE_LR).reshape(b, l, H, 2)
            nc = l // CHUNK
            to_chunks = lambda x: x.reshape(b, nc, CHUNK, H, -1).transpose(1, 0, 2, 3, 4)
            qc, kc, vc, lrc = map(to_chunks, (q, k, v, lr))
            W_in0 = jnp.broadcast_to(W_in_init, (b, D_INNER, H, HD))
            W_out0 = jnp.broadcast_to(W_out_init, (b, D_INNER, H, HD))
            mask = jnp.tril(jnp.ones((CHUNK, CHUNK), jnp.float32))

            def step(carry, xs):
                W_in, W_out = carry
                q_t, k_t, v_t, lr_t = xs
                k_h = jax.nn.softmax(jnp.einsum('blhd,bDhd->blhD', k_t, W_in), axis=-1) * lr_t[..., 1:]
                q_h = jax.nn.softmax(jnp.einsum('blhd,bDhd->blhD', q_t, W_in), axis=-1)
                qk = jnp.einsum('bqhD,bkhD->bhqk', q_h, k_h) * mask
                o_t = jnp.einsum('bqhD,bDhd->bqhd', q_h, W_out) + jnp.einsum('bhqk,bkhd->bqhd', qk, v_t)
                W_out = W_out + jnp.einsum('bnhD,bnhd->bDhd', k_h, v_t)
                lr_in = lr_t[:, :1, :, 0:1]
                lr_out = lr_t[:, :1, :, 1:2]
                for _ in range(2):
                    g_out = -attn(W_in, k_t, v_t)
                    g_in = -attn(W_out, v_t, k_t)
                    W_in = W_in - lr_in * g_in
                    W_out = W_out - lr_out * g_out
                return ((W_in, W_out), o_t)
            _, o = lax.scan(step, (W_in0, W_out0), (qc, kc, vc, lrc))
            o = o.transpose(1, 0, 2, 3, 4).reshape(b, l, H, HD)
            mu = o.mean(-1, keepdims=True)
            var = ((o - mu) ** 2).mean(-1, keepdims=True)
            o = (o - mu) / jnp.sqrt(var + 1e-05) * ln_g + ln_b
            o = o.reshape(b, l, DIM)
            gate = hidden_states @ Wg.T
            return o * gate @ Wo.T
        key = jax.random.key(seed)
        ks = jax.random.split(key, 12)
        b, l = (4, 512)
        s = 1.0 / np.sqrt(DIM)
        return {'hidden_states': jax.random.normal(ks[0], (b, l, DIM), jnp.float32), 'Wq': jax.random.normal(ks[1], (DIM, DIM), jnp.float32) * s, 'Wk': jax.random.normal(ks[2], (DIM, DIM), jnp.float32) * s, 'Wv': jax.random.normal(ks[3], (DIM, DIM), jnp.float32) * s, 'Wlr': jax.random.normal(ks[4], (H * 2, DIM), jnp.float32) * s, 'Wg': jax.random.normal(ks[5], (DIM, DIM), jnp.float32) * s, 'Wo': jax.random.normal(ks[6], (DIM, DIM), jnp.float32) * s, 'cq': jax.random.normal(ks[7], (DIM, KSZ), jnp.float32) * 0.1, 'ck': jax.random.normal(ks[8], (DIM, KSZ), jnp.float32) * 0.1, 'cv': jax.random.normal(ks[9], (DIM, KSZ), jnp.float32) * 0.1, 'W_in_init': jax.random.normal(ks[10], (1, D_INNER, H, HD), jnp.float32) / np.sqrt(HD), 'W_out_init': jax.random.normal(ks[11], (1, D_INNER, H, HD), jnp.float32) / np.sqrt(D_INNER), 'ln_g': jnp.ones((HD,), jnp.float32), 'ln_b': jnp.zeros((HD,), jnp.float32)}
    _L0_attn_in = _L0_attn_setup()

    def _L0_ffn_setup():
        import jax, jax.numpy as jnp
        import numpy as np
        B, S, D, F, E, TOPK = (4, 256, 128, 512, 8, 2)

        def _moe_forward(x, W_router, W_gate, W_up, W_down):
            logits = jnp.einsum('bsd,ed->bse', x, W_router)
            probs = jax.nn.softmax(logits, axis=-1)
            gates, indices = jax.lax.top_k(probs, TOPK)
            gates = gates / jnp.sum(gates, axis=-1, keepdims=True)
            weights = jnp.sum(gates[..., None] * jax.nn.one_hot(indices, E, dtype=x.dtype), axis=-2)
            weights_e = jnp.moveaxis(weights, -1, 0)

            def body(acc, params):
                wg, wu, wd, wt = params
                gate = jax.nn.silu(jnp.einsum('bsd,fd->bsf', x, wg))
                up = jnp.einsum('bsd,fd->bsf', x, wu)
                y = jnp.einsum('bsf,df->bsd', gate * up, wd)
                return (acc + wt[..., None] * y, None)
            out, _ = jax.lax.scan(body, jnp.zeros_like(x), (W_gate, W_up, W_down, weights_e))
            return out
        key = jax.random.key(seed)
        k1, k2, k3, k4, k5 = jax.random.split(key, 5)
        x = jax.random.normal(k1, (B, S, D), dtype=jnp.float32)
        W_router = jax.random.normal(k2, (E, D), dtype=jnp.float32) / np.sqrt(D)
        W_gate = jax.random.normal(k3, (E, F, D), dtype=jnp.float32) / np.sqrt(D)
        W_up = jax.random.normal(k4, (E, F, D), dtype=jnp.float32) / np.sqrt(D)
        W_down = jax.random.normal(k5, (E, D, F), dtype=jnp.float32) / np.sqrt(F)
        return {'x': x, 'W_router': W_router, 'W_gate': W_gate, 'W_up': W_up, 'W_down': W_down}
    _L0_ffn_in = _L0_ffn_setup()

    def _L1_attn_setup():
        import jax, jax.numpy as jnp
        import numpy as np
        DIM, D_INNER, D_STATE, DT_RANK, D_CONV = (128, 256, 16, 64, 4)
        BATCH, SEQ = (2, 128)

        def _silu(v):
            return v * jax.nn.sigmoid(v)

        def _ssm_forward(x, in_proj_w, conv_w, conv_b, x_proj_w, dt_proj_w, dt_proj_b, A_log, D_param, out_proj_w):
            b, l, _ = x.shape
            d_inner, d_conv = (conv_w.shape[0], conv_w.shape[2])
            dt_rank, n = (dt_proj_w.shape[0], A_log.shape[1])
            x_and_res = x @ in_proj_w
            xp, res = (x_and_res[..., :d_inner], x_and_res[..., d_inner:])
            h = jax.lax.conv_general_dilated(xp.transpose(0, 2, 1), conv_w, window_strides=(1,), padding=[(d_conv - 1, 0)], dimension_numbers=('NCH', 'OIH', 'NCH'), feature_group_count=d_inner) + conv_b[None, :, None]
            h = _silu(h.transpose(0, 2, 1))
            A = -jnp.exp(A_log)
            x_dbl = h @ x_proj_w
            dlt, Bm, Cm = (x_dbl[..., :dt_rank], x_dbl[..., dt_rank:dt_rank + n], x_dbl[..., dt_rank + n:])
            delta = jax.nn.softplus(dlt @ dt_proj_w + dt_proj_b)
            deltaA = jnp.exp(jnp.einsum('bld,dn->bldn', delta, A))
            deltaB_u = (delta * h)[..., None] * Bm[:, :, None, :]

            def step(state, t):
                dA_t, dBu_t, c_t = t
                state = dA_t * state + dBu_t
                y_t = jnp.einsum('bdn,bn->bd', state, c_t)
                return (state, y_t)
            init = jnp.zeros((b, d_inner, n), h.dtype)
            _, ys = jax.lax.scan(step, init, (deltaA.transpose(1, 0, 2, 3), deltaB_u.transpose(1, 0, 2, 3), Cm.transpose(1, 0, 2)))
            y = ys.transpose(1, 0, 2) + h * D_param
            y = y * _silu(res)
            return y @ out_proj_w
        key = jax.random.key(seed)
        ks = jax.random.split(key, 9)
        s = 0.02
        A = jnp.tile(jnp.arange(1, D_STATE + 1, dtype=jnp.float32), (D_INNER, 1))
        return {'x': jax.random.normal(ks[0], (BATCH, SEQ, DIM), jnp.float32), 'in_proj_w': jax.random.normal(ks[1], (DIM, 2 * D_INNER), jnp.float32) * s, 'conv_w': jax.random.normal(ks[2], (D_INNER, 1, D_CONV), jnp.float32) * 0.2, 'conv_b': jax.random.normal(ks[3], (D_INNER,), jnp.float32) * 0.1, 'x_proj_w': jax.random.normal(ks[4], (D_INNER, DT_RANK + 2 * D_STATE), jnp.float32) * s, 'dt_proj_w': jax.random.normal(ks[5], (DT_RANK, D_INNER), jnp.float32) * s, 'dt_proj_b': jax.random.normal(ks[6], (D_INNER,), jnp.float32) * 0.1, 'A_log': jnp.log(A), 'D_param': jnp.ones((D_INNER,), jnp.float32), 'out_proj_w': jax.random.normal(ks[7], (D_INNER, DIM), jnp.float32) * s}
    _L1_attn_in = _L1_attn_setup()

    def _L1_ffn_setup():
        import jax, jax.numpy as jnp
        import numpy as np
        D_MODEL = 128
        FF = 512
        E = 8
        TOP_K = 2
        CAP_FACTOR = 1.25
        B, T = (4, 256)

        def _moe_forward(x, gate_w, gate_b, w1, b1, w2, b2):
            Bb, Tt, d = x.shape
            S = Bb * Tt
            C = int(CAP_FACTOR * S / E)
            xf = x.reshape(S, d)
            logits = xf @ gate_w + gate_b
            probs = jax.nn.softmax(logits, axis=1)
            topk_p, topk_i = jax.lax.top_k(probs, TOP_K)
            topk_pn = topk_p / jnp.sum(topk_p, axis=1, keepdims=True)
            rows = jnp.arange(S)
            w_te = jnp.zeros((S, E), xf.dtype).at[rows[:, None], topk_i].set(topk_pn)
            mask = jnp.zeros((S, E), bool).at[rows[:, None], topk_i].set(True)
            rank = jnp.cumsum(mask.astype(jnp.int32), axis=0)
            slot = jnp.where(mask & (rank <= C), rank - 1, C)
            e_grid = jnp.broadcast_to(jnp.arange(E), (S, E))
            t_grid = jnp.broadcast_to(rows[:, None], (S, E))
            buf = jnp.full((E, C + 1), S, jnp.int32).at[e_grid, slot].set(t_grid)
            idx = buf[:, :C]
            valid = idx < S
            x_pad = jnp.concatenate([xf, jnp.zeros((1, d), xf.dtype)], axis=0)
            xin = x_pad[idx]
            h = jax.nn.relu(jnp.einsum('ecd,edh->ech', xin, w1) + b1[:, None, :])
            out = jnp.einsum('ech,ehd->ecd', h, w2) + b2[:, None, :]
            w_pad = jnp.concatenate([w_te, jnp.zeros((1, E), xf.dtype)], axis=0)
            tok_w = w_pad[idx, jnp.arange(E)[:, None]]
            out = out * jnp.where(valid, tok_w, 0.0)[:, :, None]
            final = jnp.zeros((S + 1, d), xf.dtype).at[idx.reshape(-1)].add(out.reshape(-1, d))[:S]
            return final.reshape(Bb, Tt, d)
        key = jax.random.key(seed)
        ks = jax.random.split(key, 7)
        s = 0.02
        return {'x': jax.random.normal(ks[0], (B, T, D_MODEL), jnp.float32), 'gate_w': jax.random.normal(ks[1], (D_MODEL, E), jnp.float32) * s, 'gate_b': jnp.zeros((E,), jnp.float32), 'w1': jax.random.normal(ks[2], (E, D_MODEL, FF), jnp.float32) * s, 'b1': jnp.zeros((E, FF), jnp.float32), 'w2': jax.random.normal(ks[3], (E, FF, D_MODEL), jnp.float32) * s, 'b2': jnp.zeros((E, D_MODEL), jnp.float32)}
    _L1_ffn_in = _L1_ffn_setup()
    _d = {'L0_attn_hidden_states': _L0_attn_in['hidden_states'], 'L0_attn_Wq': _L0_attn_in['Wq'], 'L0_attn_Wk': _L0_attn_in['Wk'], 'L0_attn_Wv': _L0_attn_in['Wv'], 'L0_attn_Wlr': _L0_attn_in['Wlr'], 'L0_attn_Wg': _L0_attn_in['Wg'], 'L0_attn_Wo': _L0_attn_in['Wo'], 'L0_attn_cq': _L0_attn_in['cq'], 'L0_attn_ck': _L0_attn_in['ck'], 'L0_attn_cv': _L0_attn_in['cv'], 'L0_attn_W_in_init': _L0_attn_in['W_in_init'], 'L0_attn_W_out_init': _L0_attn_in['W_out_init'], 'L0_attn_ln_g': _L0_attn_in['ln_g'], 'L0_attn_ln_b': _L0_attn_in['ln_b'], 'L0_ffn_W_router': _L0_ffn_in['W_router'], 'L0_ffn_W_gate': _L0_ffn_in['W_gate'], 'L0_ffn_W_up': _L0_ffn_in['W_up'], 'L0_ffn_W_down': _L0_ffn_in['W_down'], 'L1_attn_in_proj_w': _L1_attn_in['in_proj_w'], 'L1_attn_conv_w': _L1_attn_in['conv_w'], 'L1_attn_conv_b': _L1_attn_in['conv_b'], 'L1_attn_x_proj_w': _L1_attn_in['x_proj_w'], 'L1_attn_dt_proj_w': _L1_attn_in['dt_proj_w'], 'L1_attn_dt_proj_b': _L1_attn_in['dt_proj_b'], 'L1_attn_A_log': _L1_attn_in['A_log'], 'L1_attn_D_param': _L1_attn_in['D_param'], 'L1_attn_out_proj_w': _L1_attn_in['out_proj_w'], 'L1_ffn_gate_w': _L1_ffn_in['gate_w'], 'L1_ffn_gate_b': _L1_ffn_in['gate_b'], 'L1_ffn_w1': _L1_ffn_in['w1'], 'L1_ffn_b1': _L1_ffn_in['b1'], 'L1_ffn_w2': _L1_ffn_in['w2'], 'L1_ffn_b2': _L1_ffn_in['b2']}
    _x0 = _d['L0_attn_hidden_states']
    _d['L0_attn_hidden_states'] = jax.random.normal(jax.random.fold_in(jax.random.key(seed), 1), (8, 512, 128), dtype=_x0.dtype)
    del _x0
    return _d

def reference(L0_attn_hidden_states, L0_attn_Wq, L0_attn_Wk, L0_attn_Wv, L0_attn_Wlr, L0_attn_Wg, L0_attn_Wo, L0_attn_cq, L0_attn_ck, L0_attn_cv, L0_attn_W_in_init, L0_attn_W_out_init, L0_attn_ln_g, L0_attn_ln_b, L0_ffn_W_router, L0_ffn_W_gate, L0_ffn_W_up, L0_ffn_W_down, L1_attn_in_proj_w, L1_attn_conv_w, L1_attn_conv_b, L1_attn_x_proj_w, L1_attn_dt_proj_w, L1_attn_dt_proj_b, L1_attn_A_log, L1_attn_D_param, L1_attn_out_proj_w, L1_ffn_gate_w, L1_ffn_gate_b, L1_ffn_w1, L1_ffn_b1, L1_ffn_w2, L1_ffn_b2):

    def _L0_attn_ref(hidden_states, Wq, Wk, Wv, Wlr, Wg, Wo, cq, ck, cv, W_in_init, W_out_init, ln_g, ln_b):
        import jax, jax.numpy as jnp
        import numpy as np
        from jax import lax
        DIM = 128
        H = 16
        HD = DIM // H
        D_INNER = 4
        CHUNK = 16
        BASE_LR = 0.001
        KSZ = 4

        def short_conv(x, w):
            xT = jnp.transpose(x, (0, 2, 1))
            y = lax.conv_general_dilated(xT, w[:, None, :], window_strides=(1,), padding=[(KSZ - 1, 0)], feature_group_count=x.shape[-1], dimension_numbers=('NCH', 'OIH', 'NCH'))
            return jnp.transpose(y + xT, (0, 2, 1))

        def l2norm(x):
            return x / jnp.linalg.norm(x, axis=-1, keepdims=True)

        def attn(q, k, v):
            s = jnp.einsum('bqhd,bkhd->bhqk', q, k) / jnp.sqrt(jnp.asarray(q.shape[-1], q.dtype))
            p = jax.nn.softmax(s, axis=-1)
            return jnp.einsum('bhqk,bkhd->bqhd', p, v)

        def _forward(hidden_states, Wq, Wk, Wv, Wlr, Wg, Wo, cq, ck, cv, W_in_init, W_out_init, ln_g, ln_b):
            b, l, _ = hidden_states.shape
            q = l2norm(jax.nn.silu(short_conv(hidden_states @ Wq.T, cq)).reshape(b, l, H, HD))
            k = l2norm(jax.nn.silu(short_conv(hidden_states @ Wk.T, ck)).reshape(b, l, H, HD))
            v = jax.nn.silu(short_conv(hidden_states @ Wv.T, cv)).reshape(b, l, H, HD)
            lr = jax.nn.softplus(hidden_states @ Wlr.T + BASE_LR).reshape(b, l, H, 2)
            nc = l // CHUNK
            to_chunks = lambda x: x.reshape(b, nc, CHUNK, H, -1).transpose(1, 0, 2, 3, 4)
            qc, kc, vc, lrc = map(to_chunks, (q, k, v, lr))
            W_in0 = jnp.broadcast_to(W_in_init, (b, D_INNER, H, HD))
            W_out0 = jnp.broadcast_to(W_out_init, (b, D_INNER, H, HD))
            mask = jnp.tril(jnp.ones((CHUNK, CHUNK), jnp.float32))

            def step(carry, xs):
                W_in, W_out = carry
                q_t, k_t, v_t, lr_t = xs
                k_h = jax.nn.softmax(jnp.einsum('blhd,bDhd->blhD', k_t, W_in), axis=-1) * lr_t[..., 1:]
                q_h = jax.nn.softmax(jnp.einsum('blhd,bDhd->blhD', q_t, W_in), axis=-1)
                qk = jnp.einsum('bqhD,bkhD->bhqk', q_h, k_h) * mask
                o_t = jnp.einsum('bqhD,bDhd->bqhd', q_h, W_out) + jnp.einsum('bhqk,bkhd->bqhd', qk, v_t)
                W_out = W_out + jnp.einsum('bnhD,bnhd->bDhd', k_h, v_t)
                lr_in = lr_t[:, :1, :, 0:1]
                lr_out = lr_t[:, :1, :, 1:2]
                for _ in range(2):
                    g_out = -attn(W_in, k_t, v_t)
                    g_in = -attn(W_out, v_t, k_t)
                    W_in = W_in - lr_in * g_in
                    W_out = W_out - lr_out * g_out
                return ((W_in, W_out), o_t)
            _, o = lax.scan(step, (W_in0, W_out0), (qc, kc, vc, lrc))
            o = o.transpose(1, 0, 2, 3, 4).reshape(b, l, H, HD)
            mu = o.mean(-1, keepdims=True)
            var = ((o - mu) ** 2).mean(-1, keepdims=True)
            o = (o - mu) / jnp.sqrt(var + 1e-05) * ln_g + ln_b
            o = o.reshape(b, l, DIM)
            gate = hidden_states @ Wg.T
            return o * gate @ Wo.T
        return _forward(hidden_states, Wq, Wk, Wv, Wlr, Wg, Wo, cq, ck, cv, W_in_init, W_out_init, ln_g, ln_b)

    def _L0_ffn_ref(x, W_router, W_gate, W_up, W_down):
        import jax, jax.numpy as jnp
        import numpy as np
        B, S, D, F, E, TOPK = (4, 256, 128, 512, 8, 2)

        def _moe_forward(x, W_router, W_gate, W_up, W_down):
            logits = jnp.einsum('bsd,ed->bse', x, W_router)
            probs = jax.nn.softmax(logits, axis=-1)
            gates, indices = jax.lax.top_k(probs, TOPK)
            gates = gates / jnp.sum(gates, axis=-1, keepdims=True)
            weights = jnp.sum(gates[..., None] * jax.nn.one_hot(indices, E, dtype=x.dtype), axis=-2)
            weights_e = jnp.moveaxis(weights, -1, 0)

            def body(acc, params):
                wg, wu, wd, wt = params
                gate = jax.nn.silu(jnp.einsum('bsd,fd->bsf', x, wg))
                up = jnp.einsum('bsd,fd->bsf', x, wu)
                y = jnp.einsum('bsf,df->bsd', gate * up, wd)
                return (acc + wt[..., None] * y, None)
            out, _ = jax.lax.scan(body, jnp.zeros_like(x), (W_gate, W_up, W_down, weights_e))
            return out
        return _moe_forward(x, W_router, W_gate, W_up, W_down)

    def _L1_attn_ref(x, in_proj_w, conv_w, conv_b, x_proj_w, dt_proj_w, dt_proj_b, A_log, D_param, out_proj_w):
        import jax, jax.numpy as jnp
        import numpy as np
        DIM, D_INNER, D_STATE, DT_RANK, D_CONV = (128, 256, 16, 64, 4)
        BATCH, SEQ = (2, 128)

        def _silu(v):
            return v * jax.nn.sigmoid(v)

        def _ssm_forward(x, in_proj_w, conv_w, conv_b, x_proj_w, dt_proj_w, dt_proj_b, A_log, D_param, out_proj_w):
            b, l, _ = x.shape
            d_inner, d_conv = (conv_w.shape[0], conv_w.shape[2])
            dt_rank, n = (dt_proj_w.shape[0], A_log.shape[1])
            x_and_res = x @ in_proj_w
            xp, res = (x_and_res[..., :d_inner], x_and_res[..., d_inner:])
            h = jax.lax.conv_general_dilated(xp.transpose(0, 2, 1), conv_w, window_strides=(1,), padding=[(d_conv - 1, 0)], dimension_numbers=('NCH', 'OIH', 'NCH'), feature_group_count=d_inner) + conv_b[None, :, None]
            h = _silu(h.transpose(0, 2, 1))
            A = -jnp.exp(A_log)
            x_dbl = h @ x_proj_w
            dlt, Bm, Cm = (x_dbl[..., :dt_rank], x_dbl[..., dt_rank:dt_rank + n], x_dbl[..., dt_rank + n:])
            delta = jax.nn.softplus(dlt @ dt_proj_w + dt_proj_b)
            deltaA = jnp.exp(jnp.einsum('bld,dn->bldn', delta, A))
            deltaB_u = (delta * h)[..., None] * Bm[:, :, None, :]

            def step(state, t):
                dA_t, dBu_t, c_t = t
                state = dA_t * state + dBu_t
                y_t = jnp.einsum('bdn,bn->bd', state, c_t)
                return (state, y_t)
            init = jnp.zeros((b, d_inner, n), h.dtype)
            _, ys = jax.lax.scan(step, init, (deltaA.transpose(1, 0, 2, 3), deltaB_u.transpose(1, 0, 2, 3), Cm.transpose(1, 0, 2)))
            y = ys.transpose(1, 0, 2) + h * D_param
            y = y * _silu(res)
            return y @ out_proj_w
        return _ssm_forward(x, in_proj_w, conv_w, conv_b, x_proj_w, dt_proj_w, dt_proj_b, A_log, D_param, out_proj_w)

    def _L1_ffn_ref(x, gate_w, gate_b, w1, b1, w2, b2):
        import jax, jax.numpy as jnp
        import numpy as np
        D_MODEL = 128
        FF = 512
        E = 8
        TOP_K = 2
        CAP_FACTOR = 1.25
        B, T = (4, 256)

        def _moe_forward(x, gate_w, gate_b, w1, b1, w2, b2):
            Bb, Tt, d = x.shape
            S = Bb * Tt
            C = int(CAP_FACTOR * S / E)
            xf = x.reshape(S, d)
            logits = xf @ gate_w + gate_b
            probs = jax.nn.softmax(logits, axis=1)
            topk_p, topk_i = jax.lax.top_k(probs, TOP_K)
            topk_pn = topk_p / jnp.sum(topk_p, axis=1, keepdims=True)
            rows = jnp.arange(S)
            w_te = jnp.zeros((S, E), xf.dtype).at[rows[:, None], topk_i].set(topk_pn)
            mask = jnp.zeros((S, E), bool).at[rows[:, None], topk_i].set(True)
            rank = jnp.cumsum(mask.astype(jnp.int32), axis=0)
            slot = jnp.where(mask & (rank <= C), rank - 1, C)
            e_grid = jnp.broadcast_to(jnp.arange(E), (S, E))
            t_grid = jnp.broadcast_to(rows[:, None], (S, E))
            buf = jnp.full((E, C + 1), S, jnp.int32).at[e_grid, slot].set(t_grid)
            idx = buf[:, :C]
            valid = idx < S
            x_pad = jnp.concatenate([xf, jnp.zeros((1, d), xf.dtype)], axis=0)
            xin = x_pad[idx]
            h = jax.nn.relu(jnp.einsum('ecd,edh->ech', xin, w1) + b1[:, None, :])
            out = jnp.einsum('ech,ehd->ecd', h, w2) + b2[:, None, :]
            w_pad = jnp.concatenate([w_te, jnp.zeros((1, E), xf.dtype)], axis=0)
            tok_w = w_pad[idx, jnp.arange(E)[:, None]]
            out = out * jnp.where(valid, tok_w, 0.0)[:, :, None]
            final = jnp.zeros((S + 1, d), xf.dtype).at[idx.reshape(-1)].add(out.reshape(-1, d))[:S]
            return final.reshape(Bb, Tt, d)
        return _moe_forward(x, gate_w, gate_b, w1, b1, w2, b2)
    x = L0_attn_hidden_states
    xn = _layernorm(x, axis=-1)
    s = _L0_attn_ref(xn, L0_attn_Wq, L0_attn_Wk, L0_attn_Wv, L0_attn_Wlr, L0_attn_Wg, L0_attn_Wo, L0_attn_cq, L0_attn_ck, L0_attn_cv, L0_attn_W_in_init, L0_attn_W_out_init, L0_attn_ln_g, L0_attn_ln_b)
    g = _silu(_L0_ffn_ref(xn, L0_ffn_W_router, L0_ffn_W_gate, L0_ffn_W_up, L0_ffn_W_down))
    x = x + s * g
    xn = _layernorm(x, axis=-1)
    s = _L1_attn_ref(xn, L1_attn_in_proj_w, L1_attn_conv_w, L1_attn_conv_b, L1_attn_x_proj_w, L1_attn_dt_proj_w, L1_attn_dt_proj_b, L1_attn_A_log, L1_attn_D_param, L1_attn_out_proj_w)
    g = _silu(_L1_ffn_ref(xn, L1_ffn_gate_w, L1_ffn_gate_b, L1_ffn_w1, L1_ffn_b1, L1_ffn_w2, L1_ffn_b2))
    x = x + s * g
    return x

_drawn_inputs = setup_inputs


def setup_inputs(seed=0):
    import zlib

    import numpy as np

    out = dict(_drawn_inputs(seed))
    spreads = {'L0_attn_ln_g': (1.0, 0.2),
     'L0_attn_ln_b': (0.0, 0.1),
     'L1_attn_D_param': (1.0, 0.2),
     'L1_ffn_gate_b': (0.0, 0.1),
     'L1_ffn_b1': (0.0, 0.1),
     'L1_ffn_b2': (0.0, 0.1)}
    factors = {}
    for name, (base, spread) in spreads.items():
        noise = np.random.default_rng([zlib.crc32(name.encode()), seed]).standard_normal(out[name].shape)
        drawn = base * np.exp(spread * noise) if base else spread * noise
        out[name] = jnp.asarray(drawn.astype(out[name].dtype))
    for name, factor in factors.items():
        out[name] = (out[name] * factor).astype(out[name].dtype)
    return out
```

```python
from contextlib import ExitStack

import concourse.bass as bass
from concourse import mybir

F32 = mybir.dt.float32
I32 = mybir.dt.int32
U32 = mybir.dt.uint32
ALU = mybir.AluOpType
ACT = mybir.ActivationFunctionType
AX_X = mybir.AxisListType.X

P = 128
B, L, D = 8, 512, 128
T = B * L
NT = T // P
G4 = NT // 4
H, HD, DI, CH = 16, 8, 4, 16
NCH = L // CH
E = 8
F = 512
FC = F // P
CONV = 4
TILES_A = 2 * T // P + E
CAP = int(1.25 * T / E)
CT = CAP // P
DIN, NS, DTR = 256, 16, 64
GD = DIN // P
TPS = 3
ROUTED_STEPS = TILES_A // TPS
EPS = 1e-5
SKIP = 1 << 20


def bc(ap, axis, n):
    a = ap.unsqueeze(axis)
    shape = list(a.shape)
    shape[axis] = n
    return a.broadcast_to(shape)


def flat(a):
    return a if len(a.shape) == 2 else a.rearrange("p a b -> p (a b)") if len(a.shape) == 3 else a.rearrange("p a b c -> p (a b c)")


class Region:

    def __init__(self, tile):
        self.cols, self.at = flat(tile), 0

    def take(self, *shape):
        n = 1
        for s in shape:
            n *= s
        a = self.cols[:, self.at:self.at + n]
        self.at += n
        assert self.at <= self.cols.shape[1]
        if len(shape) == 2:
            a = a.rearrange("p (a b) -> p a b", a=shape[0])
        if len(shape) == 3:
            a = a.rearrange("p (a b c) -> p a b c", a=shape[0], b=shape[1])
        return a


class Order:

    def __init__(self, eng, sem):
        self.eng, self.sem, self.base, self.n = eng, sem, 0, 0

    def mark(self, ins):
        self.n += 1
        ins.then_inc(self.sem, 1)
        return self.n

    def wait(self, n=None):
        n = self.n if n is None else n
        v = self.base + n
        self.eng.wait_ge(self.sem, v)

    def link(self, ins):
        self.mark(ins)
        self.wait()

    def loop(self, c, first, per):
        self.base, self.n = c * per + first, 0

    def end(self, first, per, trips):
        assert self.n == per, (self.n, per)
        self.base, self.n = first + per * trips, 0

    def total(self):
        return self.base + self.n


def build(nc, d, stop=None):
    with ExitStack() as ctx:
        def sb(name, shape, dt=F32):
            return ctx.enter_context(nc.sbuf_tensor(name, shape, dt))

        def sem(name):
            return ctx.enter_context(nc.semaphore(name))

        def dram(name, shape):
            return nc.dram_tensor(name, shape, F32).ap()

        qkv_scr = dram("qkv_scr", [3, P, T])
        lr_scr = dram("lr_scr", [2 * H, T])
        o_scr = dram("o_scr", [P, T])
        slots_x = dram("slots_x", [TILES_A * P, D])
        slots_y = dram("slots_y", [TILES_A * P, D])
        slots_x1 = dram("slots_x1", [E * CAP, D])
        slots_y1 = dram("slots_y1", [E * CAP, D])

        ps = ctx.enter_context(nc.psum_tensor("ps", [P, 8, 512], F32))
        ident = sb("ident", [P, P])
        upper = sb("upper", [P, P])
        ones = sb("ones", [P, P])
        iota_e = sb("iota_e", [P, E])
        iota_t = sb("iota_t", [P, TILES_A])
        first_of_e = sb("first_of_e", [P, E, NT])
        x = sb("x", [P, NT, D])
        xn = sb("xn", [P, NT, D])
        xnT = sb("xnT", [P, T])
        stats = sb("stats", [P, NT, 6])
        mv = sb("mv", [P, NT, 2])
        rstd = sb("rstd", [P, NT])
        wproj = sb("wproj", [P, 4 * P])
        wlr = sb("wlr", [P, 2 * H])
        wo = sb("wo", [P, D])
        taps = sb("taps", [P, 3, CONV])
        ln_gb = sb("ln_gb", [P, 2])
        wrt = sb("wrt", [P, E])
        wg_a = sb("wg_a", [P, E * F])
        wu_a = sb("wu_a", [P, E * F])
        wd_a = sb("wd_a", [P, E * FC * D])
        cv = sb("cv", [P, 4, L])
        gateT = sb("gateT", [P, T])
        K = sb("K", [P, HD, L])
        V = sb("V", [P, HD, L])
        Q = sb("Q", [P, HD, L])
        O = sb("O", [P, HD, L])
        nrm = sb("nrm", [P, 2, L])
        LR = sb("LR", [P, 2, L])
        lmx = sb("lmx", [P, NT])
        top = sb("top", [P, NT, 8])
        topi = sb("topi", [P, NT, 8], U32)
        e12 = sb("e12", [P, 2, NT])
        w12 = sb("w12", [P, 2, NT])
        wsum = sb("wsum", [P, NT])
        slot = sb("slot", [P, 2, NT])
        kept = sb("kept", [P, 2, NT])
        sl_put = sb("sl_put", [P, 2, NT], I32)
        sl_get = sb("sl_get", [P, 2, NT], I32)
        tl = sb("tl", [P, 3, E])
        tl_i = sb("tl_i", [P, E], I32)
        texp = sb("texp", [P, TILES_A])
        texp_i = sb("texp_i", [P, TILES_A], I32)
        r = Region(O[:])
        lg, mask, rank, keep = (r.take(NT, E) for _ in range(4))
        oh, prod = (r.take(2, NT, E) for _ in range(2))
        tot, inc = (r.take(E, NT) for _ in range(2))
        tcmp = r.take(TILES_A, E)
        zero = r.take(4 * D)
        TMP = xnT[:].rearrange("p (e t) -> p e t", e=HD)
        r = Region(xnT[:])
        xg, xgT, yg = r.take(TPS, D), r.take(TPS, P), r.take(TPS, D)
        r = Region(xn[:])
        th, hid, hidT = r.take(TPS, F), r.take(TPS, F), r.take(2, F)
        r = Region(cv[:])
        PP, GP = r.take(2, DI * CH, HD), r.take(2, DI * HD, CH)
        r = Region(x[:])
        LZ, PK, PQ = r.take(2, L), r.take(DI, CH, HD), r.take(DI, CH, HD)
        SC, CS = r.take(DI * HD, CH + 1), r.take(DI * HD, CH + 1)
        SS, EX = r.take(2, DI, CH), r.take(2, DI, CH)
        SQ, EK, EQ = r.take(DI, CH), r.take(DI, CH), r.take(DI, CH)
        OP = Region(LZ).take(HD, CH, DI)
        X = sb("X", [P, 2 * DI * HD])
        MK = sb("MK", [P, CH])
        MQ = sb("MQ", [P, CH])
        ZK = sb("ZK", [P, CH])
        ZQ = sb("ZQ", [P, CH])
        M8 = sb("M8", [P, 2 * DI])
        Z8 = sb("Z8", [P, 2 * DI])
        seg = sb("seg", [P, DI * HD, CH + 1])
        GR = sb("GR", [P, 2 * DI * HD])

        r = Region(wg_a[:])
        w_in1, w_x1, w_dt1, w_o1 = r.take(2 * DIN), r.take(GD, DTR + 2 * NS), r.take(DIN), r.take(GD, D)
        conv_w1, conv_b1, dt_b1, d_1 = r.take(GD, CONV), r.take(GD), r.take(GD), r.take(GD)
        a_neg, w_rt1, b_rt1, b_e1, b_e2 = r.take(GD, NS), r.take(E), r.take(E), r.take(E, FC), r.take(E * D)
        r = Region(wu_a[:])
        w_e1, w_e2, hid1 = r.take(F), r.take(FC, D), r.take(FC, CAP)
        r = Region(wd_a[:])
        xg1, xgT1, yg1 = r.take(CT, D), r.take(CAP), r.take(CT, D)
        pick = gateT[:].rearrange("p (r c) -> p r c", c=P)
        r = Region(K[:])
        h1, res1, del1, dh1 = (r.take(GD, L) for _ in range(4))
        r = Region(V[:])
        xd1, dA, sp1 = r.take(L), r.take(4, L), r.take(GD, L)
        r = Region(Q[:])
        dBu, st1, yc1 = r.take(2, L), r.take(2, L), r.take(4, L)
        b_e1_now = sb("b_e1_now", [P, FC])
        s1 = O[:].rearrange("p e t -> p (e t)")

        x_loaded = sem("x_loaded")
        w_loaded = sem("w_loaded")
        we_loaded = sem("we_loaded")
        consts_ready = sem("consts_ready")
        pool_order = sem("pool_order")
        zeroed = sem("zeroed")
        dve_order = sem("dve_order")
        act_order = sem("act_order")
        ln_var = sem("ln_var")
        ln_std = sem("ln_std")
        xn_ready = sem("xn_ready")
        xnT_ps = sem("xnT_ps")
        xnT_copied = sem("xnT_copied")
        proj_ps = sem("proj_ps")
        gate_ps = sem("gate_ps")
        lr_ps = sem("lr_ps")
        tap_first = sem("tap_first")
        taps_ready = sem("taps_ready")
        conv_done = sem("conv_done")
        silu_done = sem("silu_done")
        gate_copied = sem("gate_copied")
        lr_copied = sem("lr_copied")
        stored = [sem(f"stored{i}") for i in range(4)]
        lr_stored = sem("lr_stored")
        heads_loaded = sem("heads_loaded")
        squared = sem("squared")
        norm2 = sem("norm2")
        norm_root = sem("norm_root")
        lr_in = sem("lr_in")
        lr_log = sem("lr_log")
        logits_ps = sem("logits_ps")
        logits_ready = sem("logits_ready")
        probs_ready = sem("probs_ready")
        mask_ready = sem("mask_ready")
        ranks_ps = sem("ranks_ps")
        slots_ready = sem("slots_ready")
        scattered = sem("scattered")
        exp_k = sem("exp_k")
        exp_q = sem("exp_q")
        exp_j = sem("exp_j")
        rec_k = sem("rec_k")
        rec_q = sem("rec_q")
        rec_j = sem("rec_j")
        xg_loaded = [sem(f"xg_loaded{k}") for k in range(TPS)]
        xg_used = sem("xg_used")
        xgT_copied = sem("xgT_copied")
        gu_ps = sem("gu_ps")
        tanh_done = sem("tanh_done")
        hid_ready = sem("hid_ready")
        hidT_ps = sem("hidT_ps")
        hidT_copied = sem("hidT_copied")
        y_ps = sem("y_ps")
        y_copied = sem("y_copied")
        y_stored = [sem(f"y_stored{k}") for k in range(TPS)]
        o_centred = sem("o_centred")
        o_squared = sem("o_squared")
        o_var = sem("o_var")
        o_root = sem("o_root")
        o_ready = sem("o_ready")
        o_stored = sem("o_stored")
        oT_loaded = sem("oT_loaded")
        oT_ready = sem("oT_ready")
        s_ps = sem("s_ps")
        s_used = sem("s_used")
        y_gathered = sem("y_gathered")
        mix_ready = sem("mix_ready")
        mix_silu = sem("mix_silu")
        x1_ready = sem("x1_ready")
        out_stored = sem("out_stored")

        w1_loaded = sem("w1_loaded")
        pick_order = sem("pick_order")
        pick_ready = sem("pick_ready")
        scattered1 = sem("scattered1")
        a_ready = sem("a_ready")
        inp_ps = sem("inp_ps")
        tap1_first = sem("tap1_first")
        conv1_done = sem("conv1_done")
        h1_ready = sem("h1_ready")
        xd_ps = sem("xd_ps")
        xd_copied = sem("xd_copied")
        dl_ps = sem("dl_ps")
        sp_ready = sem("sp_ready")
        delta_ready = sem("delta_ready")
        b_ps = sem("b_ps")
        c_ps = sem("c_ps")
        b_used = sem("b_used")
        dA_ready = sem("dA_ready")
        scanned = sem("scanned")
        yc_ready = sem("yc_ready")
        yc_used = sem("yc_used")
        yt_ready = sem("yt_ready")
        s1_ps = sem("s1_ps")
        s1_copied = sem("s1_copied")
        e1_loaded = sem("e1_loaded")
        xg1_loaded = sem("xg1_loaded")
        moe_ps = sem("moe_ps")
        moe_out = sem("moe_out")
        y1_stored = sem("y1_stored")
        y1_gathered = sem("y1_gathered")
        out_ready = sem("out_ready")

        sp_log = sem("sp_log")
        N_W1 = 13
        PIECES = 12
        NCU = 3 * B
        ZEROED = 16 * (TILES_A // 4 + E * CAP // (4 * P))

        block = ctx.enter_context(nc.Block())

        @block.sync
        def _(sp):
            for g in range(4):
                sp.dma_start(x[:, 8 * g:8 * g + 8, :],
                             d["x"].rearrange("(i p) c -> p i c", p=P)[:, 8 * g:8 * g + 8, :]).then_inc(x_loaded, 16)
            for dst, src in ((wproj[:], "wproj"), (wlr[:], "wlr"), (wo[:], "wo"),
                             (taps[:].rearrange("p a b -> p (a b)"), "taps"), (ln_gb[:], "ln_gb"), (wrt[:], "wrt"),
                             (X[:], "state0")):
                sp.dma_start(dst, d[src]).then_inc(w_loaded, 16)
            for dst, src in ((wg_a, "wg_a"), (wu_a, "wu_a"), (wd_a, "wd_a")):
                sp.dma_start(dst[:], d[src]).then_inc(we_loaded, 16)
            for cu in range(NCU):
                b, w = divmod(cu, 3)
                sp.wait_ge(silu_done, cu + 1)
                sp.dma_start(qkv_scr[w, :, b * L:(b + 1) * L], cv[:, cu % 4, :]).then_inc(stored[cu % 4], 16)
            sp.wait_ge(lr_copied, B)
            sp.dma_start(lr_scr, K[0:2 * H, :, :].rearrange("p a b -> p (a b)")).then_inc(lr_stored, 16)
            for s in stored:
                sp.wait_ge(s, 16 * (NCU // 4))
            sp.wait_ge(lr_stored, 16)
            for w, dst in ((1, K), (2, V), (0, Q)):
                for b in range(B):
                    sp.dma_start(dst[b * H:(b + 1) * H, :, :],
                                 qkv_scr[w].rearrange("(h e) (b t) -> b h e t", h=H, b=B)[b]).then_inc(heads_loaded, 16)
            for b in range(B):
                sp.dma_start(LZ[b * H:(b + 1) * H, :, :],
                             lr_scr.rearrange("(h j) (b t) -> b h j t", h=H, b=B)[b]).then_inc(heads_loaded, 16)
            sp.wait_ge(scattered, 16 * 2 * NT)
            sp.wait_ge(norm2, 2)
            for k in range(TPS):
                sp.dma_start(xg[:, k, :], slots_x[k * P:(k + 1) * P, :]).then_inc(xg_loaded[k], 16)
            with sp.Fori(0, ROUTED_STEPS - 1) as c:
                for k in range(TPS):
                    sp.wait_ge(xg_used, c * TPS + (k + 1))
                    sp.dma_start(xg[:, k, :], slots_x[bass.ds((c + 1) * (TPS * P) + k * P, P), :]).then_inc(xg_loaded[k], 16)
                for k in range(TPS):
                    sp.wait_ge(y_copied, c * TPS + (k + 2))
                    sp.dma_start(slots_y[bass.ds(c * (TPS * P) + k * P, P), :], yg[:, k, :]).then_inc(y_stored[k], 16)
            for k in range(TPS):
                j = (ROUTED_STEPS - 1) * TPS + k
                sp.wait_ge(y_copied, j + 2)
                sp.dma_start(slots_y[j * P:(j + 1) * P, :], yg[:, k, :]).then_inc(y_stored[k], 16)
            sp.wait_ge(o_centred, 1)
            for g in range(4):
                sp.dma_start(x[:, 8 * g:8 * g + 8, :],
                             d["x"].rearrange("(i p) c -> p i c", p=P)[:, 8 * g:8 * g + 8, :]).then_inc(x_loaded, 16)
            sp.wait_ge(o_ready, 1)
            for b in range(B):
                sp.dma_start(o_scr.rearrange("(h e) (b t) -> b h e t", h=H, b=B)[b],
                             O[b * H:(b + 1) * H, :, :]).then_inc(o_stored, 16)
            sp.wait_ge(o_stored, 16 * B)
            sp.dma_start(K[:].rearrange("p a b -> p (a b)"), o_scr).then_inc(oT_loaded, 16)
            sp.wait_ge(y_copied, TILES_A + 1)
            for dst, src in ((w_in1, "w_in1"), (flat(w_x1), "w_x1"), (w_dt1[0:DTR, :], "w_dt1"), (flat(w_o1), "w_o1"),
                             (flat(conv_w1), "conv_w1"), (conv_b1, "conv_b1"), (dt_b1, "dt_b1"), (d_1, "d_1"),
                             (flat(a_neg), "a_log"), (w_rt1, "w_rt1"), (b_rt1, "b_rt1"), (flat(b_e1), "b_e1"),
                             (b_e2[0:1, :], "b_e2")):
                src = d[src].partition_broadcast(P).rearrange("p o e -> p (o e)") if src == "b_rt1" else d[src]
                sp.dma_start(dst, src).then_inc(w1_loaded, 16)

            def expert_loads(e):
                sp.dma_start(w_e1, d["w_e1"][bass.ds(e * P, P), :]).then_inc(e1_loaded, 16)
                sp.dma_start(flat(w_e2), d["w_e2"][:, bass.ds(e * FC * D, FC * D)]).then_inc(e1_loaded, 16)
                sp.dma_start(xg1, slots_x1[bass.ds(e * CAP, CAP), :].rearrange("(i p) c -> p i c", p=P)).then_inc(xg1_loaded, 16)

            def expert_store(e):
                sp.wait_ge(moe_out, e * PIECES + (PIECES + 1))
                sp.dma_start(slots_y1[bass.ds(e * CAP, CAP), :].rearrange("(i p) c -> p i c", p=P), yg1).then_inc(y1_stored, 16)

            sp.wait_ge(scattered1, 16 * 2 * NT)
            expert_loads(0)
            with sp.Fori(0, E - 1) as e:
                expert_store(e)
                expert_loads(e + 1)
            expert_store(E - 1)
            for g in range(G4):
                sp.wait_ge(out_ready, g + 1)
                sp.dma_start(d["out"].rearrange("(i p) c -> p i c", p=P)[:, 4 * g:4 * g + 4, :], x[:, 4 * g:4 * g + 4, :]).then_inc(out_stored, 16)
            sp.wait_ge(out_stored, 16 * G4)

        @block.gpsimd
        def _(pool):
            o = Order(pool, pool_order)
            o.mark(pool.memset(ident[:], 0.0))
            o.mark(pool.memset(ones[:], 1.0))
            o.mark(pool.memset(zero, 0.0))
            o.mark(pool.memset(first_of_e[:], 1.0))
            o.link(pool.memset(seg[:], 1.0))
            pool.affine_select(out=ident[:], in_=ident[:], compare_op=ALU.not_equal, fill=1.0, base=0,
                               pattern=[[-1, P]], channel_multiplier=1).then_inc(consts_ready, 1)
            pool.affine_select(out=upper[:], in_=ones[:], compare_op=ALU.is_ge, fill=0.0, base=0,
                               pattern=[[1, P]], channel_multiplier=-1).then_inc(consts_ready, 1)
            pool.iota(iota_e[:], [[1, E]], base=0, channel_multiplier=0,
                      allow_small_or_imprecise_dtypes=True).then_inc(consts_ready, 1)
            pool.iota(iota_t[:], [[1, TILES_A]], base=0, channel_multiplier=0,
                      allow_small_or_imprecise_dtypes=True).then_inc(consts_ready, 1)
            pool.memset(first_of_e[:, :, 0], 0.0).then_inc(consts_ready, 1)
            pool.memset(seg[:, :, 0], 0.0).then_inc(consts_ready, 1)
            for r in range(TILES_A // 4):
                pool.dma_start(slots_x[r * 4 * P:(r + 1) * 4 * P, :].rearrange("(p i) c -> p (i c)", p=P),
                               zero).then_inc(zeroed, 16)
            for r in range(E * CAP // (4 * P)):
                pool.dma_start(slots_x1[r * 4 * P:(r + 1) * 4 * P, :].rearrange("(p i) c -> p (i c)", p=P),
                               zero).then_inc(zeroed, 16)
            pool.wait_ge(zeroed, ZEROED)
            pool.wait_ge(slots_ready, 1)
            pool.wait_ge(xn_ready, NT)
            for i in range(NT):
                for j in range(2):
                    pool.indirect_dma_start(out=slots_x, out_offset=bass.IndirectOffsetOnAxis(ap=sl_put[:, j, i:i + 1], axis=0),
                                            in_=xn[:, i, :], in_offset=None).then_inc(scattered, 16)
            for k in range(TPS):
                pool.wait_ge(y_stored[k], 16 * (ROUTED_STEPS + 1))
            pool.wait_ge(o_centred, 1)
            for i in range(NT):
                for j, dst in enumerate((V, Q)):
                    rows = dst[:].rearrange("p a b -> p (a b)").rearrange("p (i c) -> p i c", c=D)
                    pool.indirect_dma_start(out=rows[:, i, :], out_offset=None, in_=slots_y,
                                            in_offset=bass.IndirectOffsetOnAxis(ap=sl_put[:, j, i:i + 1], axis=0)
                                            ).then_inc(y_gathered, 16)
            pool.wait_ge(oT_ready, 1)
            pool.wait_ge(y_gathered, 16 * 2 * NT)
            pool.memset(pick[2 * NS * 2:2 * NS * 3], 0.0).then_inc(pick_order, 1)
            pool.wait_ge(pick_order, 1)
            pool.affine_select(out=pick[DTR:DTR + 2 * NS], in_=pick[DTR:DTR + 2 * NS], compare_op=ALU.not_equal, fill=1.0,
                               base=0, pattern=[[-1, 2 * NS], [0, P]], channel_multiplier=1).then_inc(pick_ready, 1)
            pool.wait_ge(pick_ready, 1)
            pool.wait_ge(slots_ready, 2)
            pool.wait_ge(xn_ready, 2 * NT)
            for i in range(NT):
                for j in range(2):
                    pool.indirect_dma_start(out=slots_x1, out_offset=bass.IndirectOffsetOnAxis(ap=sl_put[:, j, i:i + 1], axis=0),
                                            in_=xn[:, i, :], in_offset=None, bounds_check=E * CAP - 1,
                                            oob_is_err=False).then_inc(scattered1, 16)
            pool.wait_ge(y1_stored, 16 * (E + 1))
            pool.wait_ge(s1_copied, B + 1)
            for i in range(NT):
                for j, dst in enumerate((V, Q)):
                    rows = dst[:].rearrange("p a b -> p (a b)").rearrange("p (i c) -> p i c", c=D)
                    pool.indirect_dma_start(out=rows[:, i, :], out_offset=None, in_=slots_y1,
                                            in_offset=bass.IndirectOffsetOnAxis(ap=sl_get[:, j, i:i + 1], axis=0)
                                            ).then_inc(y1_gathered, 16)

        @block.tensor
        def _(pe):
            pe.wait_ge(consts_ready, 6)

            def transposes(layer):
                for g in range(G4):
                    n = layer * G4 + g
                    if n >= 2:
                        pe.wait_ge(xnT_copied, n - 1)
                    for j in range(4):
                        i = 4 * g + j
                        pe.wait_ge(xn_ready, layer * NT + i + 1)
                        t = pe.transpose(ps[:, g % 2, j * P:(j + 1) * P], xn[:, i, :], ident[:])
                    t.then_inc(xnT_ps, 1)

            def router(layer, w):
                pe.wait_ge(xnT_copied, (layer + 1) * G4)
                for i in range(NT):
                    m = pe.matmul(ps[:, 0, i * E:(i + 1) * E], xnT[:, i * P:(i + 1) * P], w, start=True, stop=True)
                m.then_inc(logits_ps, 1)
                pe.wait_ge(mask_ready, layer + 1)
                mk = mask.rearrange("p i e -> p (i e)")
                pe.matmul(ps[:, 1, 0:NT * E], upper[:], mk, start=True, stop=True).then_inc(ranks_ps, 1)
                pe.matmul(ps[:, 0, 0:NT * E], ones[:], mk, start=True, stop=True).then_inc(ranks_ps, 1)

            transposes(0)
            pe.wait_ge(w_loaded, 16 * 7)
            for b in range(B):
                rhs = xnT[:, b * L:(b + 1) * L]
                pe.wait_ge(xnT_copied, b + 1)
                for w in range(3):
                    cu = 3 * b + w
                    if cu >= 4:
                        pe.wait_ge(conv_done, cu - 3)
                    pe.matmul(ps[:, 2 + cu % 4, :], wproj[:, w * P:(w + 1) * P], rhs, start=True, stop=True).then_inc(proj_ps, 1)
                if b >= 1:
                    pe.wait_ge(gate_copied, b)
                    pe.wait_ge(lr_copied, b)
                pe.matmul(ps[:, 6, :], wproj[:, 3 * P:4 * P], rhs, start=True, stop=True).then_inc(gate_ps, 1)
                pe.matmul(ps[0:2 * H, 7, :], wlr[:], rhs, start=True, stop=True).then_inc(lr_ps, 1)
            router(0, wrt[:])
            pe.wait_ge(slots_ready, 1)
            pe.wait_ge(we_loaded, 16 * 3)
            def up(c, k):
                n0 = c * TPS
                off = pe.value_load(texp_i[0:1, bass.ds(n0 + k, 1)], min_val=0, max_val=(E - 1) * F)
                pe.wait_ge(xg_loaded[k], c * 16 + 16)
                pe.transpose(ps[:, 0, 0:P], xg[:, k, :], ident[:]).then_inc(xg_used, 1)
                pe.wait_ge(xgT_copied, n0 + (k + 1))
                if k == 2:
                    pe.wait_ge(hid_ready, n0 + 1)
                pe.matmul(ps[:, 1 + 2 * (k % 2), :], xgT[:, k, :], wg_a[:, bass.ds(off, F)], start=True, stop=True).then_inc(gu_ps, 1)
                pe.matmul(ps[:, 2 + 2 * (k % 2), :], xgT[:, k, :], wu_a[:, bass.ds(off, F)], start=True, stop=True).then_inc(gu_ps, 1)

            def down(c, k):
                n0 = c * TPS
                off = pe.value_load(texp_i[0:1, bass.ds(n0 + k, 1)], min_val=0, max_val=(E - 1) * F)
                pe.wait_ge(hid_ready, n0 + (k + 1))
                if k >= 1:
                    pe.wait_ge(hidT_copied, n0 + k)
                for f in range(FC):
                    t = pe.transpose(ps[:, 5, f * P:(f + 1) * P], hid[:, k, f * P:(f + 1) * P], ident[:])
                t.then_inc(hidT_ps, 1)
                pe.wait_ge(hidT_copied, n0 + (k + 1))
                if k != 1:
                    pe.wait_ge(y_copied, n0 + (k // 2 + 1))
                for f in range(FC):
                    m = pe.matmul(ps[:, 6 + k % 2, 0:D], hidT[:, k % 2, f * P:(f + 1) * P],
                                  wd_a[:, bass.ds(off + f * D, D)], start=(f == 0), stop=(f == FC - 1))
                m.then_inc(y_ps, 1)

            with pe.Fori(0, ROUTED_STEPS) as c:
                up(c, 0)
                up(c, 1)
                down(c, 0)
                up(c, 2)
                down(c, 1)
                down(c, 2)
            pe.wait_ge(oT_ready, 1)
            oT = K[:].rearrange("p a b -> p (a b)")
            for g in range(G4):
                if g >= 2:
                    pe.wait_ge(s_used, g - 1)
                for j in range(4):
                    i = 4 * g + j
                    m = pe.matmul(ps[:, 1 + g % 2, j * P:(j + 1) * P], oT[:, i * P:(i + 1) * P], wo[:], start=True, stop=True)
                m.then_inc(s_ps, 1)

            transposes(1)
            pe.wait_ge(w1_loaded, 16 * N_W1)
            router(1, w_rt1)
            pe.wait_ge(slots_ready, 2)
            pe.wait_ge(pick_ready, 1)

            def piece(c, p):
                if p == 0:
                    pe.wait_ge(xg1_loaded, c * 16 + 16)
                    pe.wait_ge(e1_loaded, c * 32 + 32)
                pe.wait_ge(moe_out, c * PIECES + (3 if p == 2 else 11 if p >= 10 else max(p, 1)))
                bank = ps[:, 6 + p % 2, :]
                if p < 2:
                    for i in range(4 * p, min(4 * p + 4, CT)):
                        m = pe.transpose(bank[:, (i % 4) * P:(i % 4 + 1) * P], xg1[:, i, :], ident[:])
                elif p < 10:
                    f, half = divmod(p - 2, 2)
                    m = pe.matmul(bank[:, 0:CAP // 2], w_e1[:, f * P:(f + 1) * P],
                                  xgT1[:, half * (CAP // 2):(half + 1) * (CAP // 2)], start=True, stop=True)
                else:
                    for i in range(4 * (p - 10), min(4 * (p - 10) + 4, CT)):
                        o_ = bank[:, (i % 4) * D:(i % 4 + 1) * D]
                        for f in range(FC):
                            pe.matmul(o_, hid1[:, f, i * P:(i + 1) * P], w_e2[:, f, :], start=(f == 0), stop=False)
                        m = pe.matmul(o_, ones[0:1, :], b_e2[0:1, bass.ds(c * D, D)], start=False, stop=True)
                m.then_inc(moe_ps, 1)

            with pe.Fori(0, B) as c:
                pe.wait_ge(s1_copied, c + 1)
                for g in range(2 * GD):
                    pe.matmul(ps[:, g, :], w_in1[:, g * P:(g + 1) * P], xnT[:, bass.ds(c * L, L)], start=True, stop=True).then_inc(inp_ps, 1)
                pe.wait_ge(h1_ready, c * GD + GD)
                for g in range(GD):
                    m = pe.matmul(ps[0:DTR + 2 * NS, 4, :], w_x1[:, g, :], h1[:, g, :], start=(g == 0), stop=(g == GD - 1))
                m.then_inc(xd_ps, 1)
                pe.wait_ge(xd_copied, c + 1)
                for g in range(GD):
                    pe.matmul(ps[:, g, :], w_dt1[0:DTR, g * P:(g + 1) * P], xd1[0:DTR, :], start=True, stop=True).then_inc(dl_ps, 1)

                def accumulate(n):
                    for g in range(GD):
                        pe.wait_ge(yc_ready, c * (GD * NS) + (GD * n + g + 1))
                        pe.matmul(ps[:, 4 + g, :], ident[:], yc1[:, (GD * n + g) % 4, :], start=(n == 0), stop=(n == NS - 1)).then_inc(yc_used, 1)

                for n in range(NS):
                    if n >= 2:
                        pe.wait_ge(b_used, c * NS + (n - 1))
                    pe.matmul(ps[:, 2 + n % 2, :], pick[DTR:DTR + 2 * NS, n, :], xd1[DTR:DTR + 2 * NS, :], start=True, stop=True).then_inc(b_ps, 1)
                    if n == 0:
                        pe.wait_ge(sp_ready, c * GD + GD)
                    pe.matmul(ps[:, n % 2, :], pick[DTR:DTR + 2 * NS, NS + n, :], xd1[DTR:DTR + 2 * NS, :], start=True, stop=True).then_inc(c_ps, 1)
                    if n >= 1:
                        accumulate(n - 1)
                    if 1 <= n <= PIECES:
                        piece(c, n - 1)
                accumulate(NS - 1)
                pe.wait_ge(yt_ready, c * GD + GD)
                for j in range(4):
                    for g in range(GD):
                        m = pe.matmul(ps[:, 0, j * D:(j + 1) * D], h1[:, g, j * P:(j + 1) * P], w_o1[:, g, :], start=(g == 0), stop=(g == GD - 1))
                m.then_inc(s1_ps, 1)

        @block.scalar
        def _(act):
            o = Order(act, act_order)
            for s in (y_copied, moe_out, s1_copied):
                act.sem_inc(s, 1)
            for s in (*y_stored, y1_stored):
                act.sem_inc(s, 16)
            act.wait_ge(ln_var, 1)
            act.activation(rstd[:], rstd[:], ACT.Sqrt).then_inc(ln_std, 1)
            for g in range(G4):
                act.wait_ge(xnT_ps, g + 1)
                act.activation(xnT[:, g * 512:(g + 1) * 512], ps[:, g % 2, :], ACT.Copy).then_inc(xnT_copied, 1)

            def silu(cu):
                act.wait_ge(conv_done, cu + 1)
                act.activation(cv[:, cu % 4, :], cv[:, cu % 4, :], ACT.Silu).then_inc(silu_done, 1)

            act.wait_ge(taps_ready, 1)
            for cu in range(NCU):
                b, w = divmod(cu, 3)
                act.wait_ge(proj_ps, cu + 1)
                if cu >= 4:
                    act.wait_ge(stored[cu % 4], 16 * (cu // 4))
                act.activation(cv[:, cu % 4, :], ps[:, 2 + cu % 4, :], ACT.Copy, scale=taps[:, w, 3:4]).then_inc(tap_first, 1)
                if cu >= 1:
                    silu(cu - 1)
                if w == 2:
                    act.wait_ge(gate_ps, b + 1)
                    act.activation(gateT[:, b * L:(b + 1) * L], ps[:, 6, :], ACT.Copy).then_inc(gate_copied, 1)
                    act.wait_ge(lr_ps, b + 1)
                    act.activation(K[0:2 * H, b, :], ps[0:2 * H, 7, :], ACT.Copy).then_inc(lr_copied, 1)
            silu(NCU - 1)
            act.wait_ge(logits_ready, 1)
            act.activation(lg, lg, ACT.Exp).then_inc(probs_ready, 1)
            act.wait_ge(heads_loaded, 16 * 4 * B)
            act.wait_ge(logits_ps, 1)
            for n, t in enumerate((K, Q)):
                if n == 1:
                    act.wait_ge(norm2, 1)
                act.activation(TMP, t[:], ACT.Square).then_inc(squared, 1)
            for n in range(2):
                act.wait_ge(norm2, n + 1)
                act.activation(nrm[:, n, :], nrm[:, n, :], ACT.Sqrt).then_inc(norm_root, 1)
            act.wait_ge(lr_in, 1)
            o.link(act.activation(LR[:], LZ, ACT.Abs))
            o.link(act.activation(LR[:], LR[:], ACT.Exp, scale=-1.0))
            act.activation(LR[:], LR[:], ACT.Ln, bias=1.0).then_inc(lr_log, 1)
            act.preload_act_table(ACT.Tanh)

            def step(c, routed):
                n0 = c * TPS
                if routed:
                    def xT(k):
                        act.wait_ge(xg_used, n0 + (k + 1))
                        act.activation(xgT[:, k, :], ps[:, 0, 0:P], ACT.Copy).then_inc(xgT_copied, 1)

                    def tanh(k):
                        act.wait_ge(gu_ps, n0 * 2 + (2 * k + 1))
                        act.activation(th[:, k, :], ps[:, 1 + 2 * (k % 2), :], ACT.Tanh, scale=0.5).then_inc(tanh_done, 1)

                    def hT(k):
                        act.wait_ge(hidT_ps, n0 + (k + 1))
                        if k == 2:
                            act.wait_ge(y_ps, n0 + 1)
                        act.activation(hidT[:, k % 2, :], ps[:, 5, :], ACT.Copy).then_inc(hidT_copied, 1)

                    def y(k):
                        act.wait_ge(y_ps, n0 + (k + 1))
                        act.wait_ge(y_stored[k], c * 16 + 16)
                        act.activation(yg[:, k, :], ps[:, 6 + k % 2, 0:D], ACT.Copy, scale=0.5).then_inc(y_copied, 1)
                else:
                    def xT(k):
                        pass
                    tanh = hT = y = xT
                def joint(r):
                    act.wait_ge(rec_j, c * 2 + r)
                    act.activation(EX, EX, ACT.Exp, scale=HD ** -0.5).then_inc(exp_j, 1)

                xT(0)
                act.wait_ge(rec_k, c + 1)
                act.activation(EK, EK, ACT.Exp).then_inc(exp_k, 1)
                tanh(0)
                xT(1)
                act.wait_ge(rec_q, c + 1)
                act.activation(EQ, EQ, ACT.Exp).then_inc(exp_q, 1)
                tanh(1)
                joint(1)
                hT(0)
                y(0)
                xT(2)
                tanh(2)
                hT(1)
                joint(2)
                y(1)
                hT(2)
                y(2)

            with act.Fori(0, ROUTED_STEPS) as c:
                step(c, True)
            with act.Fori(ROUTED_STEPS, NCH) as c:
                step(c, False)
            act.wait_ge(o_centred, 1)
            for k in range(TPS):
                act.wait_ge(y_stored[k], 16 * (ROUTED_STEPS + 1))
            act.activation(TMP, O[:], ACT.Square).then_inc(o_squared, 1)
            act.wait_ge(o_var, 1)
            act.activation(nrm[:, 0, :], nrm[:, 0, :], ACT.Sqrt).then_inc(o_root, 1)
            for g in range(G4):
                act.wait_ge(mix_ready, g + 1)
                v = V[:].rearrange("p a b -> p (a b)")[:, g * 512:(g + 1) * 512]
                act.activation(v, v, ACT.Silu).then_inc(mix_silu, 1)

            act.wait_ge(w1_loaded, 16 * N_W1)
            act.wait_ge(ln_var, 2)
            act.activation(rstd[:], rstd[:], ACT.Sqrt).then_inc(ln_std, 1)
            for g in range(G4):
                act.wait_ge(xnT_ps, G4 + g + 1)
                act.activation(xnT[:, g * 512:(g + 1) * 512], ps[:, g % 2, :], ACT.Copy).then_inc(xnT_copied, 1)
            o.link(act.activation(a_neg, a_neg, ACT.Exp))
            o.link(act.activation(a_neg, a_neg, ACT.Copy, scale=-1.0))
            act.wait_ge(logits_ready, 2)
            act.activation(lg, lg, ACT.Exp).then_inc(probs_ready, 1)

            def piece(c, p):
                act.wait_ge(moe_ps, c * PIECES + (p + 1))
                bank = ps[:, 6 + p % 2, :]
                if p < 2:
                    w = min(4, CT - 4 * p) * P
                    i = act.activation(xgT1[:, 4 * p * P:4 * p * P + w], bank[:, 0:w], ACT.Copy)
                elif p < 10:
                    f, half = divmod(p - 2, 2)
                    i = act.activation(hid1[:, f, half * (CAP // 2):(half + 1) * (CAP // 2)], bank[:, 0:CAP // 2], ACT.Relu,
                                       bias=b_e1_now[:, f:f + 1])
                else:
                    w = min(4, CT - 4 * (p - 10))
                    if p == 10:
                        act.wait_ge(y1_stored, c * 16 + 16)
                    i = act.activation(yg1[:, 4 * (p - 10):4 * (p - 10) + w, :], bank[:, 0:w * D].rearrange("p (i c) -> p i c", c=D), ACT.Copy)
                i.then_inc(moe_out, 1)

            base = o.total()
            PER_B = 3 * GD + 1
            with act.Fori(0, B) as c:
                o.loop(c, base, PER_B)
                o.mark(act.activation(b_e1_now[:], b_e1[:, bass.ds(c, 1), :].rearrange("p a b -> p (a b)"), ACT.Copy))
                for g in range(GD):
                    act.wait_ge(inp_ps, c * (2 * GD) + (g + 1))
                    act.activation(h1[:, g, :], ps[:, g, :], ACT.Identity, scale=conv_w1[:, g, 3:4], bias=conv_b1[:, g:g + 1]).then_inc(tap1_first, 1)
                for g in range(GD):
                    act.wait_ge(inp_ps, c * (2 * GD) + (GD + g + 1))
                    o.mark(act.activation(res1[:, g, :], ps[:, GD + g, :], ACT.Silu))
                for g in range(GD):
                    act.wait_ge(conv1_done, c * GD + (g + 1))
                    act.activation(h1[:, g, :], h1[:, g, :], ACT.Silu).then_inc(h1_ready, 1)
                act.wait_ge(xd_ps, c + 1)
                act.activation(xd1[0:DTR + 2 * NS, :], ps[0:DTR + 2 * NS, 4, :], ACT.Copy).then_inc(xd_copied, 1)
                for g in range(GD):
                    act.wait_ge(dl_ps, c * GD + (g + 1))
                    o.mark(act.activation(sp1[:, g, :], ps[:, g, :], ACT.Abs, bias=dt_b1[:, g:g + 1]))
                    act.activation(del1[:, g, :], ps[:, g, :], ACT.Relu, bias=dt_b1[:, g:g + 1]).then_inc(sp_ready, 1)
                o.wait()
                for g in range(GD):
                    o.mark(act.activation(sp1[:, g, :], sp1[:, g, :], ACT.Exp, scale=-1.0))
                o.wait()
                for g in range(GD):
                    act.activation(sp1[:, g, :], sp1[:, g, :], ACT.Ln, bias=1.0).then_inc(sp_log, 1)
                act.wait_ge(delta_ready, c * GD + GD)
                for n in range(NS):
                    for g in range(GD):
                        k = GD * n + g
                        if k >= 4:
                            act.wait_ge(scanned, c * (GD * NS) + (k - 3))
                        act.activation(dA[:, k % 4, :], del1[:, g, :], ACT.Exp, scale=a_neg[:, g, n:n + 1]).then_inc(dA_ready, 1)
                    if 2 <= n <= PIECES + 1:
                        piece(c, n - 2)
                act.wait_ge(s1_ps, c + 1)
                act.activation(s1[:, bass.ds(c * L, L)], ps[:, 0, :], ACT.Copy).then_inc(s1_copied, 1)
            o.end(base, PER_B, B)
            for g in range(G4):
                act.wait_ge(mix_ready, G4 + g + 1)
                v = V[:].rearrange("p a b -> p (a b)")[:, g * 512:(g + 1) * 512]
                act.activation(v, v, ACT.Silu).then_inc(mix_silu, 1)

        @block.vector
        def _(dve):
            o = Order(dve, dve_order)
            tt = dve.tensor_tensor

            def layernorm(layer):
                for i in range(NT):
                    o.mark(dve.bn_stats(stats[:, i, :], x[:, i, :]))
                o.wait()
                for i in range(NT):
                    o.mark(dve.bn_aggr(mv[:, i, :], stats[:, i, :]))
                o.wait()
                dve.tensor_scalar_add(rstd[:], mv[:, :, 1], EPS).then_inc(ln_var, 1)
                dve.wait_ge(ln_std, layer + 1)
                o.link(dve.reciprocal(rstd[:], rstd[:]))
                for i in range(NT):
                    dve.tensor_scalar(xn[:, i, :], x[:, i, :], mv[:, i, 0:1], rstd[:, i:i + 1], ALU.subtract, ALU.mult).then_inc(xn_ready, 1)

            def dispatch(layer):
                lgf = ps[:, 0, 0:NT * E].rearrange("p (i e) -> p i e", e=E)
                dve.wait_ge(logits_ps, layer + 1)
                if layer == 0:
                    o.link(dve.tensor_copy(lg, lgf))
                else:
                    o.link(tt(lg, lgf, bc(b_rt1, 1, NT), ALU.add))
                o.link(dve.tensor_reduce(lmx[:], lg, AX_X, ALU.max))
                tt(lg, lg, bc(lmx[:], 2, E), ALU.subtract).then_inc(logits_ready, 1)
                dve.wait_ge(probs_ready, layer + 1)
                o.link(dve.tensor_reduce(lmx[:], lg, AX_X, ALU.add))
                o.link(dve.reciprocal(lmx[:], lmx[:]))
                o.link(tt(lg, lg, bc(lmx[:], 2, E), ALU.mult))
                for i in range(NT):
                    o.mark(dve.max(top[:, i, :], lg[:, i, :]))
                o.wait()
                for i in range(NT):
                    o.mark(dve.max_index(topi[:, i, :], top[:, i, :], lg[:, i, :]))
                o.wait()
                o.mark(dve.tensor_copy(e12[:, 0, :], topi[:, :, 0]))
                o.mark(dve.tensor_copy(e12[:, 1, :], topi[:, :, 1]))
                o.link(tt(wsum[:], top[:, :, 0], top[:, :, 1], ALU.add))
                o.link(dve.reciprocal(wsum[:], wsum[:]))
                for j in range(2):
                    o.mark(tt(w12[:, j, :], top[:, :, j], wsum[:], ALU.mult))
                    o.mark(tt(oh[:, j], bc(iota_e[:], 1, NT), bc(e12[:, j, :], 2, E), ALU.is_equal))
                o.wait()
                tt(mask, oh[:, 0], oh[:, 1], ALU.add).then_inc(mask_ready, 1)
                dve.wait_ge(ranks_ps, 2 * layer + 2)
                o.link(dve.tensor_copy(tot, ps[:, 0, 0:NT * E].rearrange("p (i e) -> p e i", e=E)))
                o.link(dve.tensor_tensor_scan(flat(inc), flat(first_of_e[:]), flat(tot), 0.0, ALU.mult, ALU.add))
                o.link(tt(tot, inc, tot, ALU.subtract))
                o.link(tt(rank, tot.rearrange("p e i -> p i e"),
                          ps[:, 1, 0:NT * E].rearrange("p (i e) -> p i e", e=E), ALU.add))
                if layer == 0:
                    o.link(dve.tensor_scalar(tl[:, 0, :], inc[:, :, NT - 1], float(P - 1), 1.0 / P, ALU.add, ALU.mult))
                    o.link(dve.tensor_scalar_add(tl[:, 0, :], tl[:, 0, :], -0.5 + 0.5 / P))
                    o.link(dve.tensor_copy(tl_i[:], tl[:, 0, :]))
                    o.link(dve.tensor_copy(tl[:, 0, :], tl_i[:]))
                    o.link(dve.tensor_tensor_scan(tl[:, 1, :], ones[:, 0:E], tl[:, 0, :], 0.0, ALU.mult, ALU.add))
                    o.link(tt(tl[:, 2, :], tl[:, 1, :], tl[:, 0, :], ALU.subtract))
                    o.link(dve.tensor_scalar(tl[:, 2, :], tl[:, 2, :], float(P), -1.0, ALU.mult, ALU.add))
                    o.link(tt(rank, rank, bc(tl[:, 2, :], 1, NT), ALU.add))
                    o.link(tt(tcmp, bc(iota_t[:], 2, E), bc(tl[:, 1, :], 1, TILES_A), ALU.is_ge))
                    o.link(dve.tensor_reduce(texp[:], tcmp, AX_X, ALU.add))
                    o.link(dve.tensor_scalar(texp[:], texp[:], float(E - 1), float(F), ALU.min, ALU.mult))
                    o.link(dve.tensor_copy(texp_i[:], texp[:]))
                else:
                    o.link(dve.tensor_scalar(keep, rank, float(CAP), None, ALU.is_le))
                    o.link(dve.tensor_scalar(tl[:, 2, :], iota_e[:], float(CAP), -1.0, ALU.mult, ALU.add))
                    o.link(tt(rank, rank, bc(tl[:, 2, :], 1, NT), ALU.add))
                for j in range(2):
                    o.mark(tt(prod[:, j], oh[:, j], rank, ALU.mult))
                o.wait()
                o.link(dve.tensor_reduce(slot[:].rearrange("p j i -> p (j i)"), prod.rearrange("p j i e -> p (j i) e"), AX_X, ALU.add))
                if layer == 0:
                    dve.tensor_copy(sl_put[:], slot[:]).then_inc(slots_ready, 1)
                    return
                for j in range(2):
                    o.mark(tt(prod[:, j], oh[:, j], keep, ALU.mult))
                o.wait()
                o.link(dve.tensor_reduce(kept[:].rearrange("p j i -> p (j i)"), prod.rearrange("p j i e -> p (j i) e"), AX_X, ALU.add))
                o.mark(tt(w12[:], w12[:], kept[:], ALU.mult))
                o.link(tt(slot[:], slot[:], kept[:], ALU.mult))
                o.mark(dve.tensor_copy(sl_get[:], slot[:]))
                o.link(dve.tensor_scalar(kept[:], kept[:], -float(SKIP), float(SKIP), ALU.mult, ALU.add))
                o.link(tt(slot[:], slot[:], kept[:], ALU.add))
                dve.tensor_copy(sl_put[:], slot[:]).then_inc(slots_ready, 1)

            dve.wait_ge(x_loaded, 64)
            layernorm(0)
            dve.wait_ge(w_loaded, 16 * 7)
            dve.tensor_scalar_add(taps[:, :, 3], taps[:, :, 3], 1.0).then_inc(taps_ready, 1)
            for cu in range(NCU):
                w, s = cu % 3, cu % 4
                dve.wait_ge(tap_first, cu + 1)
                for sh in (1, 2, 3):
                    i = dve.scalar_tensor_tensor(cv[:, s, sh:L], ps[:, 2 + s, 0:L - sh], taps[:, w, 3 - sh:4 - sh],
                                                 cv[:, s, sh:L], ALU.mult, ALU.add)
                    if sh < 3:
                        o.link(i)
                    else:
                        i.then_inc(conv_done, 1)
            dve.wait_ge(consts_ready, 6)
            dispatch(0)
            dve.wait_ge(heads_loaded, 16 * 4 * B)
            for n in range(2):
                dve.wait_ge(squared, n + 1)
                dve.tensor_reduce(nrm[:, n, :], TMP.rearrange("p e t -> p t e"), AX_X, ALU.add).then_inc(norm2, 1)
            dve.tensor_scalar_add(LZ, LZ, 1e-3).then_inc(lr_in, 1)
            for n, t in enumerate((K, Q)):
                dve.wait_ge(norm_root, n + 1)
                o.link(dve.reciprocal(nrm[:, n, :], nrm[:, n, :]))
                o.mark(tt(t[:], t[:], bc(nrm[:, n, :], 1, HD), ALU.mult))
            dve.wait_ge(lr_log, 1)
            o.link(dve.scalar_tensor_tensor(LR[:], LZ, 0.0, LR[:], ALU.max, ALU.add))
            o.wait()

            dve.wait_ge(zeroed, ZEROED)
            def rows(a):
                return bc(a.rearrange("p d l -> p l d"), 1, DI)

            def fast(a):
                return bc(a.rearrange("p (D d) -> p D d", D=DI), 2, CH)

            w_in, w_out = X[:, 0:DI * HD], X[:, DI * HD:2 * DI * HD]

            def step(c, routed):
                ts = bass.ds(c * CH, CH)
                kc, vc, qc = K[:, :, ts], V[:, :, ts], Q[:, :, ts]
                n0 = c * TPS

                def gate_up(k):
                    if not routed:
                        return
                    dve.wait_ge(tanh_done, n0 + (k + 1))
                    o.link(dve.scalar_tensor_tensor(th[:, k, :], th[:, k, :], 1.0, ps[:, 1 + 2 * (k % 2), :], ALU.add, ALU.mult))
                    dve.wait_ge(gu_ps, n0 * 2 + (2 * k + 2))
                    tt(hid[:, k, :], th[:, k, :], ps[:, 2 + 2 * (k % 2), :], ALU.mult).then_inc(hid_ready, 1)

                o.link(tt(PK, rows(kc), fast(w_in), ALU.mult))
                o.mark(dve.tensor_reduce(SS[:, 1], PK, AX_X, ALU.add))
                o.mark(tt(PQ, rows(qc), fast(w_in), ALU.mult))
                o.wait()
                o.mark(dve.tensor_reduce(MK[:], SS[:, 1].rearrange("p D l -> p l D"), AX_X, ALU.max))
                o.link(dve.tensor_reduce(SQ, PQ, AX_X, ALU.add))
                tt(EK, SS[:, 1], bc(MK[:], 1, DI), ALU.subtract).then_inc(rec_k, 1)
                o.link(dve.tensor_reduce(MQ[:], SQ.rearrange("p D l -> p l D"), AX_X, ALU.max))
                tt(EQ, SQ, bc(MQ[:], 1, DI), ALU.subtract).then_inc(rec_q, 1)
                dve.wait_ge(exp_k, c + 1)
                o.link(dve.tensor_reduce(ZK[:], EK.rearrange("p D l -> p l D"), AX_X, ALU.add))
                o.mark(dve.tensor_copy(SC[:, :, 0], w_out))
                o.link(dve.reciprocal(ZK[:], ZK[:]))
                o.link(tt(ZK[:], ZK[:], LR[:, 1, ts], ALU.mult))
                o.link(tt(EK, EK, bc(ZK[:], 1, DI), ALU.mult))
                o.link(tt(SC.rearrange("p (D d) l -> p D d l", D=DI)[:, :, :, 1:CH + 1], bc(EK, 2, HD), bc(vc, 1, DI), ALU.mult))
                o.link(dve.tensor_tensor_scan(flat(CS), flat(seg[:]), flat(SC), 0.0, ALU.mult, ALU.add))
                o.mark(dve.tensor_copy(w_out, CS[:, :, CH]))
                o.link(tt(PK, rows(vc), fast(CS[:, :, CH]), ALU.mult))
                o.link(dve.tensor_reduce(SS[:, 0], PK, AX_X, ALU.add))

                def scores_max():
                    ss = SS.rearrange("p j D l -> p (j D) l")
                    o.link(dve.tensor_reduce(M8[:], ss, AX_X, ALU.max))
                    tt(EX.rearrange("p j D l -> p (j D) l"), ss, bc(M8[:], 2, CH), ALU.subtract).then_inc(rec_j, 1)

                def update(r):
                    dve.wait_ge(exp_j, c * 2 + r)
                    o.mark(dve.tensor_reduce(Z8[:], EX.rearrange("p j D l -> p (j D) l"), AX_X, ALU.add))
                    o.mark(tt(GP[:, 0].rearrange("p (D d) l -> p D d l", D=DI), bc(EX[:, 0], 2, HD), bc(kc, 1, DI), ALU.mult))
                    o.mark(tt(GP[:, 1].rearrange("p (D d) l -> p D d l", D=DI), bc(EX[:, 1], 2, HD), bc(vc, 1, DI), ALU.mult))
                    o.wait()
                    o.mark(dve.reciprocal(Z8[:], Z8[:]))
                    o.link(dve.tensor_reduce(GR[:], GP.rearrange("p j a l -> p (j a) l"), AX_X, ALU.add))
                    z = Z8[:].rearrange("p (j D) -> p j D", j=2)
                    lr2 = LR[:, :, bass.ds(c * CH, 1)].broadcast_to([P, 2, DI])
                    o.link(tt(z, z, lr2, ALU.mult))
                    gr = GR[:].rearrange("p (a d) -> p a d", d=HD)
                    o.link(tt(gr, gr, bc(Z8[:], 2, HD), ALU.mult))
                    o.link(tt(X[:], X[:], GR[:], ALU.add))

                scores_max()
                dve.wait_ge(exp_q, c + 1)
                o.link(dve.tensor_reduce(ZQ[:], EQ.rearrange("p D l -> p l D"), AX_X, ALU.add))
                gate_up(0)
                o.link(dve.reciprocal(ZQ[:], ZQ[:]))
                o.mark(tt(EQ, EQ, bc(ZQ[:], 1, DI), ALU.mult))
                update(1)
                gate_up(1)
                o.mark(tt(PP[:, 0].rearrange("p (D l) d -> p D l d", D=DI), rows(vc), fast(w_out), ALU.mult))
                o.link(tt(PP[:, 1].rearrange("p (D l) d -> p D l d", D=DI), rows(kc), fast(w_in), ALU.mult))
                o.link(dve.tensor_reduce(SS.rearrange("p j D l -> p (j D l)"), PP.rearrange("p j a d -> p (j a) d"), AX_X, ALU.add))
                scores_max()
                o.link(tt(OP, bc(EQ.rearrange("p D l -> p l D"), 1, HD),
                          CS.rearrange("p (D d) l -> p d l D", D=DI)[:, :, 1:CH + 1, :], ALU.mult))
                o.mark(dve.tensor_reduce(O[:, :, ts], OP, AX_X, ALU.add))
                update(2)
                gate_up(2)

            first = o.total()
            PER_R, PER_P = 45, 42
            with dve.Fori(0, ROUTED_STEPS) as c:
                o.loop(c, first, PER_R)
                step(c, True)
            o.end(first, PER_R, ROUTED_STEPS)
            first2 = o.total()
            with dve.Fori(ROUTED_STEPS, NCH) as c:
                o.loop(c, first2 - ROUTED_STEPS * PER_P, PER_P)
                step(c, False)
            o.end(first2, PER_P, NCH - ROUTED_STEPS)
            o.wait()
            dT = lambda a: a.rearrange("p e t -> p t e")
            o.link(dve.tensor_reduce(nrm[:, 0, :], dT(O[:]), AX_X, ALU.add))
            o.link(dve.tensor_scalar(nrm[:, 0, :], nrm[:, 0, :], 1.0 / HD, None, ALU.mult))
            tt(O[:], O[:], bc(nrm[:, 0, :], 1, HD), ALU.subtract).then_inc(o_centred, 1)
            dve.wait_ge(o_squared, 1)
            o.link(dve.tensor_reduce(nrm[:, 0, :], dT(TMP), AX_X, ALU.add))
            dve.tensor_scalar(nrm[:, 0, :], nrm[:, 0, :], 1.0 / HD, EPS, ALU.mult, ALU.add).then_inc(o_var, 1)
            dve.wait_ge(o_root, 1)
            o.link(dve.reciprocal(nrm[:, 0, :], nrm[:, 0, :]))
            tt(O[:], O[:], bc(nrm[:, 0, :], 1, HD), ALU.mult).then_inc(o_ready, 1)
            oT = K[:].rearrange("p a b -> p (a b)")
            dve.wait_ge(oT_loaded, 16)
            o.link(dve.tensor_scalar(oT, oT, ln_gb[:, 0:1], ln_gb[:, 1:2], ALU.mult, ALU.add))
            tt(oT, oT, gateT[:], ALU.mult).then_inc(oT_ready, 1)

            def combine(g):
                r = lambda a: a[:].rearrange("p a b -> p (a b)")[:, g * 512:(g + 1) * 512].rearrange("p (i c) -> p i c", c=D)
                a, b2 = r(V), r(Q)
                o.mark(tt(a, a, bc(w12[:, 0, 4 * g:4 * g + 4], 2, D), ALU.mult))
                o.link(tt(b2, b2, bc(w12[:, 1, 4 * g:4 * g + 4], 2, D), ALU.mult))
                tt(a, a, b2, ALU.add).then_inc(mix_ready, 1)

            dve.wait_ge(y_gathered, 16 * 2 * NT)
            dve.wait_ge(x_loaded, 128)
            for g in range(G4):
                combine(g)
            for g in range(G4):
                v = V[:].rearrange("p a b -> p (a b)")[:, g * 512:(g + 1) * 512]
                xs = x[:, 4 * g:4 * g + 4, :].rearrange("p i c -> p (i c)")
                dve.wait_ge(s_ps, g + 1)
                dve.wait_ge(mix_silu, g + 1)
                i = tt(v, v, ps[:, 1 + g % 2, :], ALU.mult)
                i.then_inc(s_used, 1)
                dve.wait_ge(s_used, g + 1)
                tt(xs, xs, v, ALU.add).then_inc(x1_ready, 1)

            dve.wait_ge(x1_ready, G4)
            dve.wait_ge(w1_loaded, 16 * N_W1)
            layernorm(1)
            dispatch(1)
            base = o.total()
            PER_B = 4 * GD + NS
            with dve.Fori(0, B) as c:
                o.loop(c, base, PER_B)
                for g in range(GD):
                    dve.wait_ge(tap1_first, c * GD + (g + 1))
                    for sh in (1, 2, 3):
                        i = dve.scalar_tensor_tensor(h1[:, g, sh:L], ps[:, g, 0:L - sh], conv_w1[:, g, 3 - sh:4 - sh],
                                                     h1[:, g, sh:L], ALU.mult, ALU.add)
                        if sh < 3:
                            o.link(i)
                        else:
                            i.then_inc(conv1_done, 1)
                for g in range(GD):
                    dve.wait_ge(sp_log, c * GD + (g + 1))
                    tt(del1[:, g, :], del1[:, g, :], sp1[:, g, :], ALU.add).then_inc(delta_ready, 1)
                for g in range(GD):
                    dve.wait_ge(delta_ready, c * GD + (g + 1))
                    o.mark(tt(dh1[:, g, :], del1[:, g, :], h1[:, g, :], ALU.mult))

                def inject(n, g):
                    if g == 0:
                        dve.wait_ge(b_ps, c * NS + (n + 1))
                    i = tt(dBu[:, g, :], dh1[:, g, :], ps[:, 2 + n % 2, :], ALU.mult)
                    if g == 0:
                        o.mark(i)
                    else:
                        i.then_inc(b_used, 1)

                def scan(n, g):
                    k = GD * n + g
                    dve.wait_ge(dA_ready, c * (GD * NS) + (k + 1))
                    dve.tensor_tensor_scan(st1[:, g, :], dA[:, k % 4, :], dBu[:, g, :], 0.0, ALU.mult, ALU.add).then_inc(scanned, 1)

                def weigh(n, g):
                    k = GD * n + g
                    dve.wait_ge(scanned, c * (GD * NS) + (k + 1))
                    if g == 0:
                        dve.wait_ge(c_ps, c * NS + (n + 1))
                    if k >= 4:
                        dve.wait_ge(yc_used, c * (GD * NS) + (k - 3))
                    tt(yc1[:, k % 4, :], st1[:, g, :], ps[:, n % 2, :], ALU.mult).then_inc(yc_ready, 1)

                o.wait()
                for n in range(NS):
                    inject(n, 0)
                    inject(n, 1)
                    o.wait()
                    scan(n, 0)
                    dve.wait_ge(b_used, c * NS + (n + 1))
                    scan(n, 1)
                    weigh(n, 0)
                    weigh(n, 1)
                dve.wait_ge(yc_used, (c + 1) * (GD * NS))
                for g in range(GD):
                    o.link(dve.scalar_tensor_tensor(h1[:, g, :], h1[:, g, :], d_1[:, g:g + 1], ps[:, 4 + g, :], ALU.mult, ALU.add))
                    tt(h1[:, g, :], h1[:, g, :], res1[:, g, :], ALU.mult).then_inc(yt_ready, 1)
            o.end(base, PER_B, B)
            dve.wait_ge(y1_gathered, 16 * 2 * NT)
            dve.wait_ge(s1_copied, B + 1)
            for g in range(G4):
                combine(g)
            for g in range(G4):
                v = V[:].rearrange("p a b -> p (a b)")[:, g * 512:(g + 1) * 512]
                xs = x[:, 4 * g:4 * g + 4, :].rearrange("p i c -> p (i c)")
                dve.wait_ge(mix_silu, G4 + g + 1)
                o.link(tt(v, v, s1[:, g * 512:(g + 1) * 512], ALU.mult))
                tt(xs, xs, v, ALU.add).then_inc(out_ready, 1)


def host(inputs):
    import numpy as np
    c = np.ascontiguousarray
    a = {k: np.asarray(v) for k, v in inputs.items()}
    r = {}
    r["x"] = c(a["L0_attn_hidden_states"].reshape(T, D))
    r["wproj"] = c(np.concatenate([a[f"L0_attn_W{n}"].T for n in "qkvg"], axis=1))
    r["wlr"] = c(a["L0_attn_Wlr"].T)
    r["wo"] = c(a["L0_attn_Wo"].T)
    r["taps"] = c(np.concatenate([a["L0_attn_cq"], a["L0_attn_ck"], a["L0_attn_cv"]], axis=1))
    r["ln_gb"] = c(np.stack([np.tile(a["L0_attn_ln_g"], H), np.tile(a["L0_attn_ln_b"], H)], axis=1))
    st = np.concatenate([a[n][0].transpose(1, 0, 2).reshape(H, DI * HD) for n in ("L0_attn_W_in_init", "L0_attn_W_out_init")], axis=1)
    r["state0"] = c(np.tile(st, (B, 1)))
    r["wrt"] = c(a["L0_ffn_W_router"].T)
    r["wg_a"] = c(a["L0_ffn_W_gate"].transpose(2, 0, 1).reshape(D, E * F))
    r["wu_a"] = c(a["L0_ffn_W_up"].transpose(2, 0, 1).reshape(D, E * F))
    r["wd_a"] = c(a["L0_ffn_W_down"].reshape(E, D, FC, P).transpose(3, 0, 2, 1).reshape(P, E * FC * D))
    r["w_in1"] = c(a["L1_attn_in_proj_w"])
    rows = lambda m: c(m.reshape(GD, P, -1).transpose(1, 0, 2).reshape(P, -1))
    for n, k in (("w_x1", "x_proj_w"), ("w_o1", "out_proj_w"), ("conv_w1", "conv_w"), ("conv_b1", "conv_b"),
                 ("dt_b1", "dt_proj_b"), ("d_1", "D_param"), ("a_log", "A_log")):
        r[n] = rows(a["L1_attn_" + k])
    r["w_dt1"] = c(a["L1_attn_dt_proj_w"])
    r["w_rt1"] = c(a["L1_ffn_gate_w"])
    r["b_rt1"] = c(a["L1_ffn_gate_b"].reshape(1, E))
    r["b_e1"] = c(a["L1_ffn_b1"].reshape(E, FC, P).transpose(2, 0, 1).reshape(P, E * FC))
    r["b_e2"] = c(a["L1_ffn_b2"].reshape(1, E * D))
    r["w_e1"] = c(a["L1_ffn_w1"].reshape(E * D, F))
    r["w_e2"] = c(a["L1_ffn_w2"].reshape(E, FC, P, D).transpose(2, 0, 1, 3).reshape(P, E * FC * D))
    return r


def kernel(**inputs):
    import numpy as _np
    import concourse.bacc as _bacc
    from concourse.bass_utils import run_bass_kernel_spmd as _run

    nc = _bacc.Bacc("TRN2", target_bir_lowering=False, num_devices=1)
    arrays, d = {}, {}
    for name, a in host(inputs).items():
        arrays[f"in_{name}"] = a
        d[name] = nc.dram_tensor(f"in_{name}", a.shape, mybir.dt.from_np(a.dtype), kind="ExternalInput").ap()
    d["out"] = nc.dram_tensor("out_0_dram", (T, D), F32, kind="ExternalOutput").ap()
    build(nc, d)
    got = _run(nc, [arrays], core_ids=[0]).results[0]["out_0_dram"]
    return _np.asarray(got).reshape(B, L, D)
```

```python
from contextlib import ExitStack

import concourse.bass as bass
from concourse import mybir

F32 = mybir.dt.float32
BF16 = mybir.dt.bfloat16
I32 = mybir.dt.int32
U32 = mybir.dt.uint32
ALU = mybir.AluOpType
ACT = mybir.ActivationFunctionType
AX_X = mybir.AxisListType.X

P = 128
B, L, D = 8, 512, 128
T = B * L
NT = T // P
G4 = NT // 4
H, HD, DI, CH = 16, 8, 4, 16
NCH = L // CH
E = 8
F = 512
FC = F // P
CONV = 4
TILES_A = 2 * T // P + E
CAP = int(1.25 * T / E)
CT = CAP // P
DIN, NS, DTR = 256, 16, 64
GD = DIN // P
TPS = 3
ROUTED_STEPS = TILES_A // TPS
EPS = 1e-5
SKIP = 1 << 20


def bc(ap, axis, n):
    a = ap.unsqueeze(axis)
    shape = list(a.shape)
    shape[axis] = n
    return a.broadcast_to(shape)


def flat(a):
    return a if len(a.shape) == 2 else a.rearrange("p a b -> p (a b)") if len(a.shape) == 3 else a.rearrange("p a b c -> p (a b c)")


class Region:

    def __init__(self, tile):
        self.cols, self.at = flat(tile), 0

    def take(self, *shape):
        n = 1
        for s in shape:
            n *= s
        a = self.cols[:, self.at:self.at + n]
        self.at += n
        assert self.at <= self.cols.shape[1]
        if len(shape) == 2:
            a = a.rearrange("p (a b) -> p a b", a=shape[0])
        if len(shape) == 3:
            a = a.rearrange("p (a b c) -> p a b c", a=shape[0], b=shape[1])
        return a


class Order:

    def __init__(self, eng, sem):
        self.eng, self.sem, self.base, self.n = eng, sem, 0, 0

    def mark(self, ins):
        self.n += 1
        ins.then_inc(self.sem, 1)
        return self.n

    def wait(self, n=None):
        n = self.n if n is None else n
        v = self.base + n
        self.eng.wait_ge(self.sem, v)

    def link(self, ins):
        self.mark(ins)
        self.wait()

    def loop(self, c, first, per):
        self.base, self.n = c * per + first, 0

    def end(self, first, per, trips):
        assert self.n == per, (self.n, per)
        self.base, self.n = first + per * trips, 0

    def total(self):
        return self.base + self.n


def build(nc, d, stop=None):
    with ExitStack() as ctx:
        def sb(name, shape, dt=F32):
            return ctx.enter_context(nc.sbuf_tensor(name, shape, dt))

        def sem(name):
            return ctx.enter_context(nc.semaphore(name))

        def dram(name, shape):
            return nc.dram_tensor(name, shape, F32).ap()

        qkv_scr = dram("qkv_scr", [3, P, T])
        lr_scr = dram("lr_scr", [2 * H, T])
        o_scr = dram("o_scr", [P, T])
        slots_x = dram("slots_x", [TILES_A * P, D])
        slots_y = dram("slots_y", [TILES_A * P, D])
        slots_x1 = dram("slots_x1", [E * CAP, D])
        slots_y1 = dram("slots_y1", [E * CAP, D])

        ps = ctx.enter_context(nc.psum_tensor("ps", [P, 8, 512], F32))
        ident = sb("ident", [P, P])
        upper = sb("upper", [P, P])
        ones = sb("ones", [P, P])
        iota_e = sb("iota_e", [P, E])
        iota_t = sb("iota_t", [P, TILES_A])
        first_of_e = sb("first_of_e", [P, E, NT])
        x = sb("x", [P, NT, D])
        xn = sb("xn", [P, NT, D])
        xnT = sb("xnT", [P, T])
        stats = sb("stats", [P, NT, 6])
        mv = sb("mv", [P, NT, 2])
        rstd = sb("rstd", [P, NT])
        wproj = sb("wproj", [P, 4 * P])
        wlr = sb("wlr", [P, 2 * H])
        wo = sb("wo", [P, D])
        taps = sb("taps", [P, 3, CONV])
        ln_gb = sb("ln_gb", [P, 2])
        wrt = sb("wrt", [P, E])
        wg_a = sb("wg_a", [P, E * F])
        wu_a = sb("wu_a", [P, E * F])
        wd_a = sb("wd_a", [P, E * FC * D])
        cv = sb("cv", [P, 4, L])
        gateT = sb("gateT", [P, T])
        K = sb("K", [P, HD, L])
        V = sb("V", [P, HD, L])
        Q = sb("Q", [P, HD, L])
        O = sb("O", [P, HD, L])
        nrm = sb("nrm", [P, 2, L])
        LR = sb("LR", [P, 2, L])
        lmx = sb("lmx", [P, NT])
        top = sb("top", [P, NT, 8])
        topi = sb("topi", [P, NT, 8], U32)
        e12 = sb("e12", [P, 2, NT])
        w12 = sb("w12", [P, 2, NT])
        wsum = sb("wsum", [P, NT])
        slot = sb("slot", [P, 2, NT])
        kept = sb("kept", [P, 2, NT])
        sl_put = sb("sl_put", [P, 2, NT], I32)
        sl_get = sb("sl_get", [P, 2, NT], I32)
        tl = sb("tl", [P, 3, E])
        tl_i = sb("tl_i", [P, E], I32)
        texp = sb("texp", [P, TILES_A])
        texp_i = sb("texp_i", [P, TILES_A], I32)
        r = Region(O[:])
        lg, mask, rank, keep = (r.take(NT, E) for _ in range(4))
        oh, prod = (r.take(2, NT, E) for _ in range(2))
        tot, inc = (r.take(E, NT) for _ in range(2))
        tcmp = r.take(TILES_A, E)
        zero = r.take(4 * D)
        TMP = xnT[:].rearrange("p (e t) -> p e t", e=HD)
        r = Region(xnT[:])
        xg, xgT, yg = r.take(TPS, D), r.take(TPS, P), r.take(TPS, D)
        r = Region(xn[:])
        th, hid, hidT = r.take(TPS, F), r.take(TPS, F), r.take(2, F)
        r = Region(cv[:])
        GA, GB, GC, GV = (r.take(DI, HD, CH) for _ in range(4))
        r = Region(x[:])
        LZ = r.take(2, L)
        PK, PQ, PV = (r.take(DI, CH, HD) for _ in range(3))
        SC, CS = r.take(DI * HD, CH + 1), r.take(DI * HD, CH + 1)
        EK, EQ = r.take(DI, CH), r.take(DI, CH)
        r = Region(LZ)
        OP = r.take(HD, CH, DI)
        SI, SA, SV, SD, EA, EB, EC, ED = (r.take(DI, CH) for _ in range(8))
        X = sb("X", [P, 2 * DI * HD])
        w_in, w_out = X[:, 0:DI * HD], X[:, DI * HD:2 * DI * HD]
        w_in1, w_out1 = sb("w_in_1", [P, DI * HD]), sb("w_out_1", [P, DI * HD])
        MK, MQ, ZK, ZQ = (sb(n, [P, CH]) for n in ("MK", "MQ", "ZK", "ZQ"))
        MX = sb("MX", [P, 4, DI])
        ZS = sb("ZS", [P, 4, DI])
        GR = sb("GR", [P, 4, DI * HD])
        seg = sb("seg", [P, DI * HD, CH + 1])

        r = Region(wg_a[:])
        w_bc1 = r.take(GD, 3 * 2 * NS)
        w_inp, w_x1, w_dt1, w_o1 = r.take(2 * DIN), r.take(GD, DTR), r.take(DIN), r.take(GD, D)
        conv_w1, conv_b1, dt_b1, d_1 = r.take(GD, CONV), r.take(GD), r.take(GD), r.take(GD)
        a_neg, w_rt1, b_rt1, b_e1, b_e2 = r.take(GD, NS), r.take(E), r.take(E), r.take(E, FC), r.take(E * D)
        r = Region(wu_a[:])
        w_e1, w_e2, hid1 = r.take(F), r.take(FC, D), r.take(FC, CAP)
        r = Region(wd_a[:])
        xg1, xgT1, yg1 = r.take(CT, D), r.take(CAP), r.take(CT, D)
        pick_wide = gateT[0:3 * 2 * NS, :].rearrange("p (r c) -> p r c", c=P)
        pick = flat(cv[:]).bitcast(BF16).rearrange("p (r c) -> p r c", c=P)[0:3 * 2 * NS]
        even_odd = [Region(K[:]), Region(gateT[:])]
        h1, res1, del1, dh1 = ([r.take(GD, L) for r in even_odd] for _ in range(4))
        r = Region(V[:])
        xd1, dA, sp1, bc_rest = r.take(L), r.take(4, L), r.take(GD, L), r.take(L)
        r = Region(Q[:])
        dBu, st_g1, yc_g0, yc_g1 = (r.take(2, L) for _ in range(4))
        r = Region(nrm[:])
        bc_parts = [r.take(L // 2).bitcast(BF16)[0:3 * 2 * NS] for _ in range(2)]
        st_g0 = r.take(L)
        c_row = LR[:]
        b_e1_now = sb("b_e1_now", [P, FC])
        s1 = O[:].rearrange("p e t -> p (e t)")

        x_loaded = sem("x_loaded")
        w_loaded = sem("w_loaded")
        we_loaded = sem("we_loaded")
        consts_ready = sem("consts_ready")
        pool_order = sem("pool_order")
        zeroed = sem("zeroed")
        dve_order = sem("dve_order")
        act_order = sem("act_order")
        ln_var = sem("ln_var")
        ln_std = sem("ln_std")
        xn_ready = sem("xn_ready")
        xnT_ps = sem("xnT_ps")
        xnT_copied = sem("xnT_copied")
        proj_ps = sem("proj_ps")
        gate_ps = sem("gate_ps")
        lr_ps = sem("lr_ps")
        tap_first = sem("tap_first")
        taps_ready = sem("taps_ready")
        conv_done = sem("conv_done")
        silu_done = sem("silu_done")
        gate_copied = sem("gate_copied")
        lr_copied = sem("lr_copied")
        stored = [sem(f"stored{i}") for i in range(4)]
        lr_stored = sem("lr_stored")
        heads_loaded = sem("heads_loaded")
        squared = sem("squared")
        norm2 = sem("norm2")
        norm_root = sem("norm_root")
        lr_in = sem("lr_in")
        lr_log = sem("lr_log")
        logits_ps = sem("logits_ps")
        logits_ready = sem("logits_ready")
        probs_ready = sem("probs_ready")
        mask_ready = sem("mask_ready")
        ranks_ps = sem("ranks_ps")
        slots_ready = sem("slots_ready")
        scattered = sem("scattered")
        exp_k = sem("exp_k")
        exp_q = sem("exp_q")
        exp_a, exp_b, exp_c, exp_d = (sem(f"exp_{n}") for n in "abcd")
        rec_k = sem("rec_k")
        rec_q = sem("rec_q")
        rec_a, rec_b, rec_c, rec_d = (sem(f"rec_{n}") for n in "abcd")
        pq_ready = sem("pq_ready")
        q_ps = sem("q_ps")
        qh_ready = sem("qh_ready")
        op_ready = sem("op_ready")
        o_ps = sem("o_ps")
        o_copied = sem("o_copied")
        state_ready = sem("state_ready")
        xg_loaded = [sem(f"xg_loaded{k}") for k in range(TPS)]
        xg_used = sem("xg_used")
        xgT_copied = sem("xgT_copied")
        gu_ps = sem("gu_ps")
        tanh_done = sem("tanh_done")
        hid_ready = sem("hid_ready")
        hidT_ps = sem("hidT_ps")
        hidT_copied = sem("hidT_copied")
        y_ps = sem("y_ps")
        y_copied = sem("y_copied")
        y_stored = [sem(f"y_stored{k}") for k in range(TPS)]
        o_centred = sem("o_centred")
        o_squared = sem("o_squared")
        o_var = sem("o_var")
        o_root = sem("o_root")
        o_ready = sem("o_ready")
        o_stored = sem("o_stored")
        oT_loaded = sem("oT_loaded")
        oT_ready = sem("oT_ready")
        s_ps = sem("s_ps")
        s_used = sem("s_used")
        y_gathered = sem("y_gathered")
        mix_ready = sem("mix_ready")
        mix_silu = sem("mix_silu")
        x1_ready = sem("x1_ready")
        out_stored = sem("out_stored")

        w1_loaded = sem("w1_loaded")
        pick_order = sem("pick_order")
        pick_ready = sem("pick_ready")
        scattered1 = sem("scattered1")
        a_ready = sem("a_ready")
        inp_ps = sem("inp_ps")
        tap1_first = sem("tap1_first")
        conv1_done = sem("conv1_done")
        h1_ready = sem("h1_ready")
        xd_ps = sem("xd_ps")
        xd_copied = sem("xd_copied")
        dl_ps = sem("dl_ps")
        sp_ready = sem("sp_ready")
        delta_ready = sem("delta_ready")
        b_ps = sem("b_ps")
        c_ps = sem("c_ps")
        b_used = sem("b_used")
        dA_ready = sem("dA_ready")
        scanned = sem("scanned")
        yc_ready = sem("yc_ready")
        yc_used = sem("yc_used")
        yt_ready = sem("yt_ready")
        s1_ps = sem("s1_ps")
        s1_copied = sem("s1_copied")
        e1_loaded = sem("e1_loaded")
        xg1_loaded = sem("xg1_loaded")
        moe_ps = sem("moe_ps")
        moe_out = sem("moe_out")
        y1_stored = sem("y1_stored")
        y1_gathered = sem("y1_gathered")
        out_ready = sem("out_ready")

        sp_log = sem("sp_log")
        pick_wide_ready = sem("pick_wide_ready")
        res_ready = sem("res_ready")
        bc_in_ps = sem("bc_in_ps")
        bc_hi = sem("bc_hi")
        bc_rest1 = sem("bc_rest1")
        bc_mid = sem("bc_mid")
        bc_rest2 = sem("bc_rest2")
        bc_lo = sem("bc_lo")
        dh_ready = sem("dh_ready")
        c_copied = sem("c_copied")
        yc_g1_ready = sem("yc_g1_ready")
        N_W1 = 14
        PIECES_AT = {2: (0,), 4: (1,), 6: (2,), 8: (3, 4), **{n: (n - 4,) for n in range(9, 16)}}
        PIECES = 12
        NCU = 3 * B
        ZEROED = 16 * (TILES_A // 4 + E * CAP // (4 * P))

        def since(eng, s, v):
            if not (isinstance(v, int) and v <= 0):
                eng.wait_ge(s, v)

        def all_rows(eng, row, start=None, end=None):
            row(0, 0, 1)
            if start:
                start()
            with eng.Fori(0, (B - 2) // 2) as i:
                if start:
                    start(i)
                row(i * 2 + 1, 1, i * 2 + 2)
                row(i * 2 + 2, 0, i * 2 + 3)
            if end:
                end()
            row(B - 1, 1, None)

        block = ctx.enter_context(nc.Block())

        @block.sync
        def _(sp):
            for g in range(4):
                sp.dma_start(x[:, 8 * g:8 * g + 8, :],
                             d["x"].rearrange("(i p) c -> p i c", p=P)[:, 8 * g:8 * g + 8, :]).then_inc(x_loaded, 16)
            for dst, src in ((wproj[:], "wproj"), (wlr[:], "wlr"), (wo[:], "wo"),
                             (taps[:].rearrange("p a b -> p (a b)"), "taps"), (ln_gb[:], "ln_gb"), (wrt[:], "wrt"),
                             (X[:], "state0")):
                sp.dma_start(dst, d[src]).then_inc(w_loaded, 16)
            for dst, src in ((wg_a, "wg_a"), (wu_a, "wu_a"), (wd_a, "wd_a")):
                sp.dma_start(dst[:], d[src]).then_inc(we_loaded, 16)
            for cu in range(NCU):
                b, w = divmod(cu, 3)
                sp.wait_ge(silu_done, cu + 1)
                sp.dma_start(qkv_scr[w, :, b * L:(b + 1) * L], cv[:, cu % 4, :]).then_inc(stored[cu % 4], 16)
            sp.wait_ge(lr_copied, B)
            sp.dma_start(lr_scr, K[0:2 * H, :, :].rearrange("p a b -> p (a b)")).then_inc(lr_stored, 16)
            for s in stored:
                sp.wait_ge(s, 16 * (NCU // 4))
            sp.wait_ge(lr_stored, 16)
            for w, dst in ((1, K), (2, V), (0, Q)):
                for b in range(B):
                    sp.dma_start(dst[b * H:(b + 1) * H, :, :],
                                 qkv_scr[w].rearrange("(h e) (b t) -> b h e t", h=H, b=B)[b]).then_inc(heads_loaded, 16)
            for b in range(B):
                sp.dma_start(LZ[b * H:(b + 1) * H, :, :],
                             lr_scr.rearrange("(h j) (b t) -> b h j t", h=H, b=B)[b]).then_inc(heads_loaded, 16)
            sp.wait_ge(scattered, 16 * 2 * NT)
            sp.wait_ge(norm2, 2)
            for k in range(TPS):
                sp.dma_start(xg[:, k, :], slots_x[k * P:(k + 1) * P, :]).then_inc(xg_loaded[k], 16)
            with sp.Fori(0, ROUTED_STEPS - 1) as c:
                for k in range(TPS):
                    sp.wait_ge(xg_used, c * TPS + (k + 1))
                    sp.dma_start(xg[:, k, :], slots_x[bass.ds((c + 1) * (TPS * P) + k * P, P), :]).then_inc(xg_loaded[k], 16)
                for k in range(TPS):
                    sp.wait_ge(y_copied, c * TPS + (k + 2))
                    sp.dma_start(slots_y[bass.ds(c * (TPS * P) + k * P, P), :], yg[:, k, :]).then_inc(y_stored[k], 16)
            for k in range(TPS):
                j = (ROUTED_STEPS - 1) * TPS + k
                sp.wait_ge(y_copied, j + 2)
                sp.dma_start(slots_y[j * P:(j + 1) * P, :], yg[:, k, :]).then_inc(y_stored[k], 16)
            sp.wait_ge(o_centred, 1)
            for g in range(4):
                sp.dma_start(x[:, 8 * g:8 * g + 8, :],
                             d["x"].rearrange("(i p) c -> p i c", p=P)[:, 8 * g:8 * g + 8, :]).then_inc(x_loaded, 16)
            sp.wait_ge(o_ready, 1)
            for b in range(B):
                sp.dma_start(o_scr.rearrange("(h e) (b t) -> b h e t", h=H, b=B)[b],
                             O[b * H:(b + 1) * H, :, :]).then_inc(o_stored, 16)
            sp.wait_ge(o_stored, 16 * B)
            sp.dma_start(K[:].rearrange("p a b -> p (a b)"), o_scr).then_inc(oT_loaded, 16)
            sp.wait_ge(y_copied, TILES_A + 1)
            for dst, src in ((w_inp, "w_in1"), (flat(w_x1), "w_x1"), (flat(w_bc1), "w_bc1"), (w_dt1[0:DTR, :], "w_dt1"), (flat(w_o1), "w_o1"),
                             (flat(conv_w1), "conv_w1"), (conv_b1, "conv_b1"), (dt_b1, "dt_b1"), (d_1, "d_1"),
                             (flat(a_neg), "a_log"), (w_rt1, "w_rt1"), (b_rt1, "b_rt1"), (flat(b_e1), "b_e1"),
                             (b_e2[0:1, :], "b_e2")):
                src = d[src].partition_broadcast(P).rearrange("p o e -> p (o e)") if src == "b_rt1" else d[src]
                sp.dma_start(dst, src).then_inc(w1_loaded, 16)

            def expert_loads(e):
                sp.dma_start(w_e1, d["w_e1"][bass.ds(e * P, P), :]).then_inc(e1_loaded, 16)
                sp.dma_start(flat(w_e2), d["w_e2"][:, bass.ds(e * FC * D, FC * D)]).then_inc(e1_loaded, 16)
                sp.dma_start(xg1, slots_x1[bass.ds(e * CAP, CAP), :].rearrange("(i p) c -> p i c", p=P)).then_inc(xg1_loaded, 16)

            def expert_store(e):
                sp.wait_ge(moe_out, e * PIECES + PIECES)
                sp.dma_start(slots_y1[bass.ds(e * CAP, CAP), :].rearrange("(i p) c -> p i c", p=P), yg1).then_inc(y1_stored, 16)

            sp.wait_ge(scattered1, 16 * 2 * NT)
            expert_loads(0)
            with sp.Fori(0, E - 1) as e:
                expert_store(e)
                expert_loads(e + 1)
            expert_store(E - 1)
            for g in range(G4):
                sp.wait_ge(out_ready, g + 1)
                sp.dma_start(d["out"].rearrange("(i p) c -> p i c", p=P)[:, 4 * g:4 * g + 4, :], x[:, 4 * g:4 * g + 4, :]).then_inc(out_stored, 16)
            sp.wait_ge(out_stored, 16 * G4)

        @block.gpsimd
        def _(pool):
            o = Order(pool, pool_order)
            o.mark(pool.memset(ident[:], 0.0))
            o.mark(pool.memset(ones[:], 1.0))
            o.mark(pool.memset(zero, 0.0))
            o.mark(pool.memset(first_of_e[:], 1.0))
            o.link(pool.memset(seg[:], 1.0))
            pool.affine_select(out=ident[:], in_=ident[:], compare_op=ALU.not_equal, fill=1.0, base=0,
                               pattern=[[-1, P]], channel_multiplier=1).then_inc(consts_ready, 1)
            pool.affine_select(out=upper[:], in_=ones[:], compare_op=ALU.is_ge, fill=0.0, base=0,
                               pattern=[[1, P]], channel_multiplier=-1).then_inc(consts_ready, 1)
            pool.iota(iota_e[:], [[1, E]], base=0, channel_multiplier=0,
                      allow_small_or_imprecise_dtypes=True).then_inc(consts_ready, 1)
            pool.iota(iota_t[:], [[1, TILES_A]], base=0, channel_multiplier=0,
                      allow_small_or_imprecise_dtypes=True).then_inc(consts_ready, 1)
            pool.memset(first_of_e[:, :, 0], 0.0).then_inc(consts_ready, 1)
            pool.memset(seg[:, :, 0], 0.0).then_inc(consts_ready, 1)
            for r in range(TILES_A // 4):
                pool.dma_start(slots_x[r * 4 * P:(r + 1) * 4 * P, :].rearrange("(p i) c -> p (i c)", p=P),
                               zero).then_inc(zeroed, 16)
            for r in range(E * CAP // (4 * P)):
                pool.dma_start(slots_x1[r * 4 * P:(r + 1) * 4 * P, :].rearrange("(p i) c -> p (i c)", p=P),
                               zero).then_inc(zeroed, 16)
            pool.wait_ge(zeroed, ZEROED)
            pool.wait_ge(slots_ready, 1)
            pool.wait_ge(xn_ready, NT)
            for i in range(NT):
                for j in range(2):
                    pool.indirect_dma_start(out=slots_x, out_offset=bass.IndirectOffsetOnAxis(ap=sl_put[:, j, i:i + 1], axis=0),
                                            in_=xn[:, i, :], in_offset=None).then_inc(scattered, 16)
            def q_products(c):
                ts = bass.ds(c * CH, CH)
                pool.wait_ge(state_ready, c + 1)
                pool.tensor_tensor(PQ, bc(Q[:, :, ts].rearrange("p d l -> p l d"), 1, DI),
                                   bc(w_in.rearrange("p (D d) -> p D d", D=DI), 2, CH), ALU.mult).then_inc(pq_ready, 1)

            def o_products(c):
                pool.wait_ge(qh_ready, c + 1)
                pool.wait_ge(o_ps, c + 1)
                pool.tensor_tensor(OP, bc(EQ.rearrange("p D l -> p l D"), 1, HD),
                                   CS.rearrange("p (D d) l -> p d l D", D=DI)[:, :, 1:CH + 1, :], ALU.mult).then_inc(op_ready, 1)

            with pool.Fori(0, ROUTED_STEPS) as c:
                q_products(c)
                o_products(c)
            per = NT // (NCH - ROUTED_STEPS)
            for c in range(ROUTED_STEPS, NCH):
                q_products(c)
                if c == ROUTED_STEPS:
                    for k in range(TPS):
                        pool.wait_ge(y_stored[k], 16 * (ROUTED_STEPS + 1))
                for i in range(per * (c - ROUTED_STEPS), per * (c - ROUTED_STEPS + 1)):
                    for j, dst in enumerate((xn[:], xnT[:].rearrange("p (i c) -> p i c", c=D))):
                        pool.indirect_dma_start(out=dst[:, i, :], out_offset=None, in_=slots_y,
                                                in_offset=bass.IndirectOffsetOnAxis(ap=sl_put[:, j, i:i + 1], axis=0)
                                                ).then_inc(y_gathered, 16)
                o_products(c)
            pool.wait_ge(oT_ready, 1)
            pool.wait_ge(y_gathered, 16 * 2 * NT)
            pool.memset(pick_wide, 0.0).then_inc(pick_order, 1)
            for i in range(3):
                pool.wait_ge(pick_order, i + 1)
                part = pick_wide[2 * NS * i:2 * NS * (i + 1)]
                pool.affine_select(out=part, in_=part, compare_op=ALU.not_equal, fill=1.0, base=0,
                                   pattern=[[-1, 2 * NS], [0, P]], channel_multiplier=1).then_inc(pick_order, 1)
            pool.wait_ge(pick_order, 4)
            pool.wait_ge(slots_ready, 2)
            pool.wait_ge(xn_ready, 2 * NT)
            for i in range(NT):
                for j in range(2):
                    pool.indirect_dma_start(out=slots_x1, out_offset=bass.IndirectOffsetOnAxis(ap=sl_put[:, j, i:i + 1], axis=0),
                                            in_=xn[:, i, :], in_offset=None, bounds_check=E * CAP - 1,
                                            oob_is_err=False).then_inc(scattered1, 16)
            def deltas(r, s):
                for g in range(GD):
                    pool.wait_ge(sp_log, r * GD + (g + 1))
                    pool.tensor_tensor(del1[s][:, g, :], del1[s][:, g, :], sp1[:, g, :], ALU.add).then_inc(delta_ready, 1)
                for g in range(GD):
                    pool.wait_ge(delta_ready, r * GD + (g + 1))
                    pool.tensor_tensor(dh1[s][:, g, :], del1[s][:, g, :], h1[s][:, g, :], ALU.mult).then_inc(dh_ready, 1)

            def row(c, s, nxt):
                for n in range(NS):
                    pool.wait_ge(scanned, c * (GD * NS) + (GD * n + 2))
                    pool.wait_ge(c_copied, c * NS + (n + 1))
                    since(pool, yc_used, c * (GD * NS) + (GD * (n - 2) + 2))
                    pool.tensor_tensor(yc_g1[:, n % 2, :], st_g1[:, n % 2, :], c_row[:, n % 2, :], ALU.mult).then_inc(yc_g1_ready, 1)
                    if n == 8 and nxt is not None:
                        deltas(nxt, 1 - s)

            pool.wait_ge(h1_ready, GD)
            deltas(0, 0)
            all_rows(pool, row)
            pool.wait_ge(y1_stored, 16 * (E + 1))
            pool.wait_ge(s1_copied, B)
            for i in range(NT):
                for j, dst in enumerate((V, Q)):
                    rows = dst[:].rearrange("p a b -> p (a b)").rearrange("p (i c) -> p i c", c=D)
                    pool.indirect_dma_start(out=rows[:, i, :], out_offset=None, in_=slots_y1,
                                            in_offset=bass.IndirectOffsetOnAxis(ap=sl_get[:, j, i:i + 1], axis=0)
                                            ).then_inc(y1_gathered, 16)

        @block.tensor
        def _(pe):
            pe.wait_ge(consts_ready, 6)

            def transposes(layer):
                for g in range(G4):
                    n = layer * G4 + g
                    if n >= 2:
                        pe.wait_ge(xnT_copied, n - 1)
                    for j in range(4):
                        i = 4 * g + j
                        pe.wait_ge(xn_ready, layer * NT + i + 1)
                        t = pe.transpose(ps[:, g % 2, j * P:(j + 1) * P], xn[:, i, :], ident[:])
                    t.then_inc(xnT_ps, 1)

            def router(layer, w):
                pe.wait_ge(xnT_copied, (layer + 1) * G4)
                for i in range(NT):
                    m = pe.matmul(ps[:, 0, i * E:(i + 1) * E], xnT[:, i * P:(i + 1) * P], w, start=True, stop=True)
                m.then_inc(logits_ps, 1)
                pe.wait_ge(mask_ready, layer + 1)
                mk = mask.rearrange("p i e -> p (i e)")
                pe.matmul(ps[:, 1, 0:NT * E], upper[:], mk, start=True, stop=True).then_inc(ranks_ps, 1)
                pe.matmul(ps[:, 0, 0:NT * E], ones[:], mk, start=True, stop=True).then_inc(ranks_ps, 1)

            transposes(0)
            pe.wait_ge(w_loaded, 16 * 7)
            for b in range(B):
                rhs = xnT[:, b * L:(b + 1) * L]
                pe.wait_ge(xnT_copied, b + 1)
                for w in range(3):
                    cu = 3 * b + w
                    if cu >= 4:
                        pe.wait_ge(conv_done, cu - 3)
                    pe.matmul(ps[:, 2 + cu % 4, :], wproj[:, w * P:(w + 1) * P], rhs, start=True, stop=True).then_inc(proj_ps, 1)
                if b >= 1:
                    pe.wait_ge(gate_copied, b)
                    pe.wait_ge(lr_copied, b)
                pe.matmul(ps[:, 6, :], wproj[:, 3 * P:4 * P], rhs, start=True, stop=True).then_inc(gate_ps, 1)
                pe.matmul(ps[0:2 * H, 7, :], wlr[:], rhs, start=True, stop=True).then_inc(lr_ps, 1)
            router(0, wrt[:])
            pe.wait_ge(slots_ready, 1)
            pe.wait_ge(we_loaded, 16 * 3)
            def up(c, k):
                n0 = c * TPS
                off = pe.value_load(texp_i[0:1, bass.ds(n0 + k, 1)], min_val=0, max_val=(E - 1) * F)
                pe.wait_ge(xg_loaded[k], c * 16 + 16)
                pe.transpose(ps[:, 0, 0:P], xg[:, k, :], ident[:]).then_inc(xg_used, 1)
                pe.wait_ge(xgT_copied, n0 + (k + 1))
                if k == 2:
                    pe.wait_ge(hid_ready, n0 + 1)
                if k == 0 and not (isinstance(c, int) and c == 0):
                    pe.wait_ge(hid_ready, n0)
                pe.matmul(ps[:, 1 + 2 * (k % 2), :], xgT[:, k, :], wg_a[:, bass.ds(off, F)], start=True, stop=True).then_inc(gu_ps, 1)
                pe.matmul(ps[:, 2 + 2 * (k % 2), :], xgT[:, k, :], wu_a[:, bass.ds(off, F)], start=True, stop=True).then_inc(gu_ps, 1)

            def down(c, k, between=None):
                n0 = c * TPS
                off = pe.value_load(texp_i[0:1, bass.ds(n0 + k, 1)], min_val=0, max_val=(E - 1) * F)
                pe.wait_ge(hid_ready, n0 + (k + 1))
                if k >= 1:
                    pe.wait_ge(hidT_copied, n0 + k)
                for f in range(FC):
                    t = pe.transpose(ps[:, 5, f * P:(f + 1) * P], hid[:, k, f * P:(f + 1) * P], ident[:])
                t.then_inc(hidT_ps, 1)
                if between:
                    between()
                pe.wait_ge(hidT_copied, n0 + (k + 1))
                pe.wait_ge(y_copied, n0 + (k + 1))
                for f in range(FC):
                    m = pe.matmul(ps[:, 6, 0:D], hidT[:, k % 2, f * P:(f + 1) * P],
                                  wd_a[:, bass.ds(off + f * D, D)], start=(f == 0), stop=(f == FC - 1))
                m.then_inc(y_ps, 1)

            def q_sums(c):
                pe.wait_ge(pq_ready, c + 1)
                pe.wait_ge(o_copied, c + 1)
                for e in range(HD):
                    m = pe.matmul(ps[:, 7, 0:DI * CH], ident[:], PQ[:, :, :, e], start=(e == 0), stop=(e == HD - 1))
                m.then_inc(q_ps, 1)

            def o_sums(c):
                pe.wait_ge(op_ready, c + 2)
                for r in range(DI):
                    m = pe.matmul(ps[:, 7, 0:HD * CH], ident[:], OP[:, :, :, r], start=(r == 0), stop=(r == DI - 1))
                m.then_inc(o_ps, 1)

            def step(c, routed, before):
                if routed:
                    up(c, 0)
                if before >= 1:
                    o_sums(c - 1)
                if before >= 2:
                    down(c - 1, 2, lambda: q_sums(c))
                else:
                    q_sums(c)
                if routed:
                    up(c, 1)
                    down(c, 0)
                    up(c, 2)
                    down(c, 1)

            step(0, True, 0)
            with pe.Fori(1, ROUTED_STEPS) as c:
                step(c, True, 2)
            step(ROUTED_STEPS, False, 2)
            with pe.Fori(ROUTED_STEPS + 1, NCH) as c:
                step(c, False, 1)
            o_sums(NCH - 1)
            pe.wait_ge(oT_ready, 1)
            oT = K[:].rearrange("p a b -> p (a b)")
            for g in range(G4):
                if g >= 2:
                    pe.wait_ge(s_used, g - 1)
                for j in range(4):
                    i = 4 * g + j
                    m = pe.matmul(ps[:, 1 + g % 2, j * P:(j + 1) * P], oT[:, i * P:(i + 1) * P], wo[:], start=True, stop=True)
                m.then_inc(s_ps, 1)

            transposes(1)
            pe.wait_ge(w1_loaded, 16 * N_W1)
            router(1, w_rt1)
            pe.wait_ge(slots_ready, 2)
            pe.wait_ge(pick_ready, 1)

            def piece(c, p):
                if p == 0:
                    pe.wait_ge(xg1_loaded, c * 16 + 16)
                    pe.wait_ge(e1_loaded, c * 32 + 32)
                since(pe, moe_out, c * PIECES + (2 if p == 2 else 10 if p >= 10 else p - 1))
                bank = ps[:, 6 + p % 2, :]
                if p < 2:
                    for i in range(4 * p, min(4 * p + 4, CT)):
                        m = pe.transpose(bank[:, (i % 4) * P:(i % 4 + 1) * P], xg1[:, i, :], ident[:])
                elif p < 10:
                    f, half = divmod(p - 2, 2)
                    m = pe.matmul(bank[:, 0:CAP // 2], w_e1[:, f * P:(f + 1) * P],
                                  xgT1[:, half * (CAP // 2):(half + 1) * (CAP // 2)], start=True, stop=True)
                else:
                    for i in range(4 * (p - 10), min(4 * (p - 10) + 4, CT)):
                        o_ = bank[:, (i % 4) * D:(i % 4 + 1) * D]
                        for f in range(FC):
                            pe.matmul(o_, hid1[:, f, i * P:(i + 1) * P], w_e2[:, f, :], start=(f == 0), stop=False)
                        m = pe.matmul(o_, ones[0:1, :], b_e2[0:1, bass.ds(c * D, D)], start=False, stop=True)
                m.then_inc(moe_ps, 1)

            def inner(r, g):
                pe.matmul(ps[:, (6, 7, 7, 6)[g], :], w_inp[:, g * P:(g + 1) * P], xnT[:, bass.ds(r * L, L)], start=True, stop=True).then_inc(inp_ps, 1)

            def low_rank(r, s):
                pe.wait_ge(h1_ready, r * GD + GD)
                for g in range(GD):
                    m = pe.matmul(ps[0:DTR, 6, :], w_x1[:, g, :], h1[s][:, g, :], start=(g == 0), stop=(g == GD - 1))
                m.then_inc(xd_ps, 1)

            def b_and_c(r, s):
                for g in range(GD):
                    m = pe.matmul(ps[0:3 * 2 * NS, 7, :], w_bc1[:, g, :], h1[s][:, g, :], start=(g == 0), stop=(g == GD - 1))
                m.then_inc(bc_in_ps, 1)

            def delta(r, g):
                pe.matmul(ps[:, 7 - g, :], w_dt1[0:DTR, g * P:(g + 1) * P], xd1[0:DTR, :], start=True, stop=True).then_inc(dl_ps, 1)

            def spread(c, s, n):
                if n == 0:
                    pe.wait_ge(bc_lo, c + 1)
                since(pe, b_used, c * NS + (n - 1))
                pe.matmul(ps[:, 2 + n % 2, :], pick[:, n, :], bc_parts[s], start=True, stop=True).then_inc(b_ps, 1)
                since(pe, yc_ready, c * NS + (n - 1))
                pe.matmul(ps[:, n % 2, :], pick[:, NS + n, :], bc_parts[s], start=True, stop=True).then_inc(c_ps, 1)

            def accumulate(c, n):
                if n == 0 and not (isinstance(c, int) and c == 0):
                    pe.wait_ge(s1_copied, c)
                for g, (yc, ready) in enumerate(((yc_g0, yc_ready), (yc_g1, yc_g1_ready))):
                    pe.wait_ge(ready, c * NS + (n + 1))
                    pe.matmul(ps[:, 4 + g, :], ident[:], yc[:, n % 2, :], start=(n == 0), stop=(n == NS - 1)).then_inc(yc_used, 1)

            def out_proj(c, s):
                pe.wait_ge(yt_ready, c * GD + GD)
                for j in range(4):
                    for g in range(GD):
                        m = pe.matmul(ps[:, 4, j * D:(j + 1) * D], h1[s][:, g, j * P:(j + 1) * P], w_o1[:, g, :], start=(g == 0), stop=(g == GD - 1))
                m.then_inc(s1_ps, 1)

            def row(c, s, nxt):
                first = isinstance(c, int) and c == 0
                for n in range(NS):
                    if n < NS - 1:
                        spread(c, s, n + 1)
                    elif nxt is not None:
                        spread(nxt, 1 - s, 0)
                    if n >= 1:
                        if n == 1 and not first:
                            out_proj(c - 1, 1 - s)
                        accumulate(c, n - 1)
                    elif not first:
                        accumulate(c - 1, NS - 1)
                    if nxt is not None:
                        if n == 0:
                            pe.wait_ge(sp_ready, nxt * GD)
                            since(pe, moe_out, c * PIECES - 1)
                            inner(nxt, 0)
                            since(pe, moe_out, c * PIECES)
                            inner(nxt, 1)
                        if n == 2:
                            pe.wait_ge(conv1_done, nxt * GD + 1)
                        if n == 3:
                            pe.wait_ge(conv1_done, nxt * GD + 2)
                            inner(nxt, 2)
                            pe.wait_ge(moe_out, c * PIECES + 1)
                            inner(nxt, 3)
                        if n == 4:
                            pe.wait_ge(res_ready, nxt * GD + 1)
                        if n == 5:
                            pe.wait_ge(res_ready, nxt * GD + 2)
                            low_rank(nxt, 1 - s)
                            pe.wait_ge(moe_out, c * PIECES + 2)
                            b_and_c(nxt, 1 - s)
                        if n == 6:
                            pe.wait_ge(xd_copied, nxt + 1)
                        if n == 7:
                            pe.wait_ge(bc_rest1, nxt + 1)
                            delta(nxt, 0)
                            pe.wait_ge(moe_out, c * PIECES + 3)
                            delta(nxt, 1)
                        if n == 8:
                            pe.wait_ge(sp_ready, nxt * GD + GD)
                    for p in PIECES_AT.get(n, ()):
                        piece(c, p)

            inner(0, 0)
            inner(0, 1)
            pe.wait_ge(conv1_done, 2)
            inner(0, 2)
            inner(0, 3)
            pe.wait_ge(res_ready, 2)
            low_rank(0, 0)
            b_and_c(0, 0)
            pe.wait_ge(xd_copied, 1)
            pe.wait_ge(bc_rest1, 1)
            delta(0, 0)
            delta(0, 1)
            spread(0, 0, 0)
            all_rows(pe, row)
            accumulate(B - 1, NS - 1)
            out_proj(B - 1, 1)

        @block.scalar
        def _(act):
            o = Order(act, act_order)
            for s in (y_copied, o_copied, o_ps, op_ready):
                act.sem_inc(s, 1)
            for s in (*y_stored, y1_stored):
                act.sem_inc(s, 16)
            act.wait_ge(ln_var, 1)
            act.activation(rstd[:], rstd[:], ACT.Sqrt).then_inc(ln_std, 1)
            for g in range(G4):
                act.wait_ge(xnT_ps, g + 1)
                act.activation(xnT[:, g * 512:(g + 1) * 512], ps[:, g % 2, :], ACT.Copy).then_inc(xnT_copied, 1)

            def silu(cu):
                act.wait_ge(conv_done, cu + 1)
                act.activation(cv[:, cu % 4, :], cv[:, cu % 4, :], ACT.Silu).then_inc(silu_done, 1)

            act.wait_ge(taps_ready, 1)
            for cu in range(NCU):
                b, w = divmod(cu, 3)
                act.wait_ge(proj_ps, cu + 1)
                if cu >= 4:
                    act.wait_ge(stored[cu % 4], 16 * (cu // 4))
                act.activation(cv[:, cu % 4, :], ps[:, 2 + cu % 4, :], ACT.Copy, scale=taps[:, w, 3:4]).then_inc(tap_first, 1)
                if cu >= 1:
                    silu(cu - 1)
                if w == 2:
                    act.wait_ge(gate_ps, b + 1)
                    act.activation(gateT[:, b * L:(b + 1) * L], ps[:, 6, :], ACT.Copy).then_inc(gate_copied, 1)
                    act.wait_ge(lr_ps, b + 1)
                    act.activation(K[0:2 * H, b, :], ps[0:2 * H, 7, :], ACT.Copy).then_inc(lr_copied, 1)
            silu(NCU - 1)
            act.wait_ge(logits_ready, 1)
            act.activation(lg, lg, ACT.Exp).then_inc(probs_ready, 1)
            act.wait_ge(heads_loaded, 16 * 4 * B)
            act.wait_ge(logits_ps, 1)
            for n, t in enumerate((K, Q)):
                if n == 1:
                    act.wait_ge(norm2, 1)
                act.activation(TMP, t[:], ACT.Square).then_inc(squared, 1)
            for n in range(2):
                act.wait_ge(norm2, n + 1)
                act.activation(nrm[:, n, :], nrm[:, n, :], ACT.Sqrt).then_inc(norm_root, 1)
            act.wait_ge(lr_in, 1)
            o.link(act.activation(LR[:], LZ, ACT.Abs))
            o.link(act.activation(LR[:], LR[:], ACT.Exp, scale=-1.0))
            act.activation(LR[:], LR[:], ACT.Ln, bias=1.0).then_inc(lr_log, 1)
            act.preload_act_table(ACT.Tanh)

            temper = HD ** -0.5

            def xT(c, k):
                act.wait_ge(xg_used, c * TPS + (k + 1))
                act.activation(xgT[:, k, :], ps[:, 0, 0:P], ACT.Copy).then_inc(xgT_copied, 1)

            def tanh(c, k):
                act.wait_ge(gu_ps, c * (2 * TPS) + (2 * k + 1))
                act.activation(th[:, k, :], ps[:, 1 + 2 * (k % 2), :], ACT.Tanh, scale=0.5).then_inc(tanh_done, 1)

            def hT(c, k):
                act.wait_ge(hidT_ps, c * TPS + (k + 1))
                if k == 2:
                    act.wait_ge(y_ps, c * TPS + 1)
                act.activation(hidT[:, k % 2, :], ps[:, 5, :], ACT.Copy).then_inc(hidT_copied, 1)

            def y(c, k):
                act.wait_ge(y_ps, c * TPS + (k + 1))
                act.wait_ge(y_stored[k], c * 16 + 16)
                act.activation(yg[:, k, :], ps[:, 6, 0:D], ACT.Copy, scale=0.5).then_inc(y_copied, 1)

            def o_copy(c):
                act.wait_ge(o_ps, c + 2)
                act.activation(O[:, :, bass.ds(c * CH, CH)], ps[:, 7, 0:HD * CH].rearrange("p (d l) -> p d l", d=HD), ACT.Copy).then_inc(o_copied, 1)

            def step(c, routed, before):
                def exp(t, ready, done, scale=1.0):
                    act.wait_ge(ready, c + 1)
                    act.activation(t, t, ACT.Exp, scale=scale).then_inc(done, 1)

                if routed:
                    xT(c, 0)
                exp(EK, rec_k, exp_k)
                exp(EB, rec_b, exp_b, temper)
                if routed:
                    tanh(c, 0)
                if before >= 1:
                    o_copy(c - 1)
                if before >= 2:
                    hT(c - 1, 2)
                    y(c - 1, 2)
                if routed:
                    xT(c, 1)
                exp(EA, rec_a, exp_a, temper)
                if routed:
                    tanh(c, 1)
                if routed:
                    hT(c, 0)
                exp(EC, rec_c, exp_c, temper)
                exp(EQ, rec_q, exp_q)
                if routed:
                    y(c, 0)
                    xT(c, 2)
                    tanh(c, 2)
                exp(ED, rec_d, exp_d, temper)
                if routed:
                    hT(c, 1)
                    y(c, 1)

            step(0, True, 0)
            with act.Fori(1, ROUTED_STEPS) as c:
                step(c, True, 2)
            step(ROUTED_STEPS, False, 2)
            with act.Fori(ROUTED_STEPS + 1, NCH) as c:
                step(c, False, 1)
            o_copy(NCH - 1)
            act.wait_ge(o_centred, 1)
            for k in range(TPS):
                act.wait_ge(y_stored[k], 16 * (ROUTED_STEPS + 1))
            act.activation(V[:], O[:], ACT.Square).then_inc(o_squared, 1)
            act.wait_ge(o_var, 1)
            act.activation(nrm[:, 0, :], nrm[:, 0, :], ACT.Sqrt).then_inc(o_root, 1)
            for g in range(G4):
                act.wait_ge(mix_ready, g + 1)
                v = flat(xn[:])[:, g * 512:(g + 1) * 512]
                act.activation(v, v, ACT.Silu).then_inc(mix_silu, 1)

            act.wait_ge(w1_loaded, 16 * N_W1)
            act.wait_ge(ln_var, 2)
            act.activation(rstd[:], rstd[:], ACT.Sqrt).then_inc(ln_std, 1)
            for g in range(G4):
                act.wait_ge(xnT_ps, G4 + g + 1)
                act.activation(xnT[:, g * 512:(g + 1) * 512], ps[:, g % 2, :], ACT.Copy).then_inc(xnT_copied, 1)
            o.link(act.activation(a_neg, a_neg, ACT.Exp))
            o.link(act.activation(a_neg, a_neg, ACT.Copy, scale=-1.0))
            act.wait_ge(logits_ready, 2)
            act.activation(lg, lg, ACT.Exp).then_inc(probs_ready, 1)

            def piece(c, p):
                act.wait_ge(moe_ps, c * PIECES + (p + 1))
                bank = ps[:, 6 + p % 2, :]
                if p < 2:
                    w = min(4, CT - 4 * p) * P
                    i = act.activation(xgT1[:, 4 * p * P:4 * p * P + w], bank[:, 0:w], ACT.Copy)
                elif p < 10:
                    f, half = divmod(p - 2, 2)
                    i = act.activation(hid1[:, f, half * (CAP // 2):(half + 1) * (CAP // 2)], bank[:, 0:CAP // 2], ACT.Relu,
                                       bias=b_e1_now[:, f:f + 1])
                else:
                    w = min(4, CT - 4 * (p - 10))
                    if p == 10:
                        act.wait_ge(y1_stored, c * 16 + 16)
                    i = act.activation(yg1[:, 4 * (p - 10):4 * (p - 10) + w, :], bank[:, 0:w * D].rearrange("p (i c) -> p i c", c=D), ACT.Copy)
                i.then_inc(moe_out, 1)

            act.wait_ge(pick_order, 4)
            act.activation(pick, pick_wide, ACT.Copy).then_inc(pick_ready, 1)

            def taps1(r, s):
                for g in range(GD):
                    act.wait_ge(inp_ps, r * (2 * GD) + (g + 1))
                    act.activation(h1[s][:, g, :], ps[:, 6 + g, :], ACT.Identity, scale=conv_w1[:, g, 3:4], bias=conv_b1[:, g:g + 1]).then_inc(tap1_first, 1)

            def silus(r, s):
                for g in range(GD):
                    act.wait_ge(inp_ps, r * (2 * GD) + (GD + g + 1))
                    act.activation(res1[s][:, g, :], ps[:, 7 - g, :], ACT.Silu).then_inc(res_ready, 1)
                for g in range(GD):
                    act.wait_ge(conv1_done, r * GD + (g + 1))
                    act.activation(h1[s][:, g, :], h1[s][:, g, :], ACT.Silu).then_inc(h1_ready, 1)

            def xd_copy(r, s):
                act.wait_ge(xd_ps, r + 1)
                act.activation(xd1[0:DTR, :], ps[0:DTR, 6, :], ACT.Copy).then_inc(xd_copied, 1)

            def part_hi(r, s):
                act.wait_ge(bc_in_ps, r + 1)
                act.activation(bc_parts[s], ps[0:3 * 2 * NS, 7, :], ACT.Copy).then_inc(bc_hi, 1)

            def part_mid(r, s):
                act.wait_ge(bc_rest1, r + 1)
                act.activation(bc_parts[s][0:2 * 2 * NS], bc_rest[0:2 * 2 * NS, :], ACT.Copy).then_inc(bc_mid, 1)

            def part_lo(r, s):
                act.wait_ge(bc_rest2, r + 1)
                act.activation(bc_parts[s][0:2 * NS], bc_rest[0:2 * NS, :], ACT.Copy).then_inc(bc_lo, 1)

            def softplus(r, s):
                for g in range(GD):
                    act.wait_ge(dl_ps, r * GD + (g + 1))
                    o.mark(act.activation(sp1[:, g, :], ps[:, 7 - g, :], ACT.Abs, bias=dt_b1[:, g:g + 1]))
                    act.activation(del1[s][:, g, :], ps[:, 7 - g, :], ACT.Relu, bias=dt_b1[:, g:g + 1]).then_inc(sp_ready, 1)
                o.wait()
                for g in range(GD):
                    o.mark(act.activation(sp1[:, g, :], sp1[:, g, :], ACT.Exp, scale=-1.0))
                o.wait()
                for g in range(GD):
                    act.activation(sp1[:, g, :], sp1[:, g, :], ACT.Ln, bias=1.0).then_inc(sp_log, 1)

            def row(c, s, nxt):
                t = 1 - s
                act.wait_ge(delta_ready, c * GD + GD)
                for n in range(NS):
                    for g in range(GD):
                        k = GD * n + g
                        since(act, scanned, c * (GD * NS) + (k - 3))
                        act.activation(dA[:, k % 4, :], del1[s][:, g, :], ACT.Exp, scale=a_neg[:, g, n:n + 1]).then_inc(dA_ready, 1)
                    if n == 0:
                        o.mark(act.activation(b_e1_now[:], b_e1[:, bass.ds(c, 1), :].rearrange("p a b -> p (a b)"), ACT.Copy))
                    act.wait_ge(c_ps, c * NS + (n + 1))
                    since(act, yc_g1_ready, c * NS + (n - 1))
                    act.activation(c_row[:, n % 2, :], ps[:, n % 2, :], ACT.Copy).then_inc(c_copied, 1)
                    if n == 1 and not (isinstance(c, int) and c == 0):
                        s1_copy(c - 1)
                    if nxt is not None:
                        if n == 1:
                            taps1(nxt, t)
                        if n == 3:
                            silus(nxt, t)
                        if n == 5:
                            xd_copy(nxt, t)
                            part_hi(nxt, t)
                        if n == 6:
                            part_mid(nxt, t)
                        if n == 7:
                            part_lo(nxt, t)
                            softplus(nxt, t)
                    if n == 1:
                        o.wait()
                    for p in PIECES_AT.get(n, ()):
                        piece(c, p)

            def s1_copy(c):
                act.wait_ge(s1_ps, c + 1)
                act.activation(s1[:, bass.ds(c * L, L)], ps[:, 4, :], ACT.Copy).then_inc(s1_copied, 1)

            taps1(0, 0)
            silus(0, 0)
            xd_copy(0, 0)
            part_hi(0, 0)
            part_mid(0, 0)
            part_lo(0, 0)
            softplus(0, 0)
            PER_B = 2 * (2 * GD + 1)
            base = 0

            def pairs(i=None):
                nonlocal base
                if i is None:
                    base = o.total()
                else:
                    o.loop(i, base, PER_B)

            all_rows(act, row, pairs, lambda: o.end(base, PER_B, (B - 2) // 2))
            s1_copy(B - 1)
            for g in range(G4):
                act.wait_ge(mix_ready, G4 + g + 1)
                v = V[:].rearrange("p a b -> p (a b)")[:, g * 512:(g + 1) * 512]
                act.activation(v, v, ACT.Silu).then_inc(mix_silu, 1)

        @block.vector
        def _(dve):
            o = Order(dve, dve_order)
            tt = dve.tensor_tensor

            def layernorm(layer):
                for i in range(NT):
                    o.mark(dve.bn_stats(stats[:, i, :], x[:, i, :]))
                o.wait()
                for i in range(NT):
                    o.mark(dve.bn_aggr(mv[:, i, :], stats[:, i, :]))
                o.wait()
                dve.tensor_scalar_add(rstd[:], mv[:, :, 1], EPS).then_inc(ln_var, 1)
                dve.wait_ge(ln_std, layer + 1)
                o.link(dve.reciprocal(rstd[:], rstd[:]))
                for i in range(NT):
                    dve.tensor_scalar(xn[:, i, :], x[:, i, :], mv[:, i, 0:1], rstd[:, i:i + 1], ALU.subtract, ALU.mult).then_inc(xn_ready, 1)

            def dispatch(layer):
                lgf = ps[:, 0, 0:NT * E].rearrange("p (i e) -> p i e", e=E)
                dve.wait_ge(logits_ps, layer + 1)
                if layer == 0:
                    o.link(dve.tensor_copy(lg, lgf))
                else:
                    o.link(tt(lg, lgf, bc(b_rt1, 1, NT), ALU.add))
                o.link(dve.tensor_reduce(lmx[:], lg, AX_X, ALU.max))
                tt(lg, lg, bc(lmx[:], 2, E), ALU.subtract).then_inc(logits_ready, 1)
                dve.wait_ge(probs_ready, layer + 1)
                o.link(dve.tensor_reduce(lmx[:], lg, AX_X, ALU.add))
                o.link(dve.reciprocal(lmx[:], lmx[:]))
                o.link(tt(lg, lg, bc(lmx[:], 2, E), ALU.mult))
                for i in range(NT):
                    o.mark(dve.max(top[:, i, :], lg[:, i, :]))
                o.wait()
                for i in range(NT):
                    o.mark(dve.max_index(topi[:, i, :], top[:, i, :], lg[:, i, :]))
                o.wait()
                o.mark(dve.tensor_copy(e12[:, 0, :], topi[:, :, 0]))
                o.mark(dve.tensor_copy(e12[:, 1, :], topi[:, :, 1]))
                o.link(tt(wsum[:], top[:, :, 0], top[:, :, 1], ALU.add))
                o.link(dve.reciprocal(wsum[:], wsum[:]))
                for j in range(2):
                    o.mark(tt(w12[:, j, :], top[:, :, j], wsum[:], ALU.mult))
                    o.mark(tt(oh[:, j], bc(iota_e[:], 1, NT), bc(e12[:, j, :], 2, E), ALU.is_equal))
                o.wait()
                tt(mask, oh[:, 0], oh[:, 1], ALU.add).then_inc(mask_ready, 1)
                dve.wait_ge(ranks_ps, 2 * layer + 2)
                o.link(dve.tensor_copy(tot, ps[:, 0, 0:NT * E].rearrange("p (i e) -> p e i", e=E)))
                o.link(dve.tensor_tensor_scan(flat(inc), flat(first_of_e[:]), flat(tot), 0.0, ALU.mult, ALU.add))
                o.link(tt(tot, inc, tot, ALU.subtract))
                o.link(tt(rank, tot.rearrange("p e i -> p i e"),
                          ps[:, 1, 0:NT * E].rearrange("p (i e) -> p i e", e=E), ALU.add))
                if layer == 0:
                    o.link(dve.tensor_scalar(tl[:, 0, :], inc[:, :, NT - 1], float(P - 1), 1.0 / P, ALU.add, ALU.mult))
                    o.link(dve.tensor_scalar_add(tl[:, 0, :], tl[:, 0, :], -0.5 + 0.5 / P))
                    o.link(dve.tensor_copy(tl_i[:], tl[:, 0, :]))
                    o.link(dve.tensor_copy(tl[:, 0, :], tl_i[:]))
                    o.link(dve.tensor_tensor_scan(tl[:, 1, :], ones[:, 0:E], tl[:, 0, :], 0.0, ALU.mult, ALU.add))
                    o.link(tt(tl[:, 2, :], tl[:, 1, :], tl[:, 0, :], ALU.subtract))
                    o.link(dve.tensor_scalar(tl[:, 2, :], tl[:, 2, :], float(P), -1.0, ALU.mult, ALU.add))
                    o.link(tt(rank, rank, bc(tl[:, 2, :], 1, NT), ALU.add))
                    o.link(tt(tcmp, bc(iota_t[:], 2, E), bc(tl[:, 1, :], 1, TILES_A), ALU.is_ge))
                    o.link(dve.tensor_reduce(texp[:], tcmp, AX_X, ALU.add))
                    o.link(dve.tensor_scalar(texp[:], texp[:], float(E - 1), float(F), ALU.min, ALU.mult))
                    o.link(dve.tensor_copy(texp_i[:], texp[:]))
                else:
                    o.link(dve.tensor_scalar(keep, rank, float(CAP), None, ALU.is_le))
                    o.link(dve.tensor_scalar(tl[:, 2, :], iota_e[:], float(CAP), -1.0, ALU.mult, ALU.add))
                    o.link(tt(rank, rank, bc(tl[:, 2, :], 1, NT), ALU.add))
                for j in range(2):
                    o.mark(tt(prod[:, j], oh[:, j], rank, ALU.mult))
                o.wait()
                o.link(dve.tensor_reduce(slot[:].rearrange("p j i -> p (j i)"), prod.rearrange("p j i e -> p (j i) e"), AX_X, ALU.add))
                if layer == 0:
                    dve.tensor_copy(sl_put[:], slot[:]).then_inc(slots_ready, 1)
                    return
                for j in range(2):
                    o.mark(tt(prod[:, j], oh[:, j], keep, ALU.mult))
                o.wait()
                o.link(dve.tensor_reduce(kept[:].rearrange("p j i -> p (j i)"), prod.rearrange("p j i e -> p (j i) e"), AX_X, ALU.add))
                o.mark(tt(w12[:], w12[:], kept[:], ALU.mult))
                o.link(tt(slot[:], slot[:], kept[:], ALU.mult))
                o.mark(dve.tensor_copy(sl_get[:], slot[:]))
                o.link(dve.tensor_scalar(kept[:], kept[:], -float(SKIP), float(SKIP), ALU.mult, ALU.add))
                o.link(tt(slot[:], slot[:], kept[:], ALU.add))
                dve.tensor_copy(sl_put[:], slot[:]).then_inc(slots_ready, 1)

            dve.wait_ge(x_loaded, 64)
            layernorm(0)
            dve.wait_ge(w_loaded, 16 * 7)
            dve.tensor_scalar_add(taps[:, :, 3], taps[:, :, 3], 1.0).then_inc(taps_ready, 1)
            for cu in range(NCU):
                w, s = cu % 3, cu % 4
                dve.wait_ge(tap_first, cu + 1)
                for sh in (1, 2, 3):
                    i = dve.scalar_tensor_tensor(cv[:, s, sh:L], ps[:, 2 + s, 0:L - sh], taps[:, w, 3 - sh:4 - sh],
                                                 cv[:, s, sh:L], ALU.mult, ALU.add)
                    if sh < 3:
                        o.link(i)
                    else:
                        i.then_inc(conv_done, 1)
            dve.wait_ge(consts_ready, 6)
            dispatch(0)
            dve.wait_ge(heads_loaded, 16 * 4 * B)
            for n in range(2):
                dve.wait_ge(squared, n + 1)
                dve.tensor_reduce(nrm[:, n, :], TMP.rearrange("p e t -> p t e"), AX_X, ALU.add).then_inc(norm2, 1)
            dve.tensor_scalar_add(LZ, LZ, 1e-3).then_inc(lr_in, 1)
            for n, t in enumerate((K, Q)):
                dve.wait_ge(norm_root, n + 1)
                o.link(dve.reciprocal(nrm[:, n, :], nrm[:, n, :]))
                o.mark(tt(t[:], t[:], bc(nrm[:, n, :], 1, HD), ALU.mult))
            dve.wait_ge(lr_log, 1)
            o.link(dve.scalar_tensor_tensor(LR[:], LZ, 0.0, LR[:], ALU.max, ALU.add))
            o.wait()

            dve.wait_ge(zeroed, ZEROED)
            def rows(a):
                return bc(a.rearrange("p d l -> p l d"), 1, DI)

            def fast(a):
                return bc(a.rearrange("p (D d) -> p D d", D=DI), 2, CH)

            def weigh(a, e):
                return bc(e, 2, HD), bc(a, 1, DI)

            def keys_of(c):
                return K[:, :, bass.ds(c * CH, CH)]

            o.mark(tt(PK, rows(K[:, :, 0:CH]), fast(w_in), ALU.mult))
            o.wait()
            o.link(dve.tensor_reduce(SI, PK, AX_X, ALU.add))
            dve.sem_inc(state_ready, 1)

            def step(c, routed, last=False):
                ts = bass.ds(c * CH, CH)
                kc, vc = K[:, :, ts], V[:, :, ts]
                lr_of = lambda j: LR[:, j, bass.ds(c * CH, 1)]
                n0 = c * TPS
                red = dve.tensor_reduce
                over_D = lambda a: a.rearrange("p D l -> p l D")
                grid = lambda a: a.rearrange("p (D d) -> p D d", D=DI)

                def gate_up(k):
                    if not routed:
                        return
                    dve.wait_ge(tanh_done, n0 + (k + 1))
                    g, u = ps[:, 1 + 2 * (k % 2), :], ps[:, 2 + 2 * (k % 2), :]
                    m = o.mark(dve.scalar_tensor_tensor(th[:, k, :], th[:, k, :], 1.0, g, ALU.add, ALU.mult))
                    return m, k, u

                def gate_up2(started):
                    if not routed:
                        return
                    m, k, u = started
                    o.wait(m)
                    dve.wait_ge(gu_ps, n0 * 2 + (2 * k + 2))
                    tt(hid[:, k, :], th[:, k, :], u, ALU.mult).then_inc(hid_ready, 1)

                finished = o.n
                dve.wait_ge(state_ready, c + 1)
                m_k = o.mark(red(MK[:], over_D(SI), AX_X, ALU.max))
                m_b = o.mark(red(MX[:, 1], SI, AX_X, ALU.max))
                o.wait(m_k)
                tt(EK, SI, bc(MK[:], 1, DI), ALU.subtract).then_inc(rec_k, 1)
                o.wait(m_b)
                tt(EB, SI, bc(MX[:, 1], 2, CH), ALU.subtract).then_inc(rec_b, 1)
                o.wait(finished)
                o.mark(dve.tensor_copy(SC[:, :, 0], w_out))
                dve.wait_ge(exp_k, c + 1)
                z_k = o.mark(red(ZK[:], over_D(EK), AX_X, ALU.add))
                dve.wait_ge(exp_b, c + 1)
                z_b = o.mark(red(ZS[:, 1], EB, AX_X, ALU.add))
                o.wait(z_k)
                r_k = o.mark(dve.reciprocal(ZK[:], ZK[:]))
                o.wait(z_b)
                r_b = o.mark(dve.reciprocal(ZS[:, 1], ZS[:, 1]))
                o.wait(r_k)
                l_k = o.mark(tt(ZK[:], ZK[:], LR[:, 1, ts], ALU.mult))
                g_b = o.mark(tt(GB, *weigh(vc, EB), ALU.mult))
                o.wait(l_k)
                h_k = o.mark(tt(EK, EK, bc(ZK[:], 1, DI), ALU.mult))
                o.wait(g_b)
                s_b = o.mark(red(GR[:, 1].rearrange("p (D d) -> p D d", D=DI), GB, AX_X, ALU.add))
                o.wait(h_k)
                x_k = o.mark(tt(SC.rearrange("p (D d) l -> p D d l", D=DI)[:, :, :, 1:CH + 1], *weigh(vc, EK), ALU.mult))
                o.wait(s_b)
                n_b = o.mark(tt(grid(GR[:, 1]), grid(GR[:, 1]), bc(ZS[:, 1], 2, HD), ALU.mult))
                dve.wait_ge(op_ready, c + 1)
                o.wait(x_k)
                run = o.mark(dve.tensor_tensor_scan(flat(CS), flat(seg[:]), flat(SC), 0.0, ALU.mult, ALU.add))
                u0 = gate_up(0)
                o.wait(run)
                p_a = o.mark(tt(PV, rows(vc), fast(CS[:, :, CH]), ALU.mult))
                o.wait(n_b)
                wo1 = o.mark(dve.scalar_tensor_tensor(w_out1[:], GR[:, 1], lr_of(1), CS[:, :, CH], ALU.mult, ALU.add))
                o.wait(p_a)
                s_a = o.mark(red(SA, PV, AX_X, ALU.add))
                gate_up2(u0)
                o.wait(wo1)
                p_c = o.mark(tt(PK, rows(vc), fast(w_out1[:]), ALU.mult))
                o.wait(s_a)
                m_a = o.mark(red(MX[:, 0], SA, AX_X, ALU.max))
                o.wait(m_a)
                tt(EA, SA, bc(MX[:, 0], 2, CH), ALU.subtract).then_inc(rec_a, 1)
                o.wait(p_c)
                s_c = o.mark(red(SV, PK, AX_X, ALU.add))
                dve.wait_ge(q_ps, c + 1)
                m_q = o.mark(red(MQ[:], ps[:, 7, 0:DI * CH].rearrange("p (D l) -> p l D", D=DI), AX_X, ALU.max))
                o.wait(s_c)
                m_c = o.mark(red(MX[:, 2], SV, AX_X, ALU.max))
                dve.wait_ge(exp_a, c + 1)
                z_a = o.mark(red(ZS[:, 0], EA, AX_X, ALU.add))
                o.wait(m_c)
                tt(EC, SV, bc(MX[:, 2], 2, CH), ALU.subtract).then_inc(rec_c, 1)
                o.wait(m_q)
                tt(EQ, ps[:, 7, 0:DI * CH].rearrange("p (D l) -> p D l", D=DI), bc(MQ[:], 1, DI), ALU.subtract).then_inc(rec_q, 1)
                g_a = o.mark(tt(GA, *weigh(kc, EA), ALU.mult))
                o.wait(z_a)
                r_a = o.mark(dve.reciprocal(ZS[:, 0], ZS[:, 0]))
                u1 = gate_up(1)
                o.wait(g_a)
                s_a = o.mark(red(grid(GR[:, 0]), GA, AX_X, ALU.add))
                dve.wait_ge(exp_c, c + 1)
                z_c = o.mark(red(ZS[:, 2], EC, AX_X, ALU.add))
                o.wait(s_a)
                n_a = o.mark(tt(grid(GR[:, 0]), grid(GR[:, 0]), bc(ZS[:, 0], 2, HD), ALU.mult))
                g_c = o.mark(tt(GC, *weigh(kc, EC), ALU.mult))
                gate_up2(u1)
                o.wait(n_a)
                wi1 = o.mark(dve.scalar_tensor_tensor(w_in1[:], GR[:, 0], lr_of(0), w_in, ALU.mult, ALU.add))
                r_c = o.mark(dve.reciprocal(ZS[:, 2], ZS[:, 2]))
                o.wait(g_c)
                s_c = o.mark(red(grid(GR[:, 2]), GC, AX_X, ALU.add))
                o.wait(wi1)
                p_d = o.mark(tt(PV, rows(kc), fast(w_in1[:]), ALU.mult))
                o.wait(s_c)
                n_c = o.mark(tt(grid(GR[:, 2]), grid(GR[:, 2]), bc(ZS[:, 2], 2, HD), ALU.mult))
                o.wait(p_d)
                s_d = o.mark(red(SD, PV, AX_X, ALU.add))
                u2 = gate_up(2)
                dve.wait_ge(pq_ready, c + 1)
                o.wait(n_c)
                wi2 = o.mark(dve.scalar_tensor_tensor(w_in, GR[:, 2], lr_of(0), w_in1[:], ALU.mult, ALU.add))
                o.wait(s_d)
                m_d = o.mark(red(MX[:, 3], SD, AX_X, ALU.max))
                o.wait(wi2)
                if not last:
                    p_n = o.mark(tt(PK, rows(keys_of(c + 1)), fast(w_in), ALU.mult))
                o.wait(m_d)
                tt(ED, SD, bc(MX[:, 3], 2, CH), ALU.subtract).then_inc(rec_d, 1)
                if not last:
                    o.wait(p_n)
                    red(SI, PK, AX_X, ALU.add).then_inc(state_ready, 1)
                gate_up2(u2)
                dve.wait_ge(exp_d, c + 1)
                z_d = o.mark(red(ZS[:, 3], ED, AX_X, ALU.add))
                g_d = o.mark(tt(GV, *weigh(vc, ED), ALU.mult))
                dve.wait_ge(exp_q, c + 1)
                z_q = o.mark(red(ZQ[:], over_D(EQ), AX_X, ALU.add))
                o.wait(g_d)
                s_d = o.mark(red(grid(GR[:, 3]), GV, AX_X, ALU.add))
                r_d = o.mark(dve.reciprocal(ZS[:, 3], ZS[:, 3]))
                o.wait(z_q)
                r_q = o.mark(dve.reciprocal(ZQ[:], ZQ[:]))
                o.wait(r_d)
                n_d = o.mark(tt(grid(GR[:, 3]), grid(GR[:, 3]), bc(ZS[:, 3], 2, HD), ALU.mult))
                o.wait(r_q)
                tt(EQ, EQ, bc(ZQ[:], 1, DI), ALU.mult).then_inc(qh_ready, 1)
                o.wait(n_d)
                o.mark(dve.scalar_tensor_tensor(w_out, GR[:, 3], lr_of(1), w_out1[:], ALU.mult, ALU.add))

            first = o.total()
            PER_R, PER_P = 49, 46
            with dve.Fori(0, ROUTED_STEPS) as c:
                o.loop(c, first, PER_R)
                step(c, True)
            o.end(first, PER_R, ROUTED_STEPS)
            first2 = o.total()
            with dve.Fori(ROUTED_STEPS, NCH - 1) as c:
                o.loop(c, first2 - ROUTED_STEPS * PER_P, PER_P)
                step(c, False)
            o.end(first2, PER_P, NCH - 1 - ROUTED_STEPS)
            step(NCH - 1, False, last=True)
            o.wait()
            dve.wait_ge(o_copied, NCH + 1)
            dT = lambda a: a.rearrange("p e t -> p t e")
            o.link(dve.tensor_reduce(nrm[:, 0, :], dT(O[:]), AX_X, ALU.add))
            o.link(dve.tensor_scalar(nrm[:, 0, :], nrm[:, 0, :], 1.0 / HD, None, ALU.mult))
            tt(O[:], O[:], bc(nrm[:, 0, :], 1, HD), ALU.subtract).then_inc(o_centred, 1)
            dve.wait_ge(o_squared, 1)
            o.link(dve.tensor_reduce(nrm[:, 0, :], dT(V[:]), AX_X, ALU.add))
            dve.tensor_scalar(nrm[:, 0, :], nrm[:, 0, :], 1.0 / HD, EPS, ALU.mult, ALU.add).then_inc(o_var, 1)
            dve.wait_ge(o_root, 1)
            o.link(dve.reciprocal(nrm[:, 0, :], nrm[:, 0, :]))
            tt(O[:], O[:], bc(nrm[:, 0, :], 1, HD), ALU.mult).then_inc(o_ready, 1)
            oT = K[:].rearrange("p a b -> p (a b)")
            dve.wait_ge(oT_loaded, 16)
            o.link(dve.tensor_scalar(oT, oT, ln_gb[:, 0:1], ln_gb[:, 1:2], ALU.mult, ALU.add))
            tt(oT, oT, gateT[:], ALU.mult).then_inc(oT_ready, 1)

            def combine(g, y1, y2):
                r = lambda a: flat(a)[:, g * 512:(g + 1) * 512].rearrange("p (i c) -> p i c", c=D)
                a, b2 = r(y1), r(y2)
                o.mark(tt(a, a, bc(w12[:, 0, 4 * g:4 * g + 4], 2, D), ALU.mult))
                o.link(tt(b2, b2, bc(w12[:, 1, 4 * g:4 * g + 4], 2, D), ALU.mult))
                tt(a, a, b2, ALU.add).then_inc(mix_ready, 1)

            dve.wait_ge(y_gathered, 16 * 2 * NT)
            dve.wait_ge(x_loaded, 128)
            for g in range(G4):
                combine(g, xn[:], xnT[:])
            for g in range(G4):
                v = flat(xn[:])[:, g * 512:(g + 1) * 512]
                xs = x[:, 4 * g:4 * g + 4, :].rearrange("p i c -> p (i c)")
                dve.wait_ge(s_ps, g + 1)
                dve.wait_ge(mix_silu, g + 1)
                i = tt(v, v, ps[:, 1 + g % 2, :], ALU.mult)
                i.then_inc(s_used, 1)
                dve.wait_ge(s_used, g + 1)
                tt(xs, xs, v, ALU.add).then_inc(x1_ready, 1)

            dve.wait_ge(x1_ready, G4)
            dve.wait_ge(w1_loaded, 16 * N_W1)
            layernorm(1)
            dispatch(1)
            def conv1(r, s, g):
                dve.wait_ge(tap1_first, r * GD + (g + 1))
                for sh in (1, 2, 3):
                    i = dve.scalar_tensor_tensor(h1[s][:, g, sh:L], ps[:, 6 + g, 0:L - sh], conv_w1[:, g, 3 - sh:4 - sh],
                                                 h1[s][:, g, sh:L], ALU.mult, ALU.add)
                    if sh < 3:
                        o.link(i)
                    else:
                        i.then_inc(conv1_done, 1)

            def rest1(r, s):
                dve.wait_ge(bc_hi, r + 1)
                tt(bc_rest[0:2 * 2 * NS, :], ps[0:2 * 2 * NS, 7, :], bc_parts[s][0:2 * 2 * NS], ALU.subtract).then_inc(bc_rest1, 1)

            def rest2(r, s):
                dve.wait_ge(bc_mid, r + 1)
                tt(bc_rest[0:2 * NS, :], bc_rest[0:2 * NS, :], bc_parts[s][0:2 * NS], ALU.subtract).then_inc(bc_rest2, 1)

            def finish(c, s):
                dve.wait_ge(yc_used, (c + 1) * (GD * NS))
                for g in range(GD):
                    o.mark(dve.scalar_tensor_tensor(h1[s][:, g, :], h1[s][:, g, :], d_1[:, g:g + 1], ps[:, 4 + g, :], ALU.mult, ALU.add))
                for g in range(GD):
                    o.wait(o.n - 1 + g)
                    tt(h1[s][:, g, :], h1[s][:, g, :], res1[s][:, g, :], ALU.mult).then_inc(yt_ready, 1)

            def row(c, s, nxt):
                t = 1 - s
                first = isinstance(c, int) and c == 0
                st = lambda n, g: st_g1[:, n % 2, :] if g else st_g0

                def inject(n, g):
                    dve.wait_ge(b_ps, c * NS + (n + 1))
                    since(dve, scanned, c * (GD * NS) + (GD * (n - 1) + g + 1))
                    i = tt(dBu[:, g, :], dh1[s][:, g, :], ps[:, 2 + n % 2, :], ALU.mult)
                    if g == 0:
                        return o.mark(i)
                    i.then_inc(b_used, 1)

                def scan(n, g):
                    k = GD * n + g
                    dve.wait_ge(dA_ready, c * (GD * NS) + (k + 1))
                    if g:
                        dve.wait_ge(b_used, c * NS + (n + 1))
                        since(dve, yc_g1_ready, c * NS + (n - 1))
                    else:
                        since(dve, yc_ready, c * NS + n)
                    dve.tensor_tensor_scan(st(n, g), dA[:, k % 4, :], dBu[:, g, :], 0.0, ALU.mult, ALU.add).then_inc(scanned, 1)

                dve.wait_ge(dh_ready, c * GD + GD)
                for n in range(NS):
                    injected = inject(n, 0)
                    inject(n, 1)
                    o.wait(injected)
                    scan(n, 0)
                    scan(n, 1)
                    dve.wait_ge(scanned, c * (GD * NS) + (GD * n + 1))
                    dve.wait_ge(c_copied, c * NS + (n + 1))
                    since(dve, yc_used, c * (GD * NS) + (GD * (n - 2) + 1))
                    tt(yc_g0[:, n % 2, :], st_g0, ps[:, n % 2, :], ALU.mult).then_inc(yc_ready, 1)
                    if n == 0 and not first:
                        finish(c - 1, t)
                    if nxt is not None:
                        if n in (1, 2):
                            conv1(nxt, t, n - 1)
                        if n == 5:
                            rest1(nxt, t)
                        if n == 6:
                            rest2(nxt, t)

            for g in range(GD):
                conv1(0, 0, g)
            rest1(0, 0)
            rest2(0, 0)
            PER_B = 2 * (3 * GD + NS)
            base = 0

            def pairs(i=None):
                nonlocal base
                if i is None:
                    base = o.total()
                else:
                    o.loop(i, base, PER_B)

            all_rows(dve, row, pairs, lambda: o.end(base, PER_B, (B - 2) // 2))
            finish(B - 1, 1)
            dve.wait_ge(y1_gathered, 16 * 2 * NT)
            dve.wait_ge(s1_copied, B)
            for g in range(G4):
                combine(g, V[:], Q[:])
            for g in range(G4):
                v = V[:].rearrange("p a b -> p (a b)")[:, g * 512:(g + 1) * 512]
                xs = x[:, 4 * g:4 * g + 4, :].rearrange("p i c -> p (i c)")
                dve.wait_ge(mix_silu, G4 + g + 1)
                o.link(tt(v, v, s1[:, g * 512:(g + 1) * 512], ALU.mult))
                tt(xs, xs, v, ALU.add).then_inc(out_ready, 1)


def host(inputs):
    import numpy as np
    c = np.ascontiguousarray
    a = {k: np.asarray(v) for k, v in inputs.items()}
    r = {}
    r["x"] = c(a["L0_attn_hidden_states"].reshape(T, D))
    r["wproj"] = c(np.concatenate([a[f"L0_attn_W{n}"].T for n in "qkvg"], axis=1))
    r["wlr"] = c(a["L0_attn_Wlr"].T)
    r["wo"] = c(a["L0_attn_Wo"].T)
    r["taps"] = c(np.concatenate([a["L0_attn_cq"], a["L0_attn_ck"], a["L0_attn_cv"]], axis=1))
    r["ln_gb"] = c(np.stack([np.tile(a["L0_attn_ln_g"], H), np.tile(a["L0_attn_ln_b"], H)], axis=1))
    st = np.concatenate([a[n][0].transpose(1, 0, 2).reshape(H, DI * HD) for n in ("L0_attn_W_in_init", "L0_attn_W_out_init")], axis=1)
    r["state0"] = c(np.tile(st, (B, 1)))
    r["wrt"] = c(a["L0_ffn_W_router"].T)
    r["wg_a"] = c(a["L0_ffn_W_gate"].transpose(2, 0, 1).reshape(D, E * F))
    r["wu_a"] = c(a["L0_ffn_W_up"].transpose(2, 0, 1).reshape(D, E * F))
    r["wd_a"] = c(a["L0_ffn_W_down"].reshape(E, D, FC, P).transpose(3, 0, 2, 1).reshape(P, E * FC * D))
    r["w_in1"] = c(a["L1_attn_in_proj_w"])
    rows = lambda m: c(m.reshape(GD, P, -1).transpose(1, 0, 2).reshape(P, -1))
    for n, k in (("w_x1", "x_proj_w"), ("w_o1", "out_proj_w"), ("conv_w1", "conv_w"), ("conv_b1", "conv_b"),
                 ("dt_b1", "dt_proj_b"), ("d_1", "D_param"), ("a_log", "A_log")):
        r[n] = rows(a["L1_attn_" + k])
    r["w_bc1"] = c(np.concatenate([r["w_x1"].reshape(P, GD, -1)[:, :, DTR:]] * 3, axis=2).reshape(P, -1))
    r["w_x1"] = c(r["w_x1"].reshape(P, GD, -1)[:, :, :DTR].reshape(P, -1))
    r["w_dt1"] = c(a["L1_attn_dt_proj_w"])
    r["w_rt1"] = c(a["L1_ffn_gate_w"])
    r["b_rt1"] = c(a["L1_ffn_gate_b"].reshape(1, E))
    r["b_e1"] = c(a["L1_ffn_b1"].reshape(E, FC, P).transpose(2, 0, 1).reshape(P, E * FC))
    r["b_e2"] = c(a["L1_ffn_b2"].reshape(1, E * D))
    r["w_e1"] = c(a["L1_ffn_w1"].reshape(E * D, F))
    r["w_e2"] = c(a["L1_ffn_w2"].reshape(E, FC, P, D).transpose(2, 0, 1, 3).reshape(P, E * FC * D))
    return r


def kernel(**inputs):
    import numpy as _np
    import concourse.bacc as _bacc
    from concourse.bass_utils import run_bass_kernel_spmd as _run

    nc = _bacc.Bacc("TRN2", target_bir_lowering=False, num_devices=1)
    arrays, d = {}, {}
    for name, a in host(inputs).items():
        arrays[f"in_{name}"] = a
        d[name] = nc.dram_tensor(f"in_{name}", a.shape, mybir.dt.from_np(a.dtype), kind="ExternalInput").ap()
    d["out"] = nc.dram_tensor("out_0_dram", (T, D), F32, kind="ExternalOutput").ap()
    build(nc, d)
    got = _run(nc, [arrays], core_ids=[0]).results[0]["out_0_dram"]
    return _np.asarray(got).reshape(B, L, D)
```

```python
from contextlib import ExitStack

import concourse.bass as bass
from concourse import mybir

F32 = mybir.dt.float32
BF16 = mybir.dt.bfloat16
I32 = mybir.dt.int32
U32 = mybir.dt.uint32
ALU = mybir.AluOpType
ACT = mybir.ActivationFunctionType
AX_X = mybir.AxisListType.X

P = 128
B, L, D = 8, 512, 128
T = B * L
NT = T // P
G4 = NT // 4
H, HD, DI, CH = 16, 8, 4, 16
NCH = L // CH
E = 8
F = 512
FC = F // P
CONV = 4
TILES_A = 2 * T // P + E
CAP = int(1.25 * T / E)
CT = CAP // P
DIN, NS, DTR = 256, 16, 64
GD = DIN // P
TPS = 3
ROUTED_STEPS = TILES_A // TPS
FIRST = 3
AFTER = FIRST + ROUTED_STEPS
EPS = 1e-5
SKIP = 1 << 20


def bc(ap, axis, n):
    a = ap.unsqueeze(axis)
    shape = list(a.shape)
    shape[axis] = n
    return a.broadcast_to(shape)


def flat(a):
    return a if len(a.shape) == 2 else a.rearrange("p a b -> p (a b)") if len(a.shape) == 3 else a.rearrange("p a b c -> p (a b c)")


class Region:

    def __init__(self, tile):
        self.cols, self.at = flat(tile), 0

    def take(self, *shape):
        n = 1
        for s in shape:
            n *= s
        a = self.cols[:, self.at:self.at + n]
        self.at += n
        assert self.at <= self.cols.shape[1]
        if len(shape) == 2:
            a = a.rearrange("p (a b) -> p a b", a=shape[0])
        if len(shape) == 3:
            a = a.rearrange("p (a b c) -> p a b c", a=shape[0], b=shape[1])
        return a


class Order:

    def __init__(self, eng, sem):
        self.eng, self.sem, self.base, self.n = eng, sem, 0, 0

    def mark(self, ins):
        self.n += 1
        ins.then_inc(self.sem, 1)
        return self.n

    def wait(self, n=None):
        n = self.n if n is None else n
        v = self.base + n
        self.eng.wait_ge(self.sem, v)

    def link(self, ins):
        self.mark(ins)
        self.wait()

    def loop(self, c, first, per):
        self.base, self.n = c * per + first, 0

    def end(self, first, per, trips):
        assert self.n == per, (self.n, per)
        self.base, self.n = first + per * trips, 0

    def total(self):
        return self.base + self.n


def build(nc, d):
    with ExitStack() as ctx:
        def sb(name, shape, dt=F32):
            return ctx.enter_context(nc.sbuf_tensor(name, shape, dt))

        def sem(name):
            return ctx.enter_context(nc.semaphore(name))

        def dram(name, shape):
            return nc.dram_tensor(name, shape, F32).ap()

        qkv_scr = dram("qkv_scr", [3, P, T])
        lr_scr = dram("lr_scr", [2 * H, T])
        o_scr = dram("o_scr", [P, T])
        slots_x = dram("slots_x", [TILES_A * P, D])
        slots_y = dram("slots_y", [TILES_A * P, D])
        slots_x1 = dram("slots_x1", [E * CAP, D])
        slots_y1 = dram("slots_y1", [E * CAP, D])

        ps = ctx.enter_context(nc.psum_tensor("ps", [P, 8, 512], F32))
        ident = sb("ident", [P, P])
        upper = sb("upper", [P, P])
        ones = sb("ones", [P, P])
        iota_e = sb("iota_e", [P, E])
        iota_t = sb("iota_t", [P, TILES_A])
        first_of_e = sb("first_of_e", [P, E, NT])
        x = sb("x", [P, NT, D])
        xn = sb("xn", [P, NT, D])
        xnT = sb("xnT", [P, T])
        stats = sb("stats", [P, NT, 6])
        mv = sb("mv", [P, NT, 2])
        rstd = sb("rstd", [P, NT])
        wproj = sb("wproj", [P, 4 * P])
        wlr = sb("wlr", [P, 2 * H])
        wo = sb("wo", [P, D])
        taps = sb("taps", [P, 3, CONV])
        ln_gb = sb("ln_gb", [P, 2])
        wrt = sb("wrt", [P, E])
        wg_a = sb("wg_a", [P, E * F])
        wu_a = sb("wu_a", [P, E * F])
        wd_a = sb("wd_a", [P, E * FC * D])
        cv = sb("cv", [P, 4, L])
        gateT = sb("gateT", [P, T])
        K = sb("K", [P, HD, L])
        V = sb("V", [P, HD, L])
        Q = sb("Q", [P, HD, L])
        O = sb("O", [P, HD, L])
        nrm = sb("nrm", [P, 2, L])
        LR = sb("LR", [P, 2, L])
        lmx = sb("lmx", [P, NT])
        top = sb("top", [P, NT, 8])
        topi = sb("topi", [P, NT, 8], U32)
        e12 = sb("e12", [P, 2, NT])
        w12 = sb("w12", [P, 2, NT])
        wsum = sb("wsum", [P, NT])
        slot = sb("slot", [P, 2, NT])
        kept = sb("kept", [P, 2, NT])
        sl_put = sb("sl_put", [P, 2, NT], I32)
        sl_get = sb("sl_get", [P, 2, NT], I32)
        tl = sb("tl", [P, 3, E])
        tl_i = sb("tl_i", [P, E], I32)
        texp = sb("texp", [P, TILES_A])
        texp_i = sb("texp_i", [P, TILES_A], I32)
        r = Region(O[:])
        lg, mask, rank, keep = (r.take(NT, E) for _ in range(4))
        oh, prod = (r.take(2, NT, E) for _ in range(2))
        tot, inc = (r.take(E, NT) for _ in range(2))
        tcmp = r.take(TILES_A, E)
        zero = r.take(4 * D)
        TMP = xnT[:].rearrange("p (e t) -> p e t", e=HD)
        r = Region(xnT[:])
        xg, xgT, yg = r.take(TPS, D), r.take(TPS, P), r.take(TPS, D)
        r = Region(xn[:])
        th, hid, hidT = r.take(TPS, F), r.take(TPS, F), r.take(2, F)
        r = Region(cv[:])
        GA, GB, GC, GV = (r.take(DI, HD, CH) for _ in range(4))
        r = Region(x[:])
        LZ = r.take(2, L)
        PK, PQ, PV = (r.take(DI, CH, HD) for _ in range(3))
        SC, CS = r.take(DI * HD, CH + 1), r.take(DI * HD, CH + 1)
        EK, EQ = r.take(DI, CH), r.take(DI, CH)
        r = Region(LZ)
        OP = r.take(HD, CH, DI)
        SI, SA, SV, SD, EA, EB, EC, ED = (r.take(DI, CH) for _ in range(8))
        X = sb("X", [P, 2 * DI * HD])
        w_in, w_out = X[:, 0:DI * HD], X[:, DI * HD:2 * DI * HD]
        w_in1, w_out1 = sb("w_in_1", [P, DI * HD]), sb("w_out_1", [P, DI * HD])
        MK, MQ, ZK, ZQ = (sb(n, [P, CH]) for n in ("MK", "MQ", "ZK", "ZQ"))
        MX = sb("MX", [P, 4, DI])
        ZS = sb("ZS", [P, 4, DI])
        GR = sb("GR", [P, 4, DI * HD])
        seg = sb("seg", [P, DI * HD, CH + 1])

        r = Region(wg_a[:])
        w_bc1 = r.take(GD, 3 * 2 * NS)
        w_inp, w_x1, w_dt1, w_o1 = r.take(2 * DIN), r.take(GD, DTR), r.take(DIN), r.take(GD, D)
        conv_w1, conv_b1, dt_b1, d_1 = r.take(GD, CONV), r.take(GD), r.take(GD), r.take(GD)
        a_neg, w_rt1, b_rt1, b_e1, b_e2 = r.take(GD, NS), r.take(E), r.take(E), r.take(E, FC), r.take(E * D)
        w_e2_odd, xg1_odd = r.take(FC, D), r.take(CT, D)
        r = Region(wu_a[:])
        w_e1_even, w_e1_odd, w_e2_even, hid1 = r.take(F), r.take(F), r.take(FC, D), r.take(FC, CAP)
        r = Region(wd_a[:])
        xg1_even, xgT1, yg1, dA_far = r.take(CT, D), r.take(CAP), r.take(CT, D), r.take(4, L)
        w_e1, w_e2, xg1 = (w_e1_even, w_e1_odd), (w_e2_even, w_e2_odd), (xg1_even, xg1_odd)
        pick_wide = gateT[0:3 * 2 * NS, :].rearrange("p (r c) -> p r c", c=P)
        pick = flat(cv[:]).bitcast(BF16).rearrange("p (r c) -> p r c", c=P)[0:3 * 2 * NS]
        even_odd = [Region(K[:]), Region(gateT[:])]
        h1, res1, del1, dh1 = ([r.take(GD, L) for r in even_odd] for _ in range(4))
        r = Region(V[:])
        xd1, dA_near, sp1, bc_rest = r.take(L), r.take(4, L), r.take(GD, L), r.take(L)
        r = Region(Q[:])
        dBu, st_g1, yc_g0, yc_g1 = (r.take(2, L) for _ in range(4))
        r = Region(nrm[:])
        bc_parts = [r.take(L // 2).bitcast(BF16)[0:3 * 2 * NS] for _ in range(2)]
        st_g0 = r.take(L)
        c_row = LR[:]
        y_sum = wproj[:], flat(seg[:])[:, 0:L]

        def dA(k):
            return (dA_near, dA_far)[k // 4 % 2][:, k % 4, :]

        b_e1_now = sb("b_e1_now", [P, FC])
        s1 = O[:].rearrange("p e t -> p (e t)")

        x_loaded = sem("x_loaded")
        w_loaded = sem("w_loaded")
        we_loaded = sem("we_loaded")
        consts_ready = sem("consts_ready")
        pool_order = sem("pool_order")
        zeroed = sem("zeroed")
        dve_order = sem("dve_order")
        act_order = sem("act_order")
        ln_var = sem("ln_var")
        ln_std = sem("ln_std")
        xn_ready = sem("xn_ready")
        xnT_ps = sem("xnT_ps")
        xnT_copied = sem("xnT_copied")
        proj_ps = sem("proj_ps")
        gate_ps = sem("gate_ps")
        lr_ps = sem("lr_ps")
        tap_first = sem("tap_first")
        taps_ready = sem("taps_ready")
        conv_done = sem("conv_done")
        silu_done = sem("silu_done")
        gate_copied = sem("gate_copied")
        lr_copied = sem("lr_copied")
        stored = [sem(f"stored{i}") for i in range(4)]
        lr_stored = [sem(f"lr_stored{k}") for k in range(2)]
        heads_loaded = sem("heads_loaded")
        squared = sem("squared")
        norm2 = sem("norm2")
        norm_root = sem("norm_root")
        lr_in = sem("lr_in")
        lr_log = sem("lr_log")
        logits_ps = sem("logits_ps")
        logits_ready = sem("logits_ready")
        probs_ready = sem("probs_ready")
        mask_ready = sem("mask_ready")
        ranks_ps = sem("ranks_ps")
        slots_ready = sem("slots_ready")
        scattered = sem("scattered")
        exp_k = sem("exp_k")
        exp_q = sem("exp_q")
        exp_a, exp_b, exp_c, exp_d = (sem(f"exp_{n}") for n in "abcd")
        rec_k = sem("rec_k")
        rec_q = sem("rec_q")
        rec_a, rec_b, rec_c, rec_d = (sem(f"rec_{n}") for n in "abcd")
        pq_ready = sem("pq_ready")
        q_ps = sem("q_ps")
        qh_ready = sem("qh_ready")
        op_ready = sem("op_ready")
        o_ps = sem("o_ps")
        o_copied = sem("o_copied")
        state_ready = sem("state_ready")
        xg_loaded = [sem(f"xg_loaded{k}") for k in range(TPS)]
        xg_used = sem("xg_used")
        xgT_copied = sem("xgT_copied")
        gu_ps = sem("gu_ps")
        tanh_done = sem("tanh_done")
        hid_ready = sem("hid_ready")
        hidT_ps = sem("hidT_ps")
        hidT_copied = sem("hidT_copied")
        y_ps = sem("y_ps")
        y_copied = sem("y_copied")
        y_stored = [sem(f"y_stored{k}") for k in range(TPS)]
        o_centred = sem("o_centred")
        o_squared = sem("o_squared")
        o_var = sem("o_var")
        o_root = sem("o_root")
        o_ready = sem("o_ready")
        o_stored = sem("o_stored")
        oT_loaded = sem("oT_loaded")
        oT_ready = sem("oT_ready")
        s_ps = sem("s_ps")
        s_used = sem("s_used")
        y_gathered = sem("y_gathered")
        mix_ready = sem("mix_ready")
        mix_silu = sem("mix_silu")
        x1_ready = sem("x1_ready")
        out_stored = sem("out_stored")

        w1_loaded = sem("w1_loaded")
        pick_order = sem("pick_order")
        pick_ready = sem("pick_ready")
        scattered1 = sem("scattered1")
        inp_ps = sem("inp_ps")
        tap1_first = sem("tap1_first")
        conv1_done = sem("conv1_done")
        h1_ready = sem("h1_ready")
        xd_ps = sem("xd_ps")
        xd_copied = sem("xd_copied")
        dl_ps = sem("dl_ps")
        sp_ready = sem("sp_ready")
        delta_ready = sem("delta_ready")
        b_ps = sem("b_ps")
        c_ps = sem("c_ps")
        b_used = sem("b_used")
        dA_ready = sem("dA_ready")
        scanned = sem("scanned")
        yc_ready = sem("yc_ready")
        yc_used = sem("yc_used")
        yt_ready = sem("yt_ready")
        s1_ps = sem("s1_ps")
        s1_copied = sem("s1_copied")
        e1_loaded = [sem(f"e1_loaded{k}") for k in range(2)]
        moe_ps = sem("moe_ps")
        moe_out = sem("moe_out")
        y1_stored = sem("y1_stored")
        y1_gathered = sem("y1_gathered")
        out_ready = sem("out_ready")

        sp_log = sem("sp_log")
        sp_abs = sem("sp_abs")
        sp_exp = sem("sp_exp")
        res_ready = sem("res_ready")
        bc_in_ps = sem("bc_in_ps")
        bc_hi = sem("bc_hi")
        bc_rest1 = sem("bc_rest1")
        bc_mid = sem("bc_mid")
        bc_rest2 = sem("bc_rest2")
        bc_lo = sem("bc_lo")
        dh_ready = sem("dh_ready")
        c_copied = sem("c_copied")
        yc_g1_ready = sem("yc_g1_ready")
        yc_g1_own = sem("yc_g1_own")
        y_added = sem("y_added")
        N_W1 = 14
        PIECES = 12
        NCU = 3 * B
        ZEROED = 16 * (TILES_A // 4 + E * CAP // (4 * P))

        def since(eng, s, v):
            if not (isinstance(v, int) and v <= 0):
                eng.wait_ge(s, v)

        def all_rows(eng, row, start=None, end=None):
            row(0, 0, 1, [], False)
            row(1, 1, 2, [(0, 0, 0), (1, 0, 1)], True)
            if start:
                start()
            with eng.Fori(0, (B - 4) // 2) as i:
                if start:
                    start(i)
                row(i * 2 + 2, 0, i * 2 + 3, [(i * 2 + 2, i + 1, 0)], True)
                row(i * 2 + 3, 1, i * 2 + 4, [(i * 2 + 3, i + 1, 1)], True)
            if end:
                end()
            row(B - 2, 0, B - 1, [(E - 2, E // 2 - 1, 0), (E - 1, E // 2 - 1, 1)], True)
            row(B - 1, 1, None, [], False)

        def group1_done(c, n):
            if n < 0:
                return group1_done(c - 1, n + NS)
            if isinstance(c, int) and c in (0, B - 1):
                return yc_g1_own, (NS if c else 0) + n + 1
            return yc_g1_ready, (c - 1) * NS + (n + 1)

        def pieces_at(n, experts):
            seq = [(*e, p, part) for e in experts for p in range(PIECES) for part in ((0, 1) if p == 10 else (1,))]
            counts = {0: {},
                      1: {2: 1, 5: 1, 7: 1, 10: 2, 11: 3, 12: 2, 13: 1, 14: 1, 15: 1},
                      2: {2: 3, 5: 3, 7: 3, 10: 2, 11: 2, 12: 4, 13: 4, 14: 3, 15: 2}}[len(experts)]
            at = sum(v for k, v in counts.items() if k < n)
            return seq[at:at + counts.get(n, 0)], sum(u[4] for u in seq[:at])

        block = ctx.enter_context(nc.Block())

        @block.sync
        def _(sp):
            for g in range(4):
                sp.dma_start(x[:, 8 * g:8 * g + 8, :],
                             d["x"].rearrange("(i p) c -> p i c", p=P)[:, 8 * g:8 * g + 8, :]).then_inc(x_loaded, 16)
            for dst, src in ((wproj[:], "wproj"), (wlr[:], "wlr"), (wo[:], "wo"),
                             (taps[:].rearrange("p a b -> p (a b)"), "taps"), (ln_gb[:], "ln_gb"), (wrt[:], "wrt"),
                             (X[:], "state0")):
                sp.dma_start(dst, d[src]).then_inc(w_loaded, 16)
            for dst, src in ((wg_a, "wg_a"), (wu_a, "wu_a"), (wd_a, "wd_a")):
                sp.dma_start(dst[:], d[src]).then_inc(we_loaded, 16)

            def heads_load(b):
                for w, dst in ((1, K), (2, V), (0, Q)):
                    cu = 3 * b + w
                    sp.wait_ge(stored[cu % 4], 16 * (cu // 4 + 1))
                    sp.dma_start(dst[b * H:(b + 1) * H, :, :],
                                 qkv_scr[w].rearrange("(h e) (b t) -> b h e t", h=H, b=B)[b]).then_inc(heads_loaded, 16)
                sp.wait_ge(lr_stored[b % 2], 16 * (b // 2 + 1))
                sp.dma_start(LZ[b * H:(b + 1) * H, :, :],
                             lr_scr.rearrange("(h j) (b t) -> b h j t", h=H, b=B)[b]).then_inc(heads_loaded, 16)

            sp.wait_ge(xn_ready, NT)
            for cu in range(NCU):
                b, w = divmod(cu, 3)
                sp.wait_ge(silu_done, cu + 1)
                sp.dma_start(qkv_scr[w, :, b * L:(b + 1) * L], cv[:, cu % 4, :]).then_inc(stored[cu % 4], 16)
                if w == 0 and b >= 1:
                    sp.wait_ge(lr_copied, b)
                    sp.dma_start(lr_scr[:, (b - 1) * L:b * L], LR[0:2 * H, (b - 1) % 2, :]).then_inc(lr_stored[(b - 1) % 2], 16)
                if w == 2 and b >= 1:
                    heads_load(b - 1)
            sp.wait_ge(lr_copied, B)
            sp.dma_start(lr_scr[:, (B - 1) * L:B * L], LR[0:2 * H, (B - 1) % 2, :]).then_inc(lr_stored[(B - 1) % 2], 16)
            heads_load(B - 1)
            sp.wait_ge(scattered, 16 * 2 * NT)
            sp.wait_ge(norm2, 2)
            for k in range(TPS):
                sp.dma_start(xg[:, k, :], slots_x[k * P:(k + 1) * P, :]).then_inc(xg_loaded[k], 16)
            with sp.Fori(0, ROUTED_STEPS - 1) as c:
                for k in range(TPS):
                    sp.wait_ge(xg_used, c * TPS + (k + 1))
                    sp.dma_start(xg[:, k, :], slots_x[bass.ds((c + 1) * (TPS * P) + k * P, P), :]).then_inc(xg_loaded[k], 16)
                for k in range(TPS):
                    sp.wait_ge(y_copied, c * TPS + (k + 2))
                    sp.dma_start(slots_y[bass.ds(c * (TPS * P) + k * P, P), :], yg[:, k, :]).then_inc(y_stored[k], 16)
            for k in range(TPS):
                j = (ROUTED_STEPS - 1) * TPS + k
                sp.wait_ge(y_copied, j + 2)
                sp.dma_start(slots_y[j * P:(j + 1) * P, :], yg[:, k, :]).then_inc(y_stored[k], 16)
            sp.wait_ge(o_centred, 1)
            for g in range(4):
                sp.dma_start(x[:, 8 * g:8 * g + 8, :],
                             d["x"].rearrange("(i p) c -> p i c", p=P)[:, 8 * g:8 * g + 8, :]).then_inc(x_loaded, 16)
            sp.wait_ge(o_ready, 1)
            for b in range(B):
                sp.dma_start(o_scr.rearrange("(h e) (b t) -> b h e t", h=H, b=B)[b],
                             O[b * H:(b + 1) * H, :, :]).then_inc(o_stored, 16)
            sp.wait_ge(o_stored, 16 * B)
            sp.dma_start(K[:].rearrange("p a b -> p (a b)"), o_scr).then_inc(oT_loaded, 16)
            sp.wait_ge(y_copied, TILES_A + 1)
            for dst, src in ((w_inp, "w_in1"), (flat(w_x1), "w_x1"), (flat(w_bc1), "w_bc1"), (w_dt1[0:DTR, :], "w_dt1"), (flat(w_o1), "w_o1"),
                             (flat(conv_w1), "conv_w1"), (conv_b1, "conv_b1"), (dt_b1, "dt_b1"), (d_1, "d_1"),
                             (flat(a_neg), "a_log"), (w_rt1, "w_rt1"), (b_rt1, "b_rt1"), (flat(b_e1), "b_e1"),
                             (b_e2[0:1, :], "b_e2")):
                src = d[src].partition_broadcast(P).rearrange("p o e -> p (o e)") if src == "b_rt1" else d[src]
                sp.dma_start(dst, src).then_inc(w1_loaded, 16)

            def expert_loads(e, k):
                sp.dma_start(w_e1[k], d["w_e1"][bass.ds(e * P, P), :]).then_inc(e1_loaded[k], 16)
                sp.dma_start(flat(w_e2[k]), d["w_e2"][:, bass.ds(e * FC * D, FC * D)]).then_inc(e1_loaded[k], 16)
                sp.dma_start(xg1[k], slots_x1[bass.ds(e * CAP, CAP), :].rearrange("(i p) c -> p i c", p=P)).then_inc(e1_loaded[k], 16)

            def expert_store(e):
                sp.wait_ge(moe_out, e * PIECES + PIECES)
                sp.dma_start(slots_y1[bass.ds(e * CAP, CAP), :].rearrange("(i p) c -> p i c", p=P), yg1).then_inc(y1_stored, 16)

            sp.wait_ge(scattered1, 16 * 2 * NT)
            for k in range(2):
                expert_loads(k, k)
            with sp.Fori(0, E // 2 - 1) as i:
                for k in range(2):
                    expert_store(i * 2 + k)
                    expert_loads(i * 2 + (k + 2), k)
            for k in range(2):
                expert_store(E - 2 + k)
            for g in range(G4):
                sp.wait_ge(out_ready, g + 1)
                sp.dma_start(d["out"].rearrange("(i p) c -> p i c", p=P)[:, 4 * g:4 * g + 4, :], x[:, 4 * g:4 * g + 4, :]).then_inc(out_stored, 16)
            sp.wait_ge(out_stored, 16 * G4)

        @block.gpsimd
        def _(pool):
            o = Order(pool, pool_order)
            o.mark(pool.memset(ident[:], 0.0))
            o.mark(pool.memset(ones[:], 1.0))
            o.mark(pool.memset(zero, 0.0))
            o.mark(pool.memset(first_of_e[:], 1.0))
            o.link(pool.memset(seg[:], 1.0))
            pool.affine_select(out=ident[:], in_=ident[:], compare_op=ALU.not_equal, fill=1.0, base=0,
                               pattern=[[-1, P]], channel_multiplier=1).then_inc(consts_ready, 1)
            pool.affine_select(out=upper[:], in_=ones[:], compare_op=ALU.is_ge, fill=0.0, base=0,
                               pattern=[[1, P]], channel_multiplier=-1).then_inc(consts_ready, 1)
            pool.iota(iota_e[:], [[1, E]], base=0, channel_multiplier=0,
                      allow_small_or_imprecise_dtypes=True).then_inc(consts_ready, 1)
            pool.iota(iota_t[:], [[1, TILES_A]], base=0, channel_multiplier=0,
                      allow_small_or_imprecise_dtypes=True).then_inc(consts_ready, 1)
            pool.memset(first_of_e[:, :, 0], 0.0).then_inc(consts_ready, 1)
            pool.memset(seg[:, :, 0], 0.0).then_inc(consts_ready, 1)
            for r in range(TILES_A // 4):
                pool.dma_start(slots_x[r * 4 * P:(r + 1) * 4 * P, :].rearrange("(p i) c -> p (i c)", p=P),
                               zero).then_inc(zeroed, 16)
            for r in range(E * CAP // (4 * P)):
                pool.dma_start(slots_x1[r * 4 * P:(r + 1) * 4 * P, :].rearrange("(p i) c -> p (i c)", p=P),
                               zero).then_inc(zeroed, 16)
            pool.wait_ge(zeroed, ZEROED)
            pool.wait_ge(slots_ready, 1)
            pool.wait_ge(xn_ready, NT)
            def scatter(lo, hi):
                for i in range(lo, hi):
                    for j in range(2):
                        pool.indirect_dma_start(out=slots_x, out_offset=bass.IndirectOffsetOnAxis(ap=sl_put[:, j, i:i + 1], axis=0),
                                                in_=xn[:, i, :], in_offset=None).then_inc(scattered, 16)

            tiles_before = NT // 2 - 2
            scatter(0, tiles_before)

            def q_products(c):
                ts = bass.ds(c * CH, CH)
                pool.wait_ge(state_ready, c + 1)
                pool.tensor_tensor(PQ, bc(Q[:, :, ts].rearrange("p d l -> p l d"), 1, DI),
                                   bc(w_in.rearrange("p (D d) -> p D d", D=DI), 2, CH), ALU.mult).then_inc(pq_ready, 1)

            def o_products(c):
                pool.wait_ge(qh_ready, c + 1)
                pool.wait_ge(o_ps, c + 1)
                pool.tensor_tensor(OP, bc(EQ.rearrange("p D l -> p l D"), 1, HD),
                                   CS.rearrange("p (D d) l -> p d l D", D=DI)[:, :, 1:CH + 1, :], ALU.mult).then_inc(op_ready, 1)

            for c in range(FIRST):
                q_products(c)
                scatter(tiles_before + (NT - tiles_before) * c // FIRST, tiles_before + (NT - tiles_before) * (c + 1) // FIRST)
                o_products(c)
            with pool.Fori(FIRST, AFTER) as c:
                q_products(c)
                o_products(c)
            def gather(lo, hi):
                for i in range(lo, hi):
                    for j, dst in enumerate((xn[:], xnT[:].rearrange("p (i c) -> p i c", c=D))):
                        pool.indirect_dma_start(out=dst[:, i, :], out_offset=None, in_=slots_y,
                                                in_offset=bass.IndirectOffsetOnAxis(ap=sl_put[:, j, i:i + 1], axis=0)
                                                ).then_inc(y_gathered, 16)

            beside = 5
            for c in range(AFTER, NCH):
                q_products(c)
                if c == AFTER:
                    for k in range(TPS):
                        pool.wait_ge(y_stored[k], 16 * (ROUTED_STEPS + 1))
                gather(beside * (c - AFTER), beside * (c + 1 - AFTER))
                o_products(c)
            gather(beside * (NCH - AFTER), NT)
            pool.wait_ge(oT_ready, 1)
            pool.wait_ge(y_gathered, 16 * 2 * NT)
            pool.memset(pick_wide, 0.0).then_inc(pick_order, 1)
            for i in range(3):
                pool.wait_ge(pick_order, i + 1)
                part = pick_wide[2 * NS * i:2 * NS * (i + 1)]
                pool.affine_select(out=part, in_=part, compare_op=ALU.not_equal, fill=1.0, base=0,
                                   pattern=[[-1, 2 * NS], [0, P]], channel_multiplier=1).then_inc(pick_order, 1)
            pool.wait_ge(pick_order, 4)
            pool.wait_ge(slots_ready, 2)
            pool.wait_ge(xn_ready, 2 * NT)
            for i in range(NT):
                for j in range(2):
                    pool.indirect_dma_start(out=slots_x1, out_offset=bass.IndirectOffsetOnAxis(ap=sl_put[:, j, i:i + 1], axis=0),
                                            in_=xn[:, i, :], in_offset=None, bounds_check=E * CAP - 1,
                                            oob_is_err=False).then_inc(scattered1, 16)
            def delta_sum(r, s, g):
                pool.wait_ge(sp_log, r * GD + (g + 1))
                pool.tensor_tensor(del1[s][:, g, :], del1[s][:, g, :], sp1[:, g, :], ALU.add).then_inc(delta_ready, 1)

            def delta_h(r, s, g):
                pool.wait_ge(delta_ready, r * GD + (g + 1))
                pool.tensor_tensor(dh1[s][:, g, :], del1[s][:, g, :], h1[s][:, g, :], ALU.mult).then_inc(dh_ready, 1)

            def row(c, s, nxt, experts, shared):
                if not shared:
                    return
                for n in range(NS):
                    pool.wait_ge(scanned, c * (GD * NS) + (GD * n + 2))
                    pool.wait_ge(c_copied, (c - 1) * NS + (n + 1))
                    since(pool, y_added, (c - 1) * (NS - 1) + max(n - 2, 0))
                    y = y_sum[s] if n == 0 else yc_g1[:, n % 2, :]
                    pool.tensor_tensor(y, st_g1[:, n % 2, :], c_row[:, n % 2, :], ALU.mult).then_inc(yc_g1_ready, 1)
                    if n >= 1:
                        pool.wait_ge(yc_g1_ready, (c - 1) * NS + (n + 1))
                        since(pool, y_added, (c - 1) * (NS - 1) + (n - 1))
                        pool.tensor_tensor(y_sum[s], y_sum[s], y, ALU.add).then_inc(y_added, 1)
                    if n in (11, 12):
                        delta_sum(nxt, 1 - s, n - 11)
                    if n in (13, 14):
                        delta_h(nxt, 1 - s, n - 13)

            all_rows(pool, row)
            pool.wait_ge(y1_stored, 16 * (E + 1))
            pool.wait_ge(inp_ps, B * 2 * GD)
            for i in range(NT):
                for j, dst in enumerate((xn[:], xnT[:].rearrange("p (i c) -> p i c", c=D))):
                    pool.indirect_dma_start(out=dst[:, i, :], out_offset=None, in_=slots_y1,
                                            in_offset=bass.IndirectOffsetOnAxis(ap=sl_get[:, j, i:i + 1], axis=0)
                                            ).then_inc(y1_gathered, 16)

        @block.tensor
        def _(pe):
            pe.wait_ge(consts_ready, 6)

            def transposes(layer):
                for g in range(G4):
                    n = layer * G4 + g
                    if n >= 2:
                        pe.wait_ge(xnT_copied, n - 1)
                    for j in range(4):
                        i = 4 * g + j
                        pe.wait_ge(xn_ready, layer * NT + i + 1)
                        t = pe.transpose(ps[:, g % 2, j * P:(j + 1) * P], xn[:, i, :], ident[:])
                    t.then_inc(xnT_ps, 1)

            def router(layer, w):
                pe.wait_ge(xnT_copied, (layer + 1) * G4)
                for i in range(NT):
                    m = pe.matmul(ps[:, 0, i * E:(i + 1) * E], xnT[:, i * P:(i + 1) * P], w, start=True, stop=True)
                m.then_inc(logits_ps, 1)
                pe.wait_ge(mask_ready, layer + 1)
                mk = mask.rearrange("p i e -> p (i e)")
                pe.matmul(ps[:, 1, 0:NT * E], upper[:], mk, start=True, stop=True).then_inc(ranks_ps, 1)
                pe.matmul(ps[:, 0, 0:NT * E], ones[:], mk, start=True, stop=True).then_inc(ranks_ps, 1)

            transposes(0)
            pe.wait_ge(w_loaded, 16 * 7)
            for b in range(B):
                rhs = xnT[:, b * L:(b + 1) * L]
                pe.wait_ge(xnT_copied, b + 1)
                for w in range(3):
                    cu = 3 * b + w
                    if cu >= 4:
                        pe.wait_ge(conv_done, cu - 3)
                    pe.matmul(ps[:, 2 + cu % 4, :], wproj[:, w * P:(w + 1) * P], rhs, start=True, stop=True).then_inc(proj_ps, 1)
                if b >= 1:
                    pe.wait_ge(gate_copied, b)
                    pe.wait_ge(lr_copied, b)
                pe.matmul(ps[:, 6, :], wproj[:, 3 * P:4 * P], rhs, start=True, stop=True).then_inc(gate_ps, 1)
                pe.matmul(ps[0:2 * H, 7, :], wlr[:], rhs, start=True, stop=True).then_inc(lr_ps, 1)
            router(0, wrt[:])
            pe.wait_ge(slots_ready, 1)
            pe.wait_ge(we_loaded, 16 * 3)
            def up(c, k):
                n0 = c * TPS - FIRST * TPS
                off = pe.value_load(texp_i[0:1, bass.ds(n0 + k, 1)], min_val=0, max_val=(E - 1) * F)
                pe.wait_ge(xg_loaded[k], c * 16 - (FIRST - 1) * 16)
                pe.transpose(ps[:, 0, 0:P], xg[:, k, :], ident[:]).then_inc(xg_used, 1)
                pe.wait_ge(xgT_copied, n0 + (k + 1))
                if k == 2:
                    pe.wait_ge(hid_ready, n0 + 1)
                if k == 0 and not (isinstance(c, int) and c == FIRST):
                    pe.wait_ge(hid_ready, n0)
                pe.matmul(ps[:, 1 + 2 * (k % 2), :], xgT[:, k, :], wg_a[:, bass.ds(off, F)], start=True, stop=True).then_inc(gu_ps, 1)
                pe.matmul(ps[:, 2 + 2 * (k % 2), :], xgT[:, k, :], wu_a[:, bass.ds(off, F)], start=True, stop=True).then_inc(gu_ps, 1)

            def down(c, k, between=None):
                n0 = c * TPS - FIRST * TPS
                off = pe.value_load(texp_i[0:1, bass.ds(n0 + k, 1)], min_val=0, max_val=(E - 1) * F)
                pe.wait_ge(hid_ready, n0 + (k + 1))
                if k >= 1:
                    pe.wait_ge(hidT_copied, n0 + k)
                for f in range(FC):
                    t = pe.transpose(ps[:, 5, f * P:(f + 1) * P], hid[:, k, f * P:(f + 1) * P], ident[:])
                t.then_inc(hidT_ps, 1)
                if between:
                    between()
                pe.wait_ge(hidT_copied, n0 + (k + 1))
                pe.wait_ge(y_copied, n0 + (k + 1))
                for f in range(FC):
                    m = pe.matmul(ps[:, 6, 0:D], hidT[:, k % 2, f * P:(f + 1) * P],
                                  wd_a[:, bass.ds(off + f * D, D)], start=(f == 0), stop=(f == FC - 1))
                m.then_inc(y_ps, 1)

            def q_sums(c):
                pe.wait_ge(pq_ready, c + 1)
                pe.wait_ge(o_copied, c + 1)
                for e in range(HD):
                    m = pe.matmul(ps[:, 7, 0:DI * CH], ident[:], PQ[:, :, :, e], start=(e == 0), stop=(e == HD - 1))
                m.then_inc(q_ps, 1)

            def o_sums(c):
                pe.wait_ge(op_ready, c + 2)
                for r in range(DI):
                    m = pe.matmul(ps[:, 7, 0:HD * CH], ident[:], OP[:, :, :, r], start=(r == 0), stop=(r == DI - 1))
                m.then_inc(o_ps, 1)

            def step(c, routed, before):
                if routed:
                    up(c, 0)
                if before >= 1:
                    o_sums(c - 1)
                if before >= 2:
                    down(c - 1, 2, lambda: q_sums(c))
                else:
                    q_sums(c)
                if routed:
                    up(c, 1)
                    down(c, 0)
                    up(c, 2)
                    down(c, 1)

            step(0, False, 0)
            with pe.Fori(1, FIRST) as c:
                step(c, False, 1)
            step(FIRST, True, 1)
            with pe.Fori(FIRST + 1, AFTER) as c:
                step(c, True, 2)
            step(AFTER, False, 2)
            with pe.Fori(AFTER + 1, NCH) as c:
                step(c, False, 1)
            o_sums(NCH - 1)
            pe.wait_ge(oT_ready, 1)
            oT = K[:].rearrange("p a b -> p (a b)")
            for g in range(G4):
                if g >= 2:
                    pe.wait_ge(s_used, g - 1)
                for j in range(4):
                    i = 4 * g + j
                    m = pe.matmul(ps[:, 1 + g % 2, j * P:(j + 1) * P], oT[:, i * P:(i + 1) * P], wo[:], start=True, stop=True)
                m.then_inc(s_ps, 1)

            transposes(1)
            pe.wait_ge(w1_loaded, 16 * N_W1)
            router(1, w_rt1)
            pe.wait_ge(slots_ready, 2)
            pe.wait_ge(pick_ready, 1)

            def piece(c, half, k, p, part):
                if p == 0:
                    pe.wait_ge(e1_loaded[k], half * 48 + 48)
                if p != 10 or part == 0:
                    since(pe, moe_out, c * PIECES + (2 if p == 2 else 10 if p >= 10 else p - 1))
                bank = ps[:, 6 + p % 2, :]
                if p < 2:
                    for i in range(4 * p, min(4 * p + 4, CT)):
                        m = pe.transpose(bank[:, (i % 4) * P:(i % 4 + 1) * P], xg1[k][:, i, :], ident[:])
                elif p < 10:
                    f, half = divmod(p - 2, 2)
                    m = pe.matmul(bank[:, 0:CAP // 2], w_e1[k][:, f * P:(f + 1) * P],
                                  xgT1[:, half * (CAP // 2):(half + 1) * (CAP // 2)], start=True, stop=True)
                else:
                    for i in ((0, 1) if part == 0 else (2, 3)) if p == 10 else range(4, CT):
                        o_ = bank[:, (i % 4) * D:(i % 4 + 1) * D]
                        for f in range(FC):
                            pe.matmul(o_, hid1[:, f, i * P:(i + 1) * P], w_e2[k][:, f, :], start=(f == 0), stop=False)
                        m = pe.matmul(o_, ones[0:1, :], b_e2[0:1, bass.ds(c * D, D)], start=False, stop=True)
                if part:
                    m.then_inc(moe_ps, 1)

            def inner(r, g):
                pe.matmul(ps[:, (6, 7, 7, 6)[g], :], w_inp[:, g * P:(g + 1) * P], xnT[:, bass.ds(r * L, L)], start=True, stop=True).then_inc(inp_ps, 1)

            def low_rank(r, s):
                pe.wait_ge(h1_ready, r * GD + GD)
                for g in range(GD):
                    m = pe.matmul(ps[0:DTR, 6, :], w_x1[:, g, :], h1[s][:, g, :], start=(g == 0), stop=(g == GD - 1))
                m.then_inc(xd_ps, 1)

            def b_and_c(r, s):
                for g in range(GD):
                    m = pe.matmul(ps[0:3 * 2 * NS, 7, :], w_bc1[:, g, :], h1[s][:, g, :], start=(g == 0), stop=(g == GD - 1))
                m.then_inc(bc_in_ps, 1)

            def delta(r, g):
                pe.matmul(ps[:, 7 - g, :], w_dt1[0:DTR, g * P:(g + 1) * P], xd1[0:DTR, :], start=True, stop=True).then_inc(dl_ps, 1)

            def spread(c, s, n, both):
                if n == 0:
                    pe.wait_ge(bc_lo, c + 1)
                since(pe, b_used, c * NS + (n - 1))
                pe.matmul(ps[:, 2 + n % 2, :], pick[:, n, :], bc_parts[s], start=True, stop=True).then_inc(b_ps, 1)
                since(pe, yc_ready, c * NS + (n - 1))
                if both:
                    pe.wait_ge(*group1_done(c, n - 2))
                pe.matmul(ps[:, n % 2, :], pick[:, NS + n, :], bc_parts[s], start=True, stop=True).then_inc(c_ps, 1)

            def accumulate(c, n):
                if n == 0 and not (isinstance(c, int) and c == 0):
                    pe.wait_ge(s1_copied, c)
                shared = not (isinstance(c, int) and c in (0, B - 1))
                pe.wait_ge(yc_ready, c * NS + (n + 1))
                m = pe.matmul(ps[:, 4, :], ident[:], yc_g0[:, n % 2, :], start=(n == 0), stop=(n == NS - 1))
                if shared:
                    m.then_inc(yc_used, 2)
                    return
                m.then_inc(yc_used, 1)
                pe.wait_ge(*group1_done(c, n))
                pe.matmul(ps[:, 5, :], ident[:], yc_g1[:, n % 2, :], start=(n == 0), stop=(n == NS - 1)).then_inc(yc_used, 1)

            def out_proj(c, s):
                pe.wait_ge(yt_ready, c * GD + GD)
                for j in range(4):
                    for g in range(GD):
                        m = pe.matmul(ps[:, 4, j * D:(j + 1) * D], h1[s][:, g, j * P:(j + 1) * P], w_o1[:, g, :], start=(g == 0), stop=(g == GD - 1))
                m.then_inc(s1_ps, 1)

            def row(c, s, nxt, experts, shared):
                first = isinstance(c, int) and c == 0
                t = 1 - s
                second = isinstance(c, int) and c == 1
                for n in range(NS):
                    if n < NS - 1:
                        spread(c, s, n + 1, n >= 1 and not shared or n == 0 and second)
                    elif nxt is not None:
                        spread(nxt, t, 0, not shared)
                    if n >= 1:
                        if n == 1 and not first:
                            out_proj(c - 1, t)
                        accumulate(c, n - 1)
                    elif not first:
                        accumulate(c - 1, NS - 1)
                    now, at = pieces_at(n, experts)
                    out = experts[0][0] * PIECES + at if experts else 0
                    frees = ()
                    if nxt is not None:
                        if n == 0:
                            pe.wait_ge(sp_ready, nxt * GD)
                            since(pe, moe_out, out)
                            inner(nxt, 0)
                            inner(nxt, 1)
                        if n == 2:
                            frees = ((conv1_done, nxt * GD + 1), (conv1_done, nxt * GD + 2))
                        if n == 3:
                            pe.wait_ge(conv1_done, nxt * GD + 2)
                            since(pe, moe_out, out - 1)
                            inner(nxt, 2)
                            since(pe, moe_out, out)
                            inner(nxt, 3)
                        if n == 5:
                            frees = ((res_ready, nxt * GD + 1), (res_ready, nxt * GD + 2))
                        if n == 7:
                            frees = ((xd_copied, nxt + 1), (bc_rest1, nxt + 1))
                        if n == 6:
                            pe.wait_ge(res_ready, nxt * GD + 1)
                            since(pe, moe_out, out)
                            b_and_c(nxt, t)
                        if n == 8:
                            pe.wait_ge(bc_rest1, nxt + 1)
                            pe.wait_ge(xd_copied, nxt + 1)
                            since(pe, moe_out, out - 1)
                            delta(nxt, 0)
                            since(pe, moe_out, out)
                            delta(nxt, 1)
                        if n == 10:
                            frees = ((sp_ready, nxt * GD + 1), (sp_ready, nxt * GD + 2))
                    for i, unit in enumerate(now):
                        if i < len(frees):
                            pe.wait_ge(*frees[i])
                        piece(*unit)
                    if nxt is not None and n == 5:
                        pe.wait_ge(res_ready, nxt * GD + 2)
                        since(pe, moe_out, out + len(now) - 1)
                        low_rank(nxt, t)

            inner(0, 0)
            inner(0, 1)
            pe.wait_ge(conv1_done, 2)
            inner(0, 2)
            inner(0, 3)
            pe.wait_ge(res_ready, 2)
            low_rank(0, 0)
            b_and_c(0, 0)
            pe.wait_ge(xd_copied, 1)
            pe.wait_ge(bc_rest1, 1)
            delta(0, 0)
            delta(0, 1)
            spread(0, 0, 0, False)
            all_rows(pe, row)
            accumulate(B - 1, NS - 1)
            out_proj(B - 1, 1)

        @block.scalar
        def _(act):
            o = Order(act, act_order)
            for s in (y_copied, o_copied, o_ps, op_ready):
                act.sem_inc(s, 1)
            for s in (*y_stored, y1_stored):
                act.sem_inc(s, 16)
            act.wait_ge(ln_var, 1)
            act.activation(rstd[:], rstd[:], ACT.Sqrt).then_inc(ln_std, 1)
            for g in range(G4):
                act.wait_ge(xnT_ps, g + 1)
                act.activation(xnT[:, g * 512:(g + 1) * 512], ps[:, g % 2, :], ACT.Copy).then_inc(xnT_copied, 1)

            def silu(cu):
                act.wait_ge(conv_done, cu + 1)
                act.activation(cv[:, cu % 4, :], cv[:, cu % 4, :], ACT.Silu).then_inc(silu_done, 1)

            act.wait_ge(taps_ready, 1)
            for cu in range(NCU):
                b, w = divmod(cu, 3)
                act.wait_ge(proj_ps, cu + 1)
                if cu >= 4:
                    act.wait_ge(stored[cu % 4], 16 * (cu // 4))
                act.activation(cv[:, cu % 4, :], ps[:, 2 + cu % 4, :], ACT.Copy, scale=taps[:, w, 3:4]).then_inc(tap_first, 1)
                if cu >= 1:
                    silu(cu - 1)
                if w == 2:
                    act.wait_ge(gate_ps, b + 1)
                    act.activation(gateT[:, b * L:(b + 1) * L], ps[:, 6, :], ACT.Copy).then_inc(gate_copied, 1)
                    act.wait_ge(lr_ps, b + 1)
                    if b >= 2:
                        act.wait_ge(lr_stored[b % 2], 16 * (b // 2))
                    act.activation(LR[0:2 * H, b % 2, :], ps[0:2 * H, 7, :], ACT.Copy).then_inc(lr_copied, 1)
            silu(NCU - 1)
            act.wait_ge(logits_ready, 1)
            act.activation(lg, lg, ACT.Exp).then_inc(probs_ready, 1)
            act.wait_ge(heads_loaded, 16 * 4 * B)
            act.wait_ge(logits_ps, 1)
            for n, t in enumerate((K, Q)):
                if n == 1:
                    act.wait_ge(norm2, 1)
                act.activation(TMP, t[:], ACT.Square).then_inc(squared, 1)
            for n in range(2):
                act.wait_ge(norm2, n + 1)
                act.activation(nrm[:, n, :], nrm[:, n, :], ACT.Sqrt).then_inc(norm_root, 1)
            act.wait_ge(lr_in, 1)
            o.link(act.activation(LR[:], LZ, ACT.Abs))
            o.link(act.activation(LR[:], LR[:], ACT.Exp, scale=-1.0))
            act.activation(LR[:], LR[:], ACT.Ln, bias=1.0).then_inc(lr_log, 1)
            act.preload_act_table(ACT.Tanh)

            temper = HD ** -0.5

            def xT(c, k):
                act.wait_ge(xg_used, c * TPS - (FIRST * TPS - k - 1))
                act.activation(xgT[:, k, :], ps[:, 0, 0:P], ACT.Copy).then_inc(xgT_copied, 1)

            def tanh(c, k):
                act.wait_ge(gu_ps, c * (2 * TPS) - (FIRST * 2 * TPS - 2 * k - 1))
                act.activation(th[:, k, :], ps[:, 1 + 2 * (k % 2), :], ACT.Tanh, scale=0.5).then_inc(tanh_done, 1)

            def hT(c, k):
                act.wait_ge(hidT_ps, c * TPS - (FIRST * TPS - k - 1))
                if k == 2:
                    act.wait_ge(y_ps, c * TPS - (FIRST * TPS - 1))
                act.activation(hidT[:, k % 2, :], ps[:, 5, :], ACT.Copy).then_inc(hidT_copied, 1)

            def y(c, k):
                act.wait_ge(y_ps, c * TPS - (FIRST * TPS - k - 1))
                act.wait_ge(y_stored[k], c * 16 - (FIRST - 1) * 16)
                act.activation(yg[:, k, :], ps[:, 6, 0:D], ACT.Copy, scale=0.5).then_inc(y_copied, 1)

            def o_copy(c):
                act.wait_ge(o_ps, c + 2)
                act.activation(O[:, :, bass.ds(c * CH, CH)], ps[:, 7, 0:HD * CH].rearrange("p (d l) -> p d l", d=HD), ACT.Copy).then_inc(o_copied, 1)

            def step(c, routed, before):
                def exp(t, ready, done, scale=1.0):
                    act.wait_ge(ready, c + 1)
                    act.activation(t, t, ACT.Exp, scale=scale).then_inc(done, 1)

                if routed:
                    xT(c, 0)
                exp(EK, rec_k, exp_k)
                exp(EB, rec_b, exp_b, temper)
                if routed:
                    tanh(c, 0)
                if before >= 1:
                    o_copy(c - 1)
                if before >= 2:
                    hT(c - 1, 2)
                    y(c - 1, 2)
                if routed:
                    xT(c, 1)
                exp(EA, rec_a, exp_a, temper)
                if routed:
                    tanh(c, 1)
                if routed:
                    hT(c, 0)
                exp(EC, rec_c, exp_c, temper)
                exp(EQ, rec_q, exp_q)
                if routed:
                    y(c, 0)
                    xT(c, 2)
                    tanh(c, 2)
                exp(ED, rec_d, exp_d, temper)
                if routed:
                    hT(c, 1)
                    y(c, 1)

            step(0, False, 0)
            with act.Fori(1, FIRST) as c:
                step(c, False, 1)
            step(FIRST, True, 1)
            with act.Fori(FIRST + 1, AFTER) as c:
                step(c, True, 2)
            step(AFTER, False, 2)
            with act.Fori(AFTER + 1, NCH) as c:
                step(c, False, 1)
            o_copy(NCH - 1)
            act.wait_ge(o_centred, 1)
            for k in range(TPS):
                act.wait_ge(y_stored[k], 16 * (ROUTED_STEPS + 1))
            act.activation(V[:], O[:], ACT.Square).then_inc(o_squared, 1)
            act.wait_ge(o_var, 1)
            act.activation(nrm[:, 0, :], nrm[:, 0, :], ACT.Sqrt).then_inc(o_root, 1)
            for g in range(G4):
                act.wait_ge(mix_ready, g + 1)
                v = flat(xn[:])[:, g * 512:(g + 1) * 512]
                act.activation(v, v, ACT.Silu).then_inc(mix_silu, 1)

            act.wait_ge(w1_loaded, 16 * N_W1)
            act.wait_ge(ln_var, 2)
            act.activation(rstd[:], rstd[:], ACT.Sqrt).then_inc(ln_std, 1)
            for g in range(G4):
                act.wait_ge(xnT_ps, G4 + g + 1)
                act.activation(xnT[:, g * 512:(g + 1) * 512], ps[:, g % 2, :], ACT.Copy).then_inc(xnT_copied, 1)
            o.link(act.activation(a_neg, a_neg, ACT.Exp))
            o.link(act.activation(a_neg, a_neg, ACT.Copy, scale=-1.0))
            act.wait_ge(logits_ready, 2)
            act.activation(lg, lg, ACT.Exp).then_inc(probs_ready, 1)

            def piece(c, p):
                if p == 0:
                    since(act, moe_out, c * PIECES)
                    o.mark(act.activation(b_e1_now[:], b_e1[:, bass.ds(c, 1), :].rearrange("p a b -> p (a b)"), ACT.Copy))
                if p == 2:
                    o.wait()
                act.wait_ge(moe_ps, c * PIECES + (p + 1))
                bank = ps[:, 6 + p % 2, :]
                if p < 2:
                    w = min(4, CT - 4 * p) * P
                    i = act.activation(xgT1[:, 4 * p * P:4 * p * P + w], bank[:, 0:w], ACT.Copy)
                elif p < 10:
                    f, half = divmod(p - 2, 2)
                    i = act.activation(hid1[:, f, half * (CAP // 2):(half + 1) * (CAP // 2)], bank[:, 0:CAP // 2], ACT.Relu,
                                       bias=b_e1_now[:, f:f + 1])
                else:
                    w = min(4, CT - 4 * (p - 10))
                    if p == 10:
                        act.wait_ge(y1_stored, c * 16 + 16)
                    i = act.activation(yg1[:, 4 * (p - 10):4 * (p - 10) + w, :], bank[:, 0:w * D].rearrange("p (i c) -> p i c", c=D), ACT.Copy)
                i.then_inc(moe_out, 1)

            act.wait_ge(pick_order, 4)
            act.activation(pick, pick_wide, ACT.Copy).then_inc(pick_ready, 1)

            def taps1(r, s):
                for g in range(GD):
                    act.wait_ge(inp_ps, r * (2 * GD) + (g + 1))
                    act.activation(h1[s][:, g, :], ps[:, 6 + g, :], ACT.Identity, scale=conv_w1[:, g, 3:4], bias=conv_b1[:, g:g + 1]).then_inc(tap1_first, 1)

            def silus(r, s):
                for g in range(GD):
                    act.wait_ge(inp_ps, r * (2 * GD) + (GD + g + 1))
                    act.activation(res1[s][:, g, :], ps[:, 7 - g, :], ACT.Silu).then_inc(res_ready, 1)
                for g in range(GD):
                    act.wait_ge(conv1_done, r * GD + (g + 1))
                    act.activation(h1[s][:, g, :], h1[s][:, g, :], ACT.Silu).then_inc(h1_ready, 1)

            def xd_copy(r, s):
                act.wait_ge(xd_ps, r + 1)
                act.activation(xd1[0:DTR, :], ps[0:DTR, 6, :], ACT.Copy).then_inc(xd_copied, 1)

            def part_hi(r, s):
                act.wait_ge(bc_in_ps, r + 1)
                act.activation(bc_parts[s], ps[0:3 * 2 * NS, 7, :], ACT.Copy).then_inc(bc_hi, 1)

            def part_mid(r, s):
                act.wait_ge(bc_rest1, r + 1)
                act.activation(bc_parts[s][0:2 * 2 * NS], bc_rest[0:2 * 2 * NS, :], ACT.Copy).then_inc(bc_mid, 1)

            def part_lo(r, s):
                act.wait_ge(bc_rest2, r + 1)
                act.activation(bc_parts[s][0:2 * NS], bc_rest[0:2 * NS, :], ACT.Copy).then_inc(bc_lo, 1)

            def softplus_parts(r, s):
                for g in range(GD):
                    act.wait_ge(dl_ps, r * GD + (g + 1))
                    act.activation(sp1[:, g, :], ps[:, 7 - g, :], ACT.Abs, bias=dt_b1[:, g:g + 1]).then_inc(sp_abs, 1)
                    act.activation(del1[s][:, g, :], ps[:, 7 - g, :], ACT.Relu, bias=dt_b1[:, g:g + 1]).then_inc(sp_ready, 1)

            def softplus_exp(r, s):
                for g in range(GD):
                    act.wait_ge(sp_abs, r * GD + (g + 1))
                    act.activation(sp1[:, g, :], sp1[:, g, :], ACT.Exp, scale=-1.0).then_inc(sp_exp, 1)

            def softplus_log(r, s):
                for g in range(GD):
                    act.wait_ge(sp_exp, r * GD + (g + 1))
                    act.activation(sp1[:, g, :], sp1[:, g, :], ACT.Ln, bias=1.0).then_inc(sp_log, 1)

            def decays(c, s, n):
                if n == 0:
                    act.wait_ge(delta_ready, c * GD + GD)
                for g in range(GD):
                    k = GD * n + g
                    since(act, scanned, c * (GD * NS) + (k - 7))
                    act.activation(dA(k), del1[s][:, g, :], ACT.Exp, scale=a_neg[:, g, n:n + 1]).then_inc(dA_ready, 1)

            def row(c, s, nxt, experts, shared):
                t = 1 - s
                for n in range(NS):
                    if n + 2 < NS:
                        decays(c, s, n + 2)
                    elif nxt is not None:
                        decays(nxt, t, n + 2 - NS)
                    if shared:
                        act.wait_ge(c_ps, c * NS + (n + 1))
                        since(act, yc_g1_ready, (c - 1) * NS + (n - 1))
                        act.activation(c_row[:, n % 2, :], ps[:, n % 2, :], ACT.Copy).then_inc(c_copied, 1)
                    if n == 1 and not (isinstance(c, int) and c == 0):
                        s1_copy(c - 1)
                    if nxt is not None:
                        if n == 1:
                            taps1(nxt, t)
                        if n == 4:
                            silus(nxt, t)
                        if n == 6:
                            xd_copy(nxt, t)
                        if n == 7:
                            part_hi(nxt, t)
                        if n == 8:
                            part_mid(nxt, t)
                        if n == 9:
                            part_lo(nxt, t)
                            softplus_parts(nxt, t)
                        if n == 10:
                            softplus_exp(nxt, t)
                            softplus_log(nxt, t)
                    for e, _half, _k, p, whole in pieces_at(n, experts)[0]:
                        if whole:
                            piece(e, p)

            def s1_copy(c):
                act.wait_ge(s1_ps, c + 1)
                act.activation(s1[:, bass.ds(c * L, L)], ps[:, 4, :], ACT.Copy).then_inc(s1_copied, 1)

            taps1(0, 0)
            silus(0, 0)
            xd_copy(0, 0)
            part_hi(0, 0)
            part_mid(0, 0)
            part_lo(0, 0)
            softplus_parts(0, 0)
            softplus_exp(0, 0)
            softplus_log(0, 0)
            decays(0, 0, 0)
            decays(0, 0, 1)
            PER_B = 2
            base = 0

            def pairs(i=None):
                nonlocal base
                if i is None:
                    base = o.total()
                else:
                    o.loop(i, base, PER_B)

            all_rows(act, row, pairs, lambda: o.end(base, PER_B, (B - 4) // 2))
            s1_copy(B - 1)
            for g in range(G4):
                act.wait_ge(mix_ready, G4 + g + 1)
                v = flat(xn[:])[:, g * 512:(g + 1) * 512]
                act.activation(v, v, ACT.Silu).then_inc(mix_silu, 1)

        @block.vector
        def _(dve):
            o = Order(dve, dve_order)
            tt = dve.tensor_tensor

            def layernorm(layer):
                for i in range(NT):
                    o.mark(dve.bn_stats(stats[:, i, :], x[:, i, :]))
                o.wait()
                for i in range(NT):
                    o.mark(dve.bn_aggr(mv[:, i, :], stats[:, i, :]))
                o.wait()
                dve.tensor_scalar_add(rstd[:], mv[:, :, 1], EPS).then_inc(ln_var, 1)
                dve.wait_ge(ln_std, layer + 1)
                o.link(dve.reciprocal(rstd[:], rstd[:]))
                for i in range(NT):
                    dve.tensor_scalar(xn[:, i, :], x[:, i, :], mv[:, i, 0:1], rstd[:, i:i + 1], ALU.subtract, ALU.mult).then_inc(xn_ready, 1)

            def dispatch(layer):
                lgf = ps[:, 0, 0:NT * E].rearrange("p (i e) -> p i e", e=E)
                dve.wait_ge(logits_ps, layer + 1)
                if layer == 0:
                    o.link(dve.tensor_copy(lg, lgf))
                else:
                    o.link(tt(lg, lgf, bc(b_rt1, 1, NT), ALU.add))
                o.link(dve.tensor_reduce(lmx[:], lg, AX_X, ALU.max))
                tt(lg, lg, bc(lmx[:], 2, E), ALU.subtract).then_inc(logits_ready, 1)
                dve.wait_ge(probs_ready, layer + 1)
                o.link(dve.tensor_reduce(lmx[:], lg, AX_X, ALU.add))
                o.link(dve.reciprocal(lmx[:], lmx[:]))
                o.link(tt(lg, lg, bc(lmx[:], 2, E), ALU.mult))
                for i in range(NT):
                    o.mark(dve.max(top[:, i, :], lg[:, i, :]))
                o.wait()
                for i in range(NT):
                    o.mark(dve.max_index(topi[:, i, :], top[:, i, :], lg[:, i, :]))
                o.wait()
                o.mark(dve.tensor_copy(e12[:, 0, :], topi[:, :, 0]))
                o.mark(dve.tensor_copy(e12[:, 1, :], topi[:, :, 1]))
                o.link(tt(wsum[:], top[:, :, 0], top[:, :, 1], ALU.add))
                o.link(dve.reciprocal(wsum[:], wsum[:]))
                for j in range(2):
                    o.mark(tt(w12[:, j, :], top[:, :, j], wsum[:], ALU.mult))
                    o.mark(tt(oh[:, j], bc(iota_e[:], 1, NT), bc(e12[:, j, :], 2, E), ALU.is_equal))
                o.wait()
                tt(mask, oh[:, 0], oh[:, 1], ALU.add).then_inc(mask_ready, 1)
                dve.wait_ge(ranks_ps, 2 * layer + 2)
                o.link(dve.tensor_copy(tot, ps[:, 0, 0:NT * E].rearrange("p (i e) -> p e i", e=E)))
                o.link(dve.tensor_tensor_scan(flat(inc), flat(first_of_e[:]), flat(tot), 0.0, ALU.mult, ALU.add))
                o.link(tt(tot, inc, tot, ALU.subtract))
                o.link(tt(rank, tot.rearrange("p e i -> p i e"),
                          ps[:, 1, 0:NT * E].rearrange("p (i e) -> p i e", e=E), ALU.add))
                if layer == 0:
                    o.link(dve.tensor_scalar(tl[:, 0, :], inc[:, :, NT - 1], float(P - 1), 1.0 / P, ALU.add, ALU.mult))
                    o.link(dve.tensor_scalar_add(tl[:, 0, :], tl[:, 0, :], -0.5 + 0.5 / P))
                    o.link(dve.tensor_copy(tl_i[:], tl[:, 0, :]))
                    o.link(dve.tensor_copy(tl[:, 0, :], tl_i[:]))
                    o.link(dve.tensor_tensor_scan(tl[:, 1, :], ones[:, 0:E], tl[:, 0, :], 0.0, ALU.mult, ALU.add))
                    o.link(tt(tl[:, 2, :], tl[:, 1, :], tl[:, 0, :], ALU.subtract))
                    o.link(dve.tensor_scalar(tl[:, 2, :], tl[:, 2, :], float(P), -1.0, ALU.mult, ALU.add))
                    o.link(tt(rank, rank, bc(tl[:, 2, :], 1, NT), ALU.add))
                    o.link(tt(tcmp, bc(iota_t[:], 2, E), bc(tl[:, 1, :], 1, TILES_A), ALU.is_ge))
                    o.link(dve.tensor_reduce(texp[:], tcmp, AX_X, ALU.add))
                    o.link(dve.tensor_scalar(texp[:], texp[:], float(E - 1), float(F), ALU.min, ALU.mult))
                    o.link(dve.tensor_copy(texp_i[:], texp[:]))
                else:
                    o.link(dve.tensor_scalar(keep, rank, float(CAP), None, ALU.is_le))
                    o.link(dve.tensor_scalar(tl[:, 2, :], iota_e[:], float(CAP), -1.0, ALU.mult, ALU.add))
                    o.link(tt(rank, rank, bc(tl[:, 2, :], 1, NT), ALU.add))
                for j in range(2):
                    o.mark(tt(prod[:, j], oh[:, j], rank, ALU.mult))
                o.wait()
                o.link(dve.tensor_reduce(slot[:].rearrange("p j i -> p (j i)"), prod.rearrange("p j i e -> p (j i) e"), AX_X, ALU.add))
                if layer == 0:
                    dve.tensor_copy(sl_put[:], slot[:]).then_inc(slots_ready, 1)
                    return
                for j in range(2):
                    o.mark(tt(prod[:, j], oh[:, j], keep, ALU.mult))
                o.wait()
                o.link(dve.tensor_reduce(kept[:].rearrange("p j i -> p (j i)"), prod.rearrange("p j i e -> p (j i) e"), AX_X, ALU.add))
                o.mark(tt(w12[:], w12[:], kept[:], ALU.mult))
                o.link(tt(slot[:], slot[:], kept[:], ALU.mult))
                o.mark(dve.tensor_copy(sl_get[:], slot[:]))
                o.link(dve.tensor_scalar(kept[:], kept[:], -float(SKIP), float(SKIP), ALU.mult, ALU.add))
                o.link(tt(slot[:], slot[:], kept[:], ALU.add))
                dve.tensor_copy(sl_put[:], slot[:]).then_inc(slots_ready, 1)

            dve.wait_ge(x_loaded, 64)
            layernorm(0)
            dve.wait_ge(w_loaded, 16 * 7)
            dve.tensor_scalar_add(taps[:, :, 3], taps[:, :, 3], 1.0).then_inc(taps_ready, 1)
            for cu in range(NCU):
                w, s = cu % 3, cu % 4
                dve.wait_ge(tap_first, cu + 1)
                for sh in (1, 2, 3):
                    i = dve.scalar_tensor_tensor(cv[:, s, sh:L], ps[:, 2 + s, 0:L - sh], taps[:, w, 3 - sh:4 - sh],
                                                 cv[:, s, sh:L], ALU.mult, ALU.add)
                    if sh < 3:
                        o.link(i)
                    else:
                        i.then_inc(conv_done, 1)
            dve.wait_ge(consts_ready, 6)
            dispatch(0)
            dve.wait_ge(heads_loaded, 16 * 4 * B)
            for n in range(2):
                dve.wait_ge(squared, n + 1)
                dve.tensor_reduce(nrm[:, n, :], TMP.rearrange("p e t -> p t e"), AX_X, ALU.add).then_inc(norm2, 1)
            dve.tensor_scalar_add(LZ, LZ, 1e-3).then_inc(lr_in, 1)
            for n, t in enumerate((K, Q)):
                dve.wait_ge(norm_root, n + 1)
                o.link(dve.reciprocal(nrm[:, n, :], nrm[:, n, :]))
                o.mark(tt(t[:], t[:], bc(nrm[:, n, :], 1, HD), ALU.mult))
            dve.wait_ge(lr_log, 1)
            o.link(dve.scalar_tensor_tensor(LR[:], LZ, 0.0, LR[:], ALU.max, ALU.add))
            o.wait()

            dve.wait_ge(zeroed, ZEROED)
            def rows(a):
                return bc(a.rearrange("p d l -> p l d"), 1, DI)

            def fast(a):
                return bc(a.rearrange("p (D d) -> p D d", D=DI), 2, CH)

            def by_row(a, e):
                return bc(e, 2, HD), bc(a, 1, DI)

            def keys_of(c):
                return K[:, :, bass.ds(c * CH, CH)]

            o.mark(tt(PK, rows(K[:, :, 0:CH]), fast(w_in), ALU.mult))
            o.wait()
            o.link(dve.tensor_reduce(SI, PK, AX_X, ALU.add))
            dve.sem_inc(state_ready, 1)

            def step(c, routed, last=False):
                ts = bass.ds(c * CH, CH)
                kc, vc = K[:, :, ts], V[:, :, ts]
                lr_of = lambda j: LR[:, j, bass.ds(c * CH, 1)]
                n0 = c * TPS - FIRST * TPS
                red = dve.tensor_reduce
                over_D = lambda a: a.rearrange("p D l -> p l D")
                grid = lambda a: a.rearrange("p (D d) -> p D d", D=DI)

                def gate_up(k):
                    if not routed:
                        return
                    dve.wait_ge(tanh_done, n0 + (k + 1))
                    g, u = ps[:, 1 + 2 * (k % 2), :], ps[:, 2 + 2 * (k % 2), :]
                    m = o.mark(dve.scalar_tensor_tensor(th[:, k, :], th[:, k, :], 1.0, g, ALU.add, ALU.mult))
                    return m, k, u

                def gate_up2(started):
                    if not routed:
                        return
                    m, k, u = started
                    o.wait(m)
                    dve.wait_ge(gu_ps, n0 * 2 + (2 * k + 2))
                    tt(hid[:, k, :], th[:, k, :], u, ALU.mult).then_inc(hid_ready, 1)

                finished = o.n
                dve.wait_ge(state_ready, c + 1)
                m_k = o.mark(red(MK[:], over_D(SI), AX_X, ALU.max))
                m_b = o.mark(red(MX[:, 1], SI, AX_X, ALU.max))
                o.wait(m_k)
                tt(EK, SI, bc(MK[:], 1, DI), ALU.subtract).then_inc(rec_k, 1)
                o.wait(m_b)
                tt(EB, SI, bc(MX[:, 1], 2, CH), ALU.subtract).then_inc(rec_b, 1)
                o.wait(finished)
                o.mark(dve.tensor_copy(SC[:, :, 0], w_out))
                dve.wait_ge(exp_k, c + 1)
                z_k = o.mark(red(ZK[:], over_D(EK), AX_X, ALU.add))
                dve.wait_ge(exp_b, c + 1)
                z_b = o.mark(red(ZS[:, 1], EB, AX_X, ALU.add))
                o.wait(z_k)
                r_k = o.mark(dve.reciprocal(ZK[:], ZK[:]))
                o.wait(z_b)
                r_b = o.mark(dve.reciprocal(ZS[:, 1], ZS[:, 1]))
                o.wait(r_k)
                l_k = o.mark(tt(ZK[:], ZK[:], LR[:, 1, ts], ALU.mult))
                g_b = o.mark(tt(GB, *by_row(vc, EB), ALU.mult))
                o.wait(l_k)
                h_k = o.mark(tt(EK, EK, bc(ZK[:], 1, DI), ALU.mult))
                o.wait(g_b)
                s_b = o.mark(red(GR[:, 1].rearrange("p (D d) -> p D d", D=DI), GB, AX_X, ALU.add))
                o.wait(h_k)
                x_k = o.mark(tt(SC.rearrange("p (D d) l -> p D d l", D=DI)[:, :, :, 1:CH + 1], *by_row(vc, EK), ALU.mult))
                o.wait(s_b)
                n_b = o.mark(tt(grid(GR[:, 1]), grid(GR[:, 1]), bc(ZS[:, 1], 2, HD), ALU.mult))
                dve.wait_ge(op_ready, c + 1)
                o.wait(x_k)
                run = o.mark(dve.tensor_tensor_scan(flat(CS), flat(seg[:]), flat(SC), 0.0, ALU.mult, ALU.add))
                u0 = gate_up(0)
                o.wait(run)
                p_a = o.mark(tt(PV, rows(vc), fast(CS[:, :, CH]), ALU.mult))
                o.wait(n_b)
                wo1 = o.mark(dve.scalar_tensor_tensor(w_out1[:], GR[:, 1], lr_of(1), CS[:, :, CH], ALU.mult, ALU.add))
                o.wait(p_a)
                s_a = o.mark(red(SA, PV, AX_X, ALU.add))
                gate_up2(u0)
                o.wait(wo1)
                p_c = o.mark(tt(PK, rows(vc), fast(w_out1[:]), ALU.mult))
                o.wait(s_a)
                m_a = o.mark(red(MX[:, 0], SA, AX_X, ALU.max))
                o.wait(m_a)
                tt(EA, SA, bc(MX[:, 0], 2, CH), ALU.subtract).then_inc(rec_a, 1)
                o.wait(p_c)
                s_c = o.mark(red(SV, PK, AX_X, ALU.add))
                dve.wait_ge(q_ps, c + 1)
                m_q = o.mark(red(MQ[:], ps[:, 7, 0:DI * CH].rearrange("p (D l) -> p l D", D=DI), AX_X, ALU.max))
                o.wait(s_c)
                m_c = o.mark(red(MX[:, 2], SV, AX_X, ALU.max))
                dve.wait_ge(exp_a, c + 1)
                z_a = o.mark(red(ZS[:, 0], EA, AX_X, ALU.add))
                o.wait(m_c)
                tt(EC, SV, bc(MX[:, 2], 2, CH), ALU.subtract).then_inc(rec_c, 1)
                o.wait(m_q)
                tt(EQ, ps[:, 7, 0:DI * CH].rearrange("p (D l) -> p D l", D=DI), bc(MQ[:], 1, DI), ALU.subtract).then_inc(rec_q, 1)
                g_a = o.mark(tt(GA, *by_row(kc, EA), ALU.mult))
                o.wait(z_a)
                r_a = o.mark(dve.reciprocal(ZS[:, 0], ZS[:, 0]))
                u1 = gate_up(1)
                o.wait(g_a)
                s_a = o.mark(red(grid(GR[:, 0]), GA, AX_X, ALU.add))
                dve.wait_ge(exp_c, c + 1)
                z_c = o.mark(red(ZS[:, 2], EC, AX_X, ALU.add))
                o.wait(s_a)
                n_a = o.mark(tt(grid(GR[:, 0]), grid(GR[:, 0]), bc(ZS[:, 0], 2, HD), ALU.mult))
                g_c = o.mark(tt(GC, *by_row(kc, EC), ALU.mult))
                gate_up2(u1)
                o.wait(n_a)
                wi1 = o.mark(dve.scalar_tensor_tensor(w_in1[:], GR[:, 0], lr_of(0), w_in, ALU.mult, ALU.add))
                r_c = o.mark(dve.reciprocal(ZS[:, 2], ZS[:, 2]))
                o.wait(g_c)
                s_c = o.mark(red(grid(GR[:, 2]), GC, AX_X, ALU.add))
                o.wait(wi1)
                p_d = o.mark(tt(PV, rows(kc), fast(w_in1[:]), ALU.mult))
                o.wait(s_c)
                n_c = o.mark(tt(grid(GR[:, 2]), grid(GR[:, 2]), bc(ZS[:, 2], 2, HD), ALU.mult))
                o.wait(p_d)
                s_d = o.mark(red(SD, PV, AX_X, ALU.add))
                u2 = gate_up(2)
                dve.wait_ge(pq_ready, c + 1)
                o.wait(n_c)
                wi2 = o.mark(dve.scalar_tensor_tensor(w_in, GR[:, 2], lr_of(0), w_in1[:], ALU.mult, ALU.add))
                o.wait(s_d)
                m_d = o.mark(red(MX[:, 3], SD, AX_X, ALU.max))
                o.wait(wi2)
                if not last:
                    p_n = o.mark(tt(PK, rows(keys_of(c + 1)), fast(w_in), ALU.mult))
                o.wait(m_d)
                tt(ED, SD, bc(MX[:, 3], 2, CH), ALU.subtract).then_inc(rec_d, 1)
                if not last:
                    o.wait(p_n)
                    red(SI, PK, AX_X, ALU.add).then_inc(state_ready, 1)
                gate_up2(u2)
                dve.wait_ge(exp_d, c + 1)
                z_d = o.mark(red(ZS[:, 3], ED, AX_X, ALU.add))
                g_d = o.mark(tt(GV, *by_row(vc, ED), ALU.mult))
                dve.wait_ge(exp_q, c + 1)
                z_q = o.mark(red(ZQ[:], over_D(EQ), AX_X, ALU.add))
                o.wait(g_d)
                s_d = o.mark(red(grid(GR[:, 3]), GV, AX_X, ALU.add))
                r_d = o.mark(dve.reciprocal(ZS[:, 3], ZS[:, 3]))
                o.wait(z_q)
                r_q = o.mark(dve.reciprocal(ZQ[:], ZQ[:]))
                o.wait(r_d)
                n_d = o.mark(tt(grid(GR[:, 3]), grid(GR[:, 3]), bc(ZS[:, 3], 2, HD), ALU.mult))
                o.wait(r_q)
                tt(EQ, EQ, bc(ZQ[:], 1, DI), ALU.mult).then_inc(qh_ready, 1)
                o.wait(n_d)
                o.mark(dve.scalar_tensor_tensor(w_out, GR[:, 3], lr_of(1), w_out1[:], ALU.mult, ALU.add))

            PER_R, PER_P = 49, 46
            for lo, hi, routed in ((0, FIRST, False), (FIRST, AFTER, True), (AFTER, NCH - 1, False)):
                first, per = o.total(), PER_R if routed else PER_P
                with dve.Fori(lo, hi) as c:
                    o.loop(c, first - lo * per, per)
                    step(c, routed)
                o.end(first, per, hi - lo)
            step(NCH - 1, False, last=True)
            o.wait()
            dve.wait_ge(o_copied, NCH + 1)
            dT = lambda a: a.rearrange("p e t -> p t e")
            o.link(dve.tensor_reduce(nrm[:, 0, :], dT(O[:]), AX_X, ALU.add))
            o.link(dve.tensor_scalar(nrm[:, 0, :], nrm[:, 0, :], 1.0 / HD, None, ALU.mult))
            tt(O[:], O[:], bc(nrm[:, 0, :], 1, HD), ALU.subtract).then_inc(o_centred, 1)
            dve.wait_ge(o_squared, 1)
            o.link(dve.tensor_reduce(nrm[:, 0, :], dT(V[:]), AX_X, ALU.add))
            dve.tensor_scalar(nrm[:, 0, :], nrm[:, 0, :], 1.0 / HD, EPS, ALU.mult, ALU.add).then_inc(o_var, 1)
            dve.wait_ge(o_root, 1)
            o.link(dve.reciprocal(nrm[:, 0, :], nrm[:, 0, :]))
            tt(O[:], O[:], bc(nrm[:, 0, :], 1, HD), ALU.mult).then_inc(o_ready, 1)

            def combine(g, y1, y2):
                r = lambda a: flat(a)[:, g * 512:(g + 1) * 512].rearrange("p (i c) -> p i c", c=D)
                a, b2 = r(y1), r(y2)
                o.mark(tt(a, a, bc(w12[:, 0, 4 * g:4 * g + 4], 2, D), ALU.mult))
                o.link(tt(b2, b2, bc(w12[:, 1, 4 * g:4 * g + 4], 2, D), ALU.mult))
                tt(a, a, b2, ALU.add).then_inc(mix_ready, 1)

            dve.wait_ge(y_gathered, 16 * 2 * NT)
            for g in range(G4):
                combine(g, xn[:], xnT[:])
            oT = K[:].rearrange("p a b -> p (a b)")
            dve.wait_ge(oT_loaded, 16)
            o.link(dve.tensor_scalar(oT, oT, ln_gb[:, 0:1], ln_gb[:, 1:2], ALU.mult, ALU.add))
            tt(oT, oT, gateT[:], ALU.mult).then_inc(oT_ready, 1)

            dve.wait_ge(x_loaded, 128)
            for g in range(G4):
                v = flat(xn[:])[:, g * 512:(g + 1) * 512]
                xs = x[:, 4 * g:4 * g + 4, :].rearrange("p i c -> p (i c)")
                dve.wait_ge(s_ps, g + 1)
                dve.wait_ge(mix_silu, g + 1)
                i = tt(v, v, ps[:, 1 + g % 2, :], ALU.mult)
                i.then_inc(s_used, 1)
                dve.wait_ge(s_used, g + 1)
                tt(xs, xs, v, ALU.add).then_inc(x1_ready, 1)

            dve.wait_ge(x1_ready, G4)
            dve.wait_ge(w1_loaded, 16 * N_W1)
            layernorm(1)
            dispatch(1)
            def conv1(r, s, g):
                dve.wait_ge(tap1_first, r * GD + (g + 1))
                for sh in (1, 2, 3):
                    i = dve.scalar_tensor_tensor(h1[s][:, g, sh:L], ps[:, 6 + g, 0:L - sh], conv_w1[:, g, 3 - sh:4 - sh],
                                                 h1[s][:, g, sh:L], ALU.mult, ALU.add)
                    if sh < 3:
                        o.link(i)
                    else:
                        i.then_inc(conv1_done, 1)

            def rest1(r, s):
                dve.wait_ge(bc_hi, r + 1)
                tt(bc_rest[0:2 * 2 * NS, :], ps[0:2 * 2 * NS, 7, :], bc_parts[s][0:2 * 2 * NS], ALU.subtract).then_inc(bc_rest1, 1)

            def rest2(r, s):
                dve.wait_ge(bc_mid, r + 1)
                tt(bc_rest[0:2 * NS, :], bc_rest[0:2 * NS, :], bc_parts[s][0:2 * NS], ALU.subtract).then_inc(bc_rest2, 1)

            def finish(c, s):
                dve.wait_ge(yc_used, (c + 1) * (GD * NS))
                for g in range(GD):
                    total = ps[:, 4 + g, :]
                    if g == 1 and not (isinstance(c, int) and c in (0, B - 1)):
                        dve.wait_ge(y_added, c * (NS - 1))
                        total = y_sum[s]
                    o.mark(dve.scalar_tensor_tensor(h1[s][:, g, :], h1[s][:, g, :], d_1[:, g:g + 1], total, ALU.mult, ALU.add))
                for g in range(GD):
                    o.wait(o.n - 1 + g)
                    tt(h1[s][:, g, :], h1[s][:, g, :], res1[s][:, g, :], ALU.mult).then_inc(yt_ready, 1)

            def delta_sum(r, s, g):
                dve.wait_ge(sp_log, r * GD + (g + 1))
                tt(del1[s][:, g, :], del1[s][:, g, :], sp1[:, g, :], ALU.add).then_inc(delta_ready, 1)

            def delta_h(r, s, g):
                dve.wait_ge(delta_ready, r * GD + (g + 1))
                tt(dh1[s][:, g, :], del1[s][:, g, :], h1[s][:, g, :], ALU.mult).then_inc(dh_ready, 1)

            def row(c, s, nxt, experts, shared):
                t = 1 - s
                first = isinstance(c, int) and c == 0
                st = lambda n, g: st_g1[:, n % 2, :] if g else st_g0

                def inject(n, g):
                    dve.wait_ge(b_ps, c * NS + (n + 1))
                    since(dve, scanned, c * (GD * NS) + (GD * (n - 1) + g + 1))
                    i = tt(dBu[:, g, :], dh1[s][:, g, :], ps[:, 2 + n % 2, :], ALU.mult)
                    if g == 0:
                        return o.mark(i)
                    i.then_inc(b_used, 1)

                def scan(n, g):
                    k = GD * n + g
                    dve.wait_ge(dA_ready, c * (GD * NS) + (k + 1))
                    if g:
                        dve.wait_ge(b_used, c * NS + (n + 1))
                        if n >= 2 or not first:
                            dve.wait_ge(*group1_done(c, n - 2))
                    else:
                        since(dve, yc_ready, c * NS + n)
                    dve.tensor_tensor_scan(st(n, g), dA(k), dBu[:, g, :], 0.0, ALU.mult, ALU.add).then_inc(scanned, 1)

                dve.wait_ge(dh_ready, c * GD + GD)
                for n in range(NS):
                    injected = inject(n, 0)
                    inject(n, 1)
                    o.wait(injected)
                    scan(n, 0)
                    scan(n, 1)
                    dve.wait_ge(scanned, c * (GD * NS) + (GD * n + 1))
                    if shared:
                        dve.wait_ge(c_copied, (c - 1) * NS + (n + 1))
                    else:
                        dve.wait_ge(c_ps, c * NS + (n + 1))
                    since(dve, yc_used, c * (GD * NS) + (GD * (n - 2) + 1))
                    tt(yc_g0[:, n % 2, :], st_g0, ps[:, n % 2, :], ALU.mult).then_inc(yc_ready, 1)
                    if not shared:
                        dve.wait_ge(scanned, c * (GD * NS) + (GD * n + 2))
                        since(dve, yc_used, c * (GD * NS) + (GD * (n - 2) + 2))
                        if n == 0 and not first:
                            dve.wait_ge(y_added, (c - 1) * (NS - 1))
                        tt(yc_g1[:, n % 2, :], st(n, 1), ps[:, n % 2, :], ALU.mult).then_inc(yc_g1_own, 1)
                    if n == 0 and not first:
                        finish(c - 1, t)
                    if nxt is not None:
                        if n in (1, 2):
                            conv1(nxt, t, n - 1)
                        if n == 7:
                            rest1(nxt, t)
                        if n == 8:
                            rest2(nxt, t)
                        if not shared and n in (11, 12):
                            delta_sum(nxt, t, n - 11)
                        if not shared and n in (13, 14):
                            delta_h(nxt, t, n - 13)

            for g in range(GD):
                conv1(0, 0, g)
            rest1(0, 0)
            rest2(0, 0)
            for g in range(GD):
                delta_sum(0, 0, g)
            for g in range(GD):
                delta_h(0, 0, g)
            PER_B = 2 * (3 * GD + NS)
            base = 0

            def pairs(i=None):
                nonlocal base
                if i is None:
                    base = o.total()
                else:
                    o.loop(i, base, PER_B)

            all_rows(dve, row, pairs, lambda: o.end(base, PER_B, (B - 4) // 2))
            finish(B - 1, 1)
            dve.wait_ge(y1_gathered, 16 * 2 * NT)
            dve.wait_ge(s1_copied, B)
            for g in range(G4):
                combine(g, xn[:], xnT[:])
            for g in range(G4):
                v = flat(xn[:])[:, g * 512:(g + 1) * 512]
                xs = x[:, 4 * g:4 * g + 4, :].rearrange("p i c -> p (i c)")
                dve.wait_ge(mix_silu, G4 + g + 1)
                o.link(tt(v, v, s1[:, g * 512:(g + 1) * 512], ALU.mult))
                tt(xs, xs, v, ALU.add).then_inc(out_ready, 1)


def host(inputs):
    import numpy as np
    c = np.ascontiguousarray
    a = {k: np.asarray(v) for k, v in inputs.items()}
    r = {}
    r["x"] = c(a["L0_attn_hidden_states"].reshape(T, D))
    r["wproj"] = c(np.concatenate([a[f"L0_attn_W{n}"].T for n in "qkvg"], axis=1))
    r["wlr"] = c(a["L0_attn_Wlr"].T)
    r["wo"] = c(a["L0_attn_Wo"].T)
    r["taps"] = c(np.concatenate([a["L0_attn_cq"], a["L0_attn_ck"], a["L0_attn_cv"]], axis=1))
    r["ln_gb"] = c(np.stack([np.tile(a["L0_attn_ln_g"], H), np.tile(a["L0_attn_ln_b"], H)], axis=1))
    st = np.concatenate([a[n][0].transpose(1, 0, 2).reshape(H, DI * HD) for n in ("L0_attn_W_in_init", "L0_attn_W_out_init")], axis=1)
    r["state0"] = c(np.tile(st, (B, 1)))
    r["wrt"] = c(a["L0_ffn_W_router"].T)
    r["wg_a"] = c(a["L0_ffn_W_gate"].transpose(2, 0, 1).reshape(D, E * F))
    r["wu_a"] = c(a["L0_ffn_W_up"].transpose(2, 0, 1).reshape(D, E * F))
    r["wd_a"] = c(a["L0_ffn_W_down"].reshape(E, D, FC, P).transpose(3, 0, 2, 1).reshape(P, E * FC * D))
    r["w_in1"] = c(a["L1_attn_in_proj_w"])
    rows = lambda m: c(m.reshape(GD, P, -1).transpose(1, 0, 2).reshape(P, -1))
    for n, k in (("w_x1", "x_proj_w"), ("w_o1", "out_proj_w"), ("conv_w1", "conv_w"), ("conv_b1", "conv_b"),
                 ("dt_b1", "dt_proj_b"), ("d_1", "D_param"), ("a_log", "A_log")):
        r[n] = rows(a["L1_attn_" + k])
    r["w_bc1"] = c(np.concatenate([r["w_x1"].reshape(P, GD, -1)[:, :, DTR:]] * 3, axis=2).reshape(P, -1))
    r["w_x1"] = c(r["w_x1"].reshape(P, GD, -1)[:, :, :DTR].reshape(P, -1))
    r["w_dt1"] = c(a["L1_attn_dt_proj_w"])
    r["w_rt1"] = c(a["L1_ffn_gate_w"])
    r["b_rt1"] = c(a["L1_ffn_gate_b"].reshape(1, E))
    r["b_e1"] = c(a["L1_ffn_b1"].reshape(E, FC, P).transpose(2, 0, 1).reshape(P, E * FC))
    r["b_e2"] = c(a["L1_ffn_b2"].reshape(1, E * D))
    r["w_e1"] = c(a["L1_ffn_w1"].reshape(E * D, F))
    r["w_e2"] = c(a["L1_ffn_w2"].reshape(E, FC, P, D).transpose(2, 0, 1, 3).reshape(P, E * FC * D))
    return r


def kernel(**inputs):
    import numpy as _np
    import concourse.bacc as _bacc
    from concourse.bass_utils import run_bass_kernel_spmd as _run

    nc = _bacc.Bacc("TRN2", target_bir_lowering=False, num_devices=1)
    arrays, d = {}, {}
    for name, a in host(inputs).items():
        arrays[f"in_{name}"] = a
        d[name] = nc.dram_tensor(f"in_{name}", a.shape, mybir.dt.from_np(a.dtype), kind="ExternalInput").ap()
    d["out"] = nc.dram_tensor("out_0_dram", (T, D), F32, kind="ExternalOutput").ap()
    build(nc, d)
    got = _run(nc, [arrays], core_ids=[0]).results[0]["out_0_dram"]
    return _np.asarray(got).reshape(B, L, D)
```
